# Optimizing a Trainium2 kernel written in Bass

```python
import numpy as np
import jax
import jax.numpy as jnp

def _softmax(x, axis=-1):
    return jax.nn.softmax(x, axis=axis)

def _gelu(x):
    return jax.nn.gelu(x, approximate=True)

def _silu(x):
    return jax.nn.silu(x)

def _sigmoid(x):
    return jax.nn.sigmoid(x)

def _layernorm(x, axis=-1, eps=1e-05):
    m = jnp.mean(x, axis=axis, keepdims=True)
    v = jnp.var(x, axis=axis, keepdims=True)
    return (x - m) / jnp.sqrt(v + eps)

def _scatter_add(tgt, idx, src, axis=0):
    return tgt.at[idx].add(src)

def _segment_sum(src, seg, n):
    return jax.ops.segment_sum(src, seg, n)
kernel_name = 'mk_early_fusion_d2_tok_img256_r4_0d98c2'

def setup_inputs(seed: int=0):
    np.random.seed(seed)
    _w = jnp.asarray

    def _rec_inputs():
        import jax
        import jax.numpy as jnp
        _rk = jax.random.key(seed)
        x = -0.000202321 + 1.00025 * jax.random.normal(jax.random.fold_in(_rk, 1), (4, 64, 56, 56), jnp.float32)
        txt = 0.00140203 + 0.288157 * jax.random.normal(jax.random.fold_in(_rk, 2), (4, 32, 64), jnp.float32)
        return (x, txt)
    x, txt = _rec_inputs()

    def _L0_tok_setup():
        import jax, jax.numpy as jnp
        import numpy as np
        B, C, H, W = (8, 64, 56, 56)
        K = 3

        def _unfold3x3(x):
            b, c, h, w = x.shape
            xp = jnp.pad(x, ((0, 0), (0, 0), (1, 1), (1, 1)))
            patches = jnp.stack([xp[:, :, i:i + h, j:j + w] for i in range(K) for j in range(K)], axis=2)
            return patches.reshape(b, c * K * K, h * w).transpose(0, 2, 1)
        key = jax.random.key(seed)
        ks = jax.random.split(key, 8)
        d = C * K * K
        s1 = 1.0 / np.sqrt(d)
        s2 = 1.0 / np.sqrt(C)
        return {'x': jax.random.normal(ks[0], (B, C, H, W), jnp.float32), 'W1': jax.random.uniform(ks[1], (d, C), jnp.float32, -s1, s1), 'b1': jax.random.uniform(ks[2], (C,), jnp.float32, -s1, s1), 'W2': jax.random.uniform(ks[3], (C, d), jnp.float32, -s2, s2), 'b2': jax.random.uniform(ks[4], (d,), jnp.float32, -s2, s2), 'W3': jax.random.uniform(ks[5], (d, C), jnp.float32, -s1, s1), 'b3': jax.random.uniform(ks[6], (C,), jnp.float32, -s1, s1)}
    _L0_tok_all = _L0_tok_setup()
    _L0_tok_in = {k: v for k, v in _L0_tok_all.items() if k in ('W1', 'b1', 'W2', 'b2', 'W3', 'b3')}
    del _L0_tok_all

    def _L0_attn_setup():
        import jax, jax.numpy as jnp
        import numpy as np
        B, N, D, H = (2, 512, 64, 8)
        DH = D // H
        E = 16384
        EPS = 1e-05

        def _layer_norm(y, gamma, beta):
            mu = jnp.mean(y, axis=-1, keepdims=True)
            var = jnp.var(y, axis=-1, keepdims=True)
            return (y - mu) * jax.lax.rsqrt(var + EPS) * gamma + beta
        key = jax.random.key(seed)
        ks = jax.random.split(key, 12)
        s = 0.02
        inp = {'x': jax.random.normal(ks[0], (B, N, D), jnp.float32), 'edge_index': jax.random.randint(ks[1], (2, E), 0, N, jnp.int64), 'Wq': jax.random.normal(ks[2], (D, D), jnp.float32) * s, 'bq': jnp.zeros((D,), jnp.float32), 'Wk': jax.random.normal(ks[3], (D, D), jnp.float32) * s, 'bk': jnp.zeros((D,), jnp.float32), 'Wv': jax.random.normal(ks[4], (D, D), jnp.float32) * s, 'bv': jnp.zeros((D,), jnp.float32), 'Wo': jax.random.normal(ks[5], (D, D), jnp.float32) * s, 'bo': jnp.zeros((D,), jnp.float32), 'gamma': jnp.ones((D,), jnp.float32), 'beta': jnp.zeros((D,), jnp.float32)}
        return inp
    _L0_attn_all = _L0_attn_setup()
    _L0_attn_in = {k: v for k, v in _L0_attn_all.items() if k in ('edge_index', 'Wq', 'bq', 'Wk', 'bk', 'Wv', 'bv', 'Wo', 'bo', 'gamma', 'beta')}
    del _L0_attn_all

    def _L0_ffn_setup():
        import jax, jax.numpy as jnp
        import numpy as np
        B, S, H, F, E, K = (8, 1024, 64, 128, 16, 2)
        EPS = 1e-05
        key = jax.random.key(seed)
        ks = jax.random.split(key, 9)
        sc = 0.02
        return {'x': jax.random.normal(ks[0], (B, S, H), dtype=jnp.float32), 'gate_w': jax.random.normal(ks[1], (H, E), dtype=jnp.float32) * sc, 'gate_b': jnp.zeros((E,), dtype=jnp.float32), 'w1': jax.random.normal(ks[2], (E, H, F), dtype=jnp.float32) * sc, 'b1': jnp.zeros((E, F), dtype=jnp.float32), 'w2': jax.random.normal(ks[3], (E, F, H), dtype=jnp.float32) * sc, 'b2': jnp.zeros((E, H), dtype=jnp.float32), 'gamma': jnp.ones((H,), dtype=jnp.float32), 'beta': jnp.zeros((H,), dtype=jnp.float32)}
    _L0_ffn_all = _L0_ffn_setup()
    _L0_ffn_in = {k: v for k, v in _L0_ffn_all.items() if k in ('gate_w', 'gate_b', 'w1', 'b1', 'w2', 'b2', 'gamma', 'beta')}
    del _L0_ffn_all

    def _L1_attn_setup():
        import jax, jax.numpy as jnp
        import numpy as np
        import math
        B, N, D = (4, 1024, 64)
        key = jax.random.key(seed)
        k0, k1, k2, k3 = jax.random.split(key, 4)
        bound = math.sqrt(6.0 / D)
        return {'x': jax.random.normal(k0, (B, N, D), dtype=jnp.float32), 'Wq': jax.random.uniform(k1, (D, D), dtype=jnp.float32, minval=-bound, maxval=bound), 'Wk': jax.random.uniform(k2, (D, D), dtype=jnp.float32, minval=-bound, maxval=bound), 'Wv': jax.random.uniform(k3, (D, D), dtype=jnp.float32, minval=-bound, maxval=bound)}
    _L1_attn_all = _L1_attn_setup()
    _L1_attn_in = {k: v for k, v in _L1_attn_all.items() if k in ('Wq', 'Wk', 'Wv')}
    del _L1_attn_all

    def _L1_ffn_setup():
        import jax, jax.numpy as jnp
        import numpy as np
        B, T, D, H, E = (16, 1024, 64, 128, 8)
        key = jax.random.key(seed)
        ks = jax.random.split(key, 5)
        x = jax.random.normal(ks[0], (B, T, D), dtype=jnp.float32)
        gate_w = jax.random.normal(ks[1], (D, E), dtype=jnp.float32) * 0.02
        gate_b = jnp.zeros((E,), dtype=jnp.float32)
        W1 = jax.random.normal(ks[2], (E, D, H), dtype=jnp.float32) * 0.02
        b1 = jnp.zeros((E, H), dtype=jnp.float32)
        W2 = jax.random.normal(ks[3], (E, H, D), dtype=jnp.float32) * 0.02
        b2 = jnp.zeros((E, D), dtype=jnp.float32)
        return {'x': x, 'gate_w': gate_w, 'gate_b': gate_b, 'W1': W1, 'b1': b1, 'W2': W2, 'b2': b2}
    _L1_ffn_all = _L1_ffn_setup()
    _L1_ffn_in = {k: v for k, v in _L1_ffn_all.items() if k in ('gate_w', 'gate_b', 'W1', 'b1', 'W2', 'b2')}
    del _L1_ffn_all
    return {'x': x, 'txt': txt, 'L0_tok_W1': _L0_tok_in['W1'], 'L0_tok_b1': _L0_tok_in['b1'], 'L0_tok_W2': _L0_tok_in['W2'], 'L0_tok_b2': _L0_tok_in['b2'], 'L0_tok_W3': _L0_tok_in['W3'], 'L0_tok_b3': _L0_tok_in['b3'], 'L0_attn_edge_index': _L0_attn_in['edge_index'], 'L0_attn_Wq': _L0_attn_in['Wq'], 'L0_attn_bq': _L0_attn_in['bq'], 'L0_attn_Wk': _L0_attn_in['Wk'], 'L0_attn_bk': _L0_attn_in['bk'], 'L0_attn_Wv': _L0_attn_in['Wv'], 'L0_attn_bv': _L0_attn_in['bv'], 'L0_attn_Wo': _L0_attn_in['Wo'], 'L0_attn_bo': _L0_attn_in['bo'], 'L0_attn_gamma': _L0_attn_in['gamma'], 'L0_attn_beta': _L0_attn_in['beta'], 'L0_ffn_gate_w': _L0_ffn_in['gate_w'], 'L0_ffn_gate_b': _L0_ffn_in['gate_b'], 'L0_ffn_w1': _L0_ffn_in['w1'], 'L0_ffn_b1': _L0_ffn_in['b1'], 'L0_ffn_w2': _L0_ffn_in['w2'], 'L0_ffn_b2': _L0_ffn_in['b2'], 'L0_ffn_gamma': _L0_ffn_in['gamma'], 'L0_ffn_beta': _L0_ffn_in['beta'], 'L1_attn_Wq': _L1_attn_in['Wq'], 'L1_attn_Wk': _L1_attn_in['Wk'], 'L1_attn_Wv': _L1_attn_in['Wv'], 'L1_ffn_gate_w': _L1_ffn_in['gate_w'], 'L1_ffn_gate_b': _L1_ffn_in['gate_b'], 'L1_ffn_W1': _L1_ffn_in['W1'], 'L1_ffn_b1': _L1_ffn_in['b1'], 'L1_ffn_W2': _L1_ffn_in['W2'], 'L1_ffn_b2': _L1_ffn_in['b2']}

def reference(x, txt, L0_tok_W1, L0_tok_b1, L0_tok_W2, L0_tok_b2, L0_tok_W3, L0_tok_b3, L0_attn_edge_index, L0_attn_Wq, L0_attn_bq, L0_attn_Wk, L0_attn_bk, L0_attn_Wv, L0_attn_bv, L0_attn_Wo, L0_attn_bo, L0_attn_gamma, L0_attn_beta, L0_ffn_gate_w, L0_ffn_gate_b, L0_ffn_w1, L0_ffn_b1, L0_ffn_w2, L0_ffn_b2, L0_ffn_gamma, L0_ffn_beta, L1_attn_Wq, L1_attn_Wk, L1_attn_Wv, L1_ffn_gate_w, L1_ffn_gate_b, L1_ffn_W1, L1_ffn_b1, L1_ffn_W2, L1_ffn_b2):
    import jax
    import jax.numpy as jnp

    def _L0_tok_ref(x, W1, b1, W2, b2, W3, b3):
        import jax, jax.numpy as jnp
        import numpy as np
        B, C, H, W = (8, 64, 56, 56)
        K = 3

        def _unfold3x3(x):
            b, c, h, w = x.shape
            xp = jnp.pad(x, ((0, 0), (0, 0), (1, 1), (1, 1)))
            patches = jnp.stack([xp[:, :, i:i + h, j:j + w] for i in range(K) for j in range(K)], axis=2)
            return patches.reshape(b, c * K * K, h * w).transpose(0, 2, 1)
        t = _unfold3x3(x)
        h1 = jax.nn.relu(jnp.einsum('bld,dc->blc', t, W1) + b1)
        s = jax.nn.sigmoid(jnp.einsum('blc,cd->bld', h1, W2) + b2)
        out = jnp.einsum('bld,dc->blc', t * s, W3) + b3
        return out

    def _L0_attn_ref(x, edge_index, Wq, bq, Wk, bk, Wv, bv, Wo, bo, gamma, beta):
        import jax, jax.numpy as jnp
        import numpy as np
        B, N, D, H = (2, 512, 64, 8)
        DH = D // H
        E = 16384
        EPS = 1e-05

        def _layer_norm(y, gamma, beta):
            mu = jnp.mean(y, axis=-1, keepdims=True)
            var = jnp.var(y, axis=-1, keepdims=True)
            return (y - mu) * jax.lax.rsqrt(var + EPS) * gamma + beta
        b, n, _ = x.shape
        scale = DH ** (-0.5)
        q = (x @ Wq + bq).reshape(b, n, H, DH)
        k = (x @ Wk + bk).reshape(b, n, H, DH)
        v = (x @ Wv + bv).reshape(b, n, H, DH)
        scores = jnp.einsum('bnhd,bmhd->bhnm', q, k) * scale
        diag = jnp.arange(n)
        mask = jnp.zeros((n, n), bool).at[diag, diag].set(True)
        mask = mask.at[edge_index[0], edge_index[1]].set(True)
        scores = jnp.where(mask[None, None], scores, -jnp.inf)
        w = jax.nn.softmax(scores, axis=-1)
        attended = jnp.einsum('bhnm,bmhd->bnhd', w, v).reshape(b, n, D)
        out = attended @ Wo + bo
        return _layer_norm(out + x, gamma, beta)

    def _L0_ffn_ref(x, gate_w, gate_b, w1, b1, w2, b2, gamma, beta):
        import jax, jax.numpy as jnp
        import numpy as np
        B, S, H, F, E, K = (8, 1024, 64, 128, 16, 2)
        EPS = 1e-05
        gate_logits = x @ gate_w + gate_b
        topk_vals, topk_idx = jax.lax.top_k(gate_logits, K)
        topk_w = jax.nn.softmax(topk_vals, axis=-1)
        h = jax.nn.relu(jnp.einsum('bsh,ehf->bsef', x, w1) + b1)
        expert_out = jnp.einsum('bsef,efh->bseh', h, w2) + b2
        sel = jnp.take_along_axis(expert_out, topk_idx[:, :, :, None], axis=2)
        moe = jnp.sum(topk_w[..., None] * sel, axis=2)
        y = x + moe
        mu = jnp.mean(y, axis=-1, keepdims=True)
        var = jnp.var(y, axis=-1, keepdims=True)
        return (y - mu) / jnp.sqrt(var + EPS) * gamma + beta

    def _L1_attn_ref(x, Wq, Wk, Wv):
        import jax, jax.numpy as jnp
        import numpy as np
        import math
        B, N, D = (4, 1024, 64)
        q = x @ Wq.T
        k = x @ Wk.T
        v = x @ Wv.T
        n = x.shape[1]
        d_k = x.shape[2]
        mask = jnp.triu(jnp.ones((n, n), dtype=x.dtype), k=1)
        scale = jnp.asarray(1.0 / math.sqrt(d_k), dtype=x.dtype)
        s = (jnp.einsum('bnd,bmd->bnm', q, k) - (1.0 - mask) * 10000000000.0) * scale
        s = jax.nn.softmax(s, axis=1)
        return jnp.einsum('bnm,bmd->bnd', s, v)

    def _L1_ffn_ref(x, gate_w, gate_b, W1, b1, W2, b2):
        import jax, jax.numpy as jnp
        import numpy as np
        B, T, D, H, E = (16, 1024, 64, 128, 8)
        Bb, Tt, Dd = x.shape
        Ee = gate_w.shape[1]
        xf = x.reshape(-1, Dd)
        N = xf.shape[0]
        logits = xf @ gate_w + gate_b
        probs = jax.nn.softmax(logits, axis=-1)
        top2_vals, top2_idx = jax.lax.top_k(probs, 2)
        cw = jnp.zeros((N, Ee), dtype=xf.dtype).at[jnp.arange(N)[:, None], top2_idx].add(top2_vals)

        def step(acc, params):
            w1, bb1, w2, bb2, we = params
            h = jax.nn.gelu(xf @ w1 + bb1, approximate=False)
            y = h @ w2 + bb2
            return (acc + we[:, None] * y, None)
        out, _ = jax.lax.scan(step, jnp.zeros_like(xf), (W1, b1, W2, b2, cw.T))
        return out.reshape(Bb, Tt, Dd)
    h = _L0_tok_ref(x, L0_tok_W1, L0_tok_b1, L0_tok_W2, L0_tok_b2, L0_tok_W3, L0_tok_b3)
    h = jnp.concatenate([h, txt], axis=1)
    h = h + _L0_attn_ref(_layernorm(h, axis=-1), L0_attn_edge_index, L0_attn_Wq, L0_attn_bq, L0_attn_Wk, L0_attn_bk, L0_attn_Wv, L0_attn_bv, L0_attn_Wo, L0_attn_bo, L0_attn_gamma, L0_attn_beta)
    h = h + _L0_ffn_ref(_layernorm(h, axis=-1), L0_ffn_gate_w, L0_ffn_gate_b, L0_ffn_w1, L0_ffn_b1, L0_ffn_w2, L0_ffn_b2, L0_ffn_gamma, L0_ffn_beta)
    h = h + _L1_attn_ref(_layernorm(h, axis=-1), L1_attn_Wq, L1_attn_Wk, L1_attn_Wv)
    h = h + _L1_ffn_ref(_layernorm(h, axis=-1), L1_ffn_gate_w, L1_ffn_gate_b, L1_ffn_W1, L1_ffn_b1, L1_ffn_W2, L1_ffn_b2)
    return h

_drawn_inputs = setup_inputs


def setup_inputs(seed=0):
    import zlib

    import numpy as np

    out = dict(_drawn_inputs(seed))
    spreads = {'L0_attn_bq': (0.0, 2.0),
     'L0_attn_bk': (0.0, 2.0),
     'L0_attn_bv': (0.0, 0.434),
     'L0_attn_bo': (0.0, 0.1),
     'L0_attn_gamma': (1.0, 0.2),
     'L0_attn_beta': (0.0, 0.1),
     'L0_ffn_gate_b': (0.0, 0.1),
     'L0_ffn_b1': (0.0, 0.8),
     'L0_ffn_b2': (0.0, 0.1),
     'L0_ffn_gamma': (1.0, 0.2),
     'L0_ffn_beta': (0.0, 0.1),
     'L1_ffn_gate_b': (0.0, 0.8),
     'L1_ffn_b1': (0.0, 0.8),
     'L1_ffn_b2': (0.0, 0.8)}
    factors = {'L0_tok_b1': 8.0,
     'L0_attn_Wq': 8.0,
     'L0_attn_Wk': 8.0,
     'L0_attn_Wv': 2.812,
     'L0_ffn_w1': 7.928,
     'L0_ffn_w2': 5.653,
     'L1_ffn_gate_w': 6.943,
     'L1_ffn_W1': 8.0,
     'L1_ffn_W2': 8.0}
    for name, (base, spread) in spreads.items():
        noise = np.random.default_rng([zlib.crc32(name.encode()), seed]).standard_normal(out[name].shape)
        drawn = base * np.exp(spread * noise) if base else spread * noise
        out[name] = jnp.asarray(drawn.astype(out[name].dtype))
    for name, factor in factors.items():
        out[name] = (out[name] * factor).astype(out[name].dtype)
    return out
```

```python
from contextlib import ExitStack

import concourse.bass as bass
from concourse import mybir

F32 = mybir.dt.float32
F32R = mybir.dt.float32r
BF16 = mybir.dt.bfloat16
F16 = mybir.dt.float16
I32 = mybir.dt.int32
ALU = mybir.AluOpType
ACT = mybir.ActivationFunctionType
X = mybir.AxisListType.X

P = 128
BANK = 512
MASKED = -1.0e30
LN_EPS = 1e-5


class Chain:

    def __init__(self, eng, sem, done=0, turn=None, per=0):
        self.eng, self.sem, self.done, self.turn, self.per, self.n = eng, sem, done, turn, per, 0

    def mark(self, ins):
        ins.then_inc(self.sem, 1)
        self.n += 1
        return ins

    def value(self):
        return self.done + self.n if self.turn is None else self.turn * self.per + (self.done + self.n)

    def wait(self):
        self.eng.wait_ge(self.sem, self.value())

    def link(self, ins):
        self.mark(ins)
        self.wait()

    def close(self):
        assert self.turn is None or self.n == self.per, (self.n, self.per)
        return self.n


def build(nc, I, out):
    B, C, IH, IW = I["x"].shape
    TXT = I["txt"].shape[1]
    D = C
    IMG = IH * IW
    N = IMG + TXT
    TPB = -(-N // P)
    LAST = N - (TPB - 1) * P
    NPAD = TPB * P
    T = B * TPB
    NCH = T * P // BANK
    TPC = BANK // P
    TAPS = 9
    G5 = 5
    PW = IW + 2
    PAIRS = [(0, 1), (3, 4), (6, 7), (2, 5), (8, None)]
    ROWS = 8
    CT = ROWS * IW
    HALF = CT // 2
    CPB = IH // ROWS
    E0, _, F = I["L0_ffn_w1"].shape
    E1 = I["L1_ffn_W1"].shape[0]
    HEADS = 8
    DH = D // HEADS
    assert T * P % BANK == 0 and F == P and D == 64

    def off(tap):
        return (tap // 3) * PW + tap % 3

    cols, at = {}, 0
    for name, n in (("tok_w2", G5 * P), ("a0_q", P), ("a0_k", P), ("a0_v", P), ("a0_o", P), ("f0_g", P),
                    ("f0_w1", E0 * P), ("f0_b2", P), ("a1_q", P), ("a1_k", P), ("a1_v", P), ("f1_g", P),
                    ("f1_w1", E1 * P), ("f1_b2", P)):
        cols[name] = at
        at += n
    WCOLS = at
    rows, at = {}, 0
    for name, n in (("f0_b1", E0), ("f1_b1", E1), ("tok_b1", 1), ("tok_b3", 1), ("a0_bq", 1), ("a0_bk", 1),
                    ("a0_bv", 1), ("a0_bo", 1), ("f0_gb", 1), ("f1_gb", 1), ("tok_b2", G5)):
        rows[name] = at
        at += n
    NBIAS = at

    with ExitStack() as ctx:
        def sb(name, shape, dt=F32, stack=ctx):
            return stack.enter_context(nc.sbuf_tensor(name, shape, dt))

        def sem(name):
            return ctx.enter_context(nc.semaphore(name))

        bank = [ctx.enter_context(nc.psum_tensor(f"bank{i}", [P, BANK], F32)) for i in range(8)]

        H = sb("H", [P, T, D])
        WS = sb("WS", [P, WCOLS], F32R)
        tok_w1 = sb("tok_w1", [P, G5, D])
        tok_w3 = sb("tok_w3", [P, G5, D])
        f0_w2 = sb("f0_w2", [P, E0, D])
        f1_w2 = sb("f1_w2", [P, E1, D])
        bias = sb("bias", [P, NBIAS])
        gb = sb("gb", [P, 4, D])
        ident = sb("ident", [P, P])
        SEL = sb("SEL", [P, max(E0, E1), P], F32R)
        head_rows = sb("head_rows", [P, HEADS])
        ident_bf = sb("ident_bf", [P, P], BF16)
        mask0 = sb("mask0", [P, TPC, BANK], BF16)

        stage_done = sem("stage_done")
        stored = sem("stored")

        ln_dve = sem("ln_dve")
        ln_centred = sem("ln_centred")
        ln_squared = sem("ln_squared")
        ln_var = sem("ln_var")
        ln_std = sem("ln_std")

        def W(name, i=0, n=P):
            return WS[:, cols[name] + i * P:cols[name] + i * P + n]

        def bcol(name, i=0, lo=0, hi=P):
            return bias[lo:hi, rows[name] + i:rows[name] + i + 1]

        LOADS = [0]

        def stage_end(e, k):
            e.drain().then_inc(stage_done, 1)
            e.wait_ge(stage_done, 5 * k)

        ctx_w = ExitStack()
        WF = sb("WF", [P, WCOLS], F32, ctx_w)
        sel_f = sb("sel_f", [P, max(E0, E1), P], F32, ctx_w)
        tok_w2_raw = sb("tok_w2_raw", [P, D * TAPS], F32, ctx_w)
        brow = sb("brow", [P, P], F32, ctx_w)
        wt = sb("wt", [D, 3, P], F32, ctx_w)
        E_PER = I["L0_attn_edge_index"].shape[1] // P
        edges = sb("edges", [P, 2, E_PER], I32, ctx_w)
        edges_f = sb("edges_f", [P, 2, E_PER], F32, ctx_w)
        node = sb("node", [P, BANK], F16, ctx_w)
        HOTS = 4
        hot = sb("hot", [P, HOTS, 2, BANK], BF16, ctx_w)
        w_zeroed = sem("w_zeroed")
        edges_loaded = sem("edges_loaded")
        w_loaded = sem("w_loaded")
        edges_cast = sem("edges_cast")
        w_sorted = sem("w_sorted")
        w_rounded = sem("w_rounded")
        ident_set = sem("ident_set")
        tables_turned = sem("tables_turned")
        tables_copied = sem("tables_copied")
        hot_ready = sem("hot_ready")
        hot_used = sem("hot_used")
        counts_zeroed = sem("counts_zeroed")
        mask_thresholded = sem("mask_thresholded")
        sel_set = sem("sel_set")
        heads_set = sem("heads_set")

        def weights_sync(e):
            def load(dst, src, **kw):
                e.dma_start(dst, src, **kw).then_inc(w_loaded, 16)
                LOADS[0] += 1

            e.dma_start(edges[:, :, :], I["L0_attn_edge_index"].rearrange("a (p j) -> p a j", p=P)).then_inc(edges_loaded, 16)
            load(gb[:, 0, :], I["L0_attn_gamma"].partition_broadcast(P))
            load(gb[:, 1, :], I["L0_attn_beta"].partition_broadcast(P))
            load(gb[:, 2, :], I["L0_ffn_gamma"].partition_broadcast(P))
            load(gb[:, 3, :], I["L0_ffn_beta"].partition_broadcast(P))
            load(f0_w2[:, :, :], I["L0_ffn_w2"].rearrange("e f n -> f e n"))
            load(f1_w2[:, :, :], I["L1_ffn_W2"].rearrange("e f n -> f e n"))
            for i, name in enumerate("qkv"):
                for m in (0, D):
                    load(wt[0:D, i, m:m + D], I["L1_attn_W" + name])
            e.wait_ge(w_zeroed, 5)
            for lo in (0, D):
                half = WF[lo:lo + D, :]
                load(half[:, cols["f0_w1"]:cols["f0_w1"] + E0 * P].rearrange("k (e m) -> k e m", e=E0),
                     I["L0_ffn_w1"].rearrange("e k m -> k e m"))
                load(half[:, cols["f1_w1"]:cols["f1_w1"] + E1 * P].rearrange("k (e m) -> k e m", e=E1),
                     I["L1_ffn_W1"].rearrange("e k m -> k e m"))
                load(half[:, cols["f0_g"]:cols["f0_g"] + E0], I["L0_ffn_gate_w"])
                load(half[:, cols["f1_g"]:cols["f1_g"] + E1], I["L1_ffn_gate_w"])
                for name in "qkvo":
                    for m in (0, D):
                        c = cols["a0_" + name] + m
                        load(half[:, c:c + D], I["L0_attn_W" + name])
                load(tok_w2_raw[lo:lo + D, :], I["L0_tok_W2"])
            for name, src, n in (("f0_b2", "L0_ffn_b2", E0), ("f1_b2", "L1_ffn_b2", E1)):
                for r in range(0, P, 32):
                    load(WF[r:r + n, cols[name]:cols[name] + D], I[src])
            w1_taps = I["L0_tok_W1"].rearrange("(c t) n -> t c n", t=TAPS)
            w3_taps = I["L0_tok_W3"].rearrange("(c t) n -> t c n", t=TAPS)
            b2_taps = I["L0_tok_b2"].rearrange("(o c t) -> t o c", t=TAPS, o=1)
            for g, pair in enumerate(PAIRS):
                for h, tap in enumerate(pair):
                    if tap is not None:
                        load(tok_w1[h * D:(h + 1) * D, g, :], w1_taps[tap])
                        load(tok_w3[h * D:(h + 1) * D, g, :], w3_taps[tap])
                        r = rows["tok_b2"] + g
                        load(brow[r:r + 1, h * D:(h + 1) * D], b2_taps[tap], allow_slow_non_contiguous=True)
            load(brow[rows["f0_b1"]:rows["f0_b1"] + E0, :], I["L0_ffn_b1"])
            load(brow[rows["f1_b1"]:rows["f1_b1"] + E1, :], I["L1_ffn_b1"])
            for name, src in (("tok_b1", "L0_tok_b1"), ("tok_b3", "L0_tok_b3"), ("a0_bq", "L0_attn_bq"),
                              ("a0_bk", "L0_attn_bk"), ("a0_bv", "L0_attn_bv"), ("a0_bo", "L0_attn_bo")):
                for m in (0, D):
                    load(brow[rows[name]:rows[name] + 1, m:m + D], I[src].rearrange("(o n) -> o n", o=1))
            load(brow[rows["f0_gb"]:rows["f0_gb"] + 1, 0:E0], I["L0_ffn_gate_b"].rearrange("(o n) -> o n", o=1))
            load(brow[rows["f1_gb"]:rows["f1_gb"] + 1, 0:E1], I["L1_ffn_gate_b"].rearrange("(o n) -> o n", o=1))
            for b in range(B):
                load(H[IMG % P:IMG % P + TXT, b * TPB + TPB - 1, :], I["txt"][b])
            e.wait_ge(w_loaded, 16 * LOADS[0])

        def weights_gpsimd(e):
            e.iota(node[:, :], pattern=[[1, BANK]], base=0, channel_multiplier=0,
                   allow_small_or_imprecise_dtypes=True).then_inc(ident_set, 1)
            e.memset(brow[:, :], 0.0).then_inc(w_zeroed, 1)
            e.memset(tok_w1[:, :, :], 0.0).then_inc(w_zeroed, 1)
            e.memset(tok_w3[:, :, :], 0.0).then_inc(w_zeroed, 1)
            e.memset(WF[:, :], 0.0).then_inc(w_zeroed, 1)
            e.memset(H[:, :, :], 0.0).then_inc(w_zeroed, 1)
            e.memset(ident[:, :], 0.0).then_inc(ident_set, 1)
            e.wait_ge(ident_set, 2)
            e.affine_select(out=ident[:, :], in_=ident[:, :], compare_op=ALU.not_equal, fill=1.0, base=0,
                            pattern=[[-1, P]], channel_multiplier=1).then_inc(ident_set, 1)
            e.wait_ge(ident_set, 3)
            e.tensor_copy(ident_bf[:, :], ident[:, :]).then_inc(ident_set, 1)
            e.memset(sel_f[:, :, :], 0.0).then_inc(sel_set, 1)
            for k in range(2):
                e.wait_ge(sel_set, k + 1)
                e.affine_select(out=sel_f[:, :, :], in_=sel_f[:, :, :], compare_op=ALU.not_equal, fill=1.0,
                                base=-32 * k, pattern=[[-1, max(E0, E1)], [0, P]],
                                channel_multiplier=1).then_inc(sel_set, 1)
            e.memset(head_rows[:, :], 0.0).then_inc(heads_set, 1)
            for k, r in enumerate(range(2 * DH)):
                e.wait_ge(heads_set, k + 1)
                e.affine_select(out=head_rows[:, :], in_=head_rows[:, :], compare_op=ALU.not_equal, fill=1.0,
                                base=-(r // DH) * D - r % DH, pattern=[[-DH, HEADS]],
                                channel_multiplier=1).then_inc(heads_set, 1)
            for t in range(TPC):
                e.wait_ge(mask_thresholded, t + 1)
                e.affine_select(out=mask0[:, t, :], in_=mask0[:, t, :], compare_op=ALU.not_equal, fill=0.0,
                                base=t * P, pattern=[[-1, BANK]], channel_multiplier=1).then_inc(ident_set, 1)

        def weights_scalar(e):
            e.wait_ge(w_sorted, 1)
            e.activation(WS[:, :], WF[:, :], ACT.Copy).then_inc(w_rounded, 1)
            e.wait_ge(sel_set, 3)
            e.activation(SEL[:, :, :], sel_f[:, :, :], ACT.Copy).then_inc(w_rounded, 1)
            e.wait_ge(tables_turned, 1)
            e.activation(bias[:, :], bank[4][:, 0:NBIAS], ACT.Copy).then_inc(tables_copied, 1)

        def weights_vector(e):
            for t in range(TPC):
                e.memset(bank[t][:, :], 0.0).then_inc(counts_zeroed, 1)
            e.wait_ge(edges_loaded, 16)
            e.tensor_copy(edges_f[:, :, :], edges[:, :, :]).then_inc(edges_cast, 1)
            e.wait_ge(edges_cast, 1)
            e.wait_ge(ident_set, 1)
            with e.Fori(0, E_PER // HOTS) as i:
                for u in range(HOTS):
                    e.wait_ge(hot_used, i * HOTS + (u + 1))
                    for a in range(2):
                        e.tensor_scalar(hot[:, u, a, :], node[:, :],
                                        edges_f[:, a, bass.ds(i * HOTS + u, 1)], None,
                                        ALU.is_equal).then_inc(hot_ready, 1)
            for t in range(TPC):
                e.wait_ge(hot_used, HOTS + E_PER)
                e.tensor_scalar(mask0[:, t, :], bank[t][:, :], 0.5, MASKED, ALU.is_lt,
                                ALU.mult).then_inc(mask_thresholded, 1)
            e.wait_ge(w_loaded, 16 * LOADS[0])
            for i, name in enumerate(("a1_q", "a1_k", "a1_v")):
                e.wait_ge(tables_turned, 2)
                for m in (0, D):
                    c = cols[name] + m
                    e.tensor_copy(WF[:, c:c + D], bank[5][:, i * D:(i + 1) * D]).then_inc(edges_cast, 1)
            for g, pair in enumerate(PAIRS):
                for h, tap in enumerate(pair):
                    if tap is not None:
                        c = cols["tok_w2"] + g * P + h * D
                        e.tensor_copy(WF[:, c:c + D], tok_w2_raw[:, :].rearrange("p (c t) -> p t c", t=TAPS)[:, tap, :]
                                      ).then_inc(edges_cast, 1)
            e.wait_ge(edges_cast, 1 + 6 + TAPS)
            e.sem_inc(w_sorted, 1)
            e.wait_ge(w_rounded, 1)
            e.tensor_tensor(WS[D:P, :], WF[D:P, :], WS[D:P, :].bitcast(F32), ALU.subtract).then_inc(w_rounded, 1)

        def weights_tensor(e):
            e.sem_inc(hot_used, HOTS)
            e.wait_ge(counts_zeroed, TPC)
            with e.Fori(0, E_PER // HOTS) as i:
                for u in range(HOTS):
                    e.wait_ge(hot_ready, i * (2 * HOTS) + 2 * (u + 1))
                    for t in range(TPC):
                        mm = e.matmul(bank[t][:, :], hot[:, u, 0, t * P:(t + 1) * P], hot[:, u, 1, :],
                                      start=False, stop=False, skip_group_check=True)
                    mm.then_inc(hot_used, 1)
            e.wait_ge(ident_set, 3)
            e.wait_ge(w_loaded, 16 * LOADS[0])
            e.transpose(bank[4][:, 0:P], brow[:, :], ident[:, :]).then_inc(tables_turned, 1)
            for i in range(3):
                last = e.transpose(bank[5][:, i * D:(i + 1) * D], wt[:, i, :], ident[0:D, 0:D])
            last.then_inc(tables_turned, 1)

        ctx_w.close()

        ctx_t = ExitStack()
        PIX = PW * PW
        img = [[sb(f"img_{n}{b}", [P, PIX + PW], F32, ctx_t) for b in range(2)] for n in ("col", "row")]
        tokT = [sb(f"tokT{b}", [P, NPAD], F32, ctx_t) for b in range(2)]
        h1 = [sb(f"h1_{b}", [P, CT], F32, ctx_t) for b in range(2)]
        h1_hi = [sb(f"h1_hi{b}", [P, CT], F32R, ctx_t) for b in range(2)]
        h1_lo = [sb(f"h1_lo{b}", [P, CT], F32R, ctx_t) for b in range(2)]
        NG = 3
        gate = [sb(f"gate{b}", [P, CT], F32, ctx_t) for b in range(NG)]
        gated = [sb(f"gated{b}", [P, G5, CT], F32, ctx_t) for b in range(2)]
        GROUP = [(0, off(0)), (0, off(3)), (0, off(6)), (1, off(2)), (0, off(8))]
        UB = 2
        UC = UB * CPB
        TURNS = B // UB
        TGROUPS = -(-TPB // TPC)
        img_zeroed = sem("img_zeroed")
        img_loaded = [sem(f"img_loaded{b}") for b in range(UB)]
        img_copied = [sem(f"img_copied{b}") for b in range(UB)]
        t_h = sem("t_h")
        t_relu = sem("t_relu")
        t_split = sem("t_split")
        t_halves = sem("t_halves")
        t_logit = sem("t_logit")
        t_gate = sem("t_gate")
        t_gated = sem("t_gated")
        t_out = sem("t_out")
        t_stored = sem("t_stored")
        t_turned = sem("t_turned")
        t_inH = sem("t_inH")

        def tok_sync(e):
            e.wait_ge(img_zeroed, 2 * UB)
            for b in range(B):
                u = b % UB
                col, row = img[0][u], img[1][u]
                if b >= UB:
                    e.wait_ge(t_gated, (b - UB + 1) * CPB * G5)
                e.dma_start(col[0:D, 0:PIX].rearrange("c (h w) -> c h w", w=PW)[:, 1:IH + 1, 1:IW + 1],
                            I["x"][b]).then_inc(img_loaded[u], 16)
                e.wait_ge(img_loaded[u], (b // UB + 1) * 16)
                e.dma_start(col[D:P, 0:PIX - 1], col[0:D, 1:PIX]).then_inc(img_copied[u], 16)
                e.dma_start(row[0:D, 0:PIX], col[0:D, 0:PIX]).then_inc(img_copied[u], 16)
                e.dma_start(row[D:P, 0:PIX - PW], col[0:D, PW:PIX]).then_inc(img_copied[u], 16)

        def taps(g, u, j, lo=0, hi=ROWS):
            which, o = GROUP[g]
            o += (j * ROWS + lo) * PW
            n = hi - lo
            return img[which][u][:, o:o + n * PW].rearrange("p (h w) -> p h w", w=PW)[:, :, 0:IW]

        def tok_gpsimd(e):
            for which in range(2):
                for u in range(UB):
                    e.memset(img[which][u][:, :], 0.0).then_inc(img_zeroed, 1)
            for u in range(UB):
                e.memset(tokT[u][:, :], 0.0).then_inc(img_zeroed, 1)

        def tok_tensor(e):
            with e.Fori(0, TURNS) as i:
                def at(n, per=1):
                    return i * (UC * per) + n

                def first_product(c):
                    u, j = divmod(c, CPB)
                    if j == 0:
                        e.wait_ge(img_copied[u], i * 48 + 48)
                    e.wait_ge(t_relu, at(c + 1))
                    for g in range(G5):
                        for h in range(2):
                            mm = e.matmul(bank[c % 2][h * D:(h + 1) * D, 0:HALF], tok_w1[:, g, :],
                                          taps(g, u, j, h * ROWS // 2, (h + 1) * ROWS // 2),
                                          start=(g == 0), stop=(g == G5 - 1))
                    mm.then_inc(t_h, 1)

                def gate_logits(c):
                    if c == 0:
                        e.wait_ge(t_inH, i * (UB * TGROUPS) + 2)
                    e.wait_ge(t_split, at(c + 1))
                    for g in range(G5):
                        k = c * G5 + g
                        b = bank[2 + k % 4]
                        e.wait_ge(t_gate, i * (UC * G5) + (k + 1))
                        e.matmul(b[:, 0:CT], W("tok_w2", g), h1_hi[c % 2][:, :], start=True, stop=False)
                        e.matmul(b[:, 0:CT], W("tok_w2", g), h1_lo[c % 2][:, :], start=False, stop=True).then_inc(t_logit, 1)

                def last_product(c):
                    e.wait_ge(t_gated, i * (UC * G5) + (c + 1) * G5)
                    e.wait_ge(t_stored, at(c + 1))
                    for g in range(G5):
                        for h in range(2):
                            mm = e.matmul(bank[6 + c % 2][h * D:(h + 1) * D, 0:HALF], tok_w3[:, g, :],
                                          gated[c % 2][:, g, h * HALF:(h + 1) * HALF],
                                          start=(g == 0), stop=(g == G5 - 1))
                    mm.then_inc(t_out, 1)

                first_product(0)
                for c in range(UC):
                    if c + 1 < UC:
                        first_product(c + 1)
                    gate_logits(c)
                    if c >= 1:
                        last_product(c - 1)
                last_product(UC - 1)
                for u in range(UB):
                    for k in range(0, TPB, TPC):
                        r = u * TGROUPS + k // TPC
                        if r == 0:
                            e.wait_ge(t_stored, at(UC + 2))
                            e.wait_ge(t_gate, i * (UC * G5) + (UC * G5 + 4))
                        e.wait_ge(t_inH, i * (UB * TGROUPS) + (r + 1))
                        for t in range(k, min(k + TPC, TPB)):
                            mm = e.transpose(bank[2 + r % 2][:, (t - k) * P:(t - k + 1) * P],
                                             tokT[u][:, t * P:(t + 1) * P], ident[:, :])
                        mm.then_inc(t_turned, 1)

        def tok_scalar(e):
            e.sem_inc(t_relu, 2)
            e.sem_inc(t_gate, 4)
            with e.Fori(0, TURNS) as i:
                for c in range(UC + 1):
                    if c < UC:
                        e.wait_ge(t_h, i * UC + (c + 1))
                        e.wait_ge(t_split, i * UC + max(c - 1, 0))
                        for h in range(2):
                            for m in range(2):
                                a = e.activation(h1[c % 2][m * D:(m + 1) * D, h * HALF:(h + 1) * HALF],
                                                 bank[c % 2][h * D:(h + 1) * D, 0:HALF], ACT.Relu,
                                                 bias=bcol("tok_b1", 0, h * D, (h + 1) * D))
                        a.then_inc(t_relu, 1)
                    if c >= 1:
                        for g in range(G5):
                            k = (c - 1) * G5 + g
                            e.wait_ge(t_logit, i * (UC * G5) + (k + 1))
                            e.wait_ge(t_gated, i * (UC * G5) + max(k + 1 - NG, 0))
                            e.activation(gate[k % NG][:, :], bank[2 + k % 4][:, 0:CT], ACT.Sigmoid,
                                         bias=bcol("tok_b2", g)).then_inc(t_gate, 1)

        def tok_vector(e):
            e.sem_inc(t_stored, 2)
            e.sem_inc(t_inH, 2)
            e.wait_ge(img_zeroed, 3 * UB)
            with e.Fori(0, TURNS) as i:
                def split(c):
                    e.wait_ge(t_relu, i * UC + (c + 3))
                    e.wait_ge(t_logit, i * (UC * G5) + max(c - 1, 0) * G5)
                    hi = h1_hi[c % 2]
                    e.tensor_copy(hi[:, :], h1[c % 2][:, :]).then_inc(t_halves, 1)
                    e.wait_ge(t_halves, i * UC + (c + 1))
                    e.tensor_tensor(h1_lo[c % 2][:, :], h1[c % 2][:, :], hi[:, :].bitcast(F32),
                                    ALU.subtract).then_inc(t_split, 1)

                def store(c):
                    u, j = divmod(c, CPB)
                    e.wait_ge(t_out, i * UC + (c + 1))
                    if j == 0:
                        e.wait_ge(t_turned, i * (UB * TGROUPS))
                    for h in range(2):
                        o = j * CT + h * HALF
                        a = e.tensor_scalar(tokT[u][0:D, o:o + HALF], bank[6 + c % 2][h * D:(h + 1) * D, 0:HALF],
                                            bcol("tok_b3", 0, h * D, (h + 1) * D), None, ALU.add)
                    a.then_inc(t_stored, 1)

                split(0)
                for c in range(UC):
                    u, j = divmod(c, CPB)
                    if c + 1 < UC:
                        split(c + 1)
                    e.wait_ge(t_out, i * UC + max(c - 1, 0))
                    for g in range(G5):
                        e.wait_ge(t_gate, i * (UC * G5) + (c * G5 + g + 1 + 4))
                        e.tensor_tensor(gated[c % 2][:, g, :].rearrange("p (h w) -> p h w", w=IW),
                                        gate[(c * G5 + g) % NG][:, :].rearrange("p (h w) -> p h w", w=IW),
                                        taps(g, u, j), ALU.mult).then_inc(t_gated, 1)
                    if c >= 1:
                        store(c - 1)
                store(UC - 1)
                for u in range(UB):
                    for k in range(0, TPB, TPC):
                        r = u * TGROUPS + k // TPC
                        e.wait_ge(t_turned, i * (UB * TGROUPS) + (r + 1))
                        whole = k + TPC < TPB
                        n, hi = (TPC, P) if whole else (1, IMG % P)
                        e.tensor_copy(H[0:hi, bass.ds(i * (UB * TPB) + (u * TPB + k), n), :],
                                      bank[2 + r % 2][0:hi, :].rearrange("p (t c) -> p t c", c=P)[:, 0:n, 0:D]
                                      ).then_inc(t_inH, 1)

        ctx_t.close()
        assert TPB % TPC == 1

        Y = sb("Y", [P, T, D])
        stat = sb("stat", [P, 4, T])
        NORMS = 6
        LN_LINKS = B + 1 + B + 1

        def rows_of(t, b):
            return t[:, b * TPB:(b + 1) * TPB, :]

        def over_d(t2, b):
            return t2[:, b * TPB:(b + 1) * TPB].unsqueeze(2).broadcast_to([P, TPB, D])

        def over_t(v):
            return v.unsqueeze(1).broadcast_to([P, TPB, D])

        def norm_vector(e, k, src, affine=None):
            ch = Chain(e, ln_dve, k * LN_LINKS)
            for b in range(B):
                ch.mark(e.tensor_reduce(stat[:, 0, b * TPB:(b + 1) * TPB], rows_of(src, b), X, ALU.add))
            ch.wait()
            ch.link(e.tensor_scalar(stat[:, 1, :], stat[:, 0, :], 1.0 / D, None, ALU.mult))
            for b in range(B):
                e.tensor_tensor(rows_of(Y, b), rows_of(src, b), over_d(stat[:, 1, :], b),
                                ALU.subtract).then_inc(ln_centred, 1)
            for b in range(B):
                e.wait_ge(ln_squared, k * B + b + 1)
                ch.mark(e.tensor_reduce(stat[:, 2, b * TPB:(b + 1) * TPB], squares[k][b % 2][:, :, :], X, ALU.add))
            ch.wait()
            e.tensor_scalar(stat[:, 3, :], stat[:, 2, :], 1.0 / D, LN_EPS, ALU.mult, ALU.add).then_inc(ln_var, 1)
            e.wait_ge(ln_std, k + 1)
            ch.link(e.reciprocal(stat[:, 3, :], stat[:, 3, :]))
            for b in range(B):
                e.tensor_tensor(rows_of(Y, b), rows_of(Y, b), over_d(stat[:, 3, :], b), ALU.mult).then_inc(ln_scaled, 1)
            if affine is not None:
                for b in range(B):
                    e.wait_ge(ln_scaled, k * B + b + 1)
                    e.tensor_tensor(rows_of(Y, b), rows_of(Y, b), over_t(gb[:, affine, :]), ALU.mult).then_inc(ln_gamma, 1)
                for b in range(B):
                    e.wait_ge(ln_gamma, (affine // 2) * B + b + 1)
                    e.wait_ge(ln_beta, (affine // 2) * B + b + 1)
                    e.tensor_tensor(rows_of(H, b), rows_of(H, b), rows_of(Y, b), ALU.add).then_inc(ln_gamma_in, 1)

        def norm_scalar(e, k):
            for b in range(B):
                e.wait_ge(ln_centred, k * B + b + 1)
                if b >= 2:
                    e.wait_ge(ln_dve, k * LN_LINKS + B + 1 + b - 1)
                e.activation(squares[k][b % 2][:, :, :], rows_of(Y, b), ACT.Square).then_inc(ln_squared, 1)
            e.wait_ge(ln_var, k + 1)
            e.activation(stat[:, 3, :], stat[:, 3, :], ACT.Sqrt).then_inc(ln_std, 1)

        def norm_gpsimd(e, affine):
            for b in range(B):
                e.tensor_tensor(rows_of(H, b), rows_of(H, b), over_t(gb[:, affine + 1, :]), ALU.add).then_inc(ln_beta, 1)

        ln_scaled = sem("ln_scaled")
        ln_gamma = sem("ln_gamma")
        ln_gamma_in = sem("ln_gamma_in")
        ln_beta = sem("ln_beta")
        squares = []
        ctx_n = ExitStack()
        squares_now = [sb(f"squares{j}", [P, TPB, D], F32, ctx_n) for j in range(2)]
        for k in range(NORMS):
            squares.append(squares_now)
        ctx_n.close()

        DUPS = 2

        CHUNKS_TURNED = [0]
        t_sems = {n: sem("x_" + n) for n in ("doubled", "turned", "high", "low")}

        def turner(name, stack, banks, chunks):
            CHUNKS_TURNED[0] += chunks
            return {"dup": [sb(f"{name}_dup{j}", [P, TPC, 2, D], F32, stack) for j in range(DUPS)],
                    "banks": banks, "before": CHUNKS_TURNED[0] - chunks, **t_sems}

        def turned_by(tr, done, n):
            return done + (tr["before"] + n)

        def double_chunk(e, tr, done, k, tokens, n):
            e.wait_ge(tr["turned"], turned_by(tr, done, max(k + 1 - DUPS, 0)))
            e.activation(tr["dup"][k % DUPS][:, 0:n, :, :], tokens.unsqueeze(2).broadcast_to([P, n, 2, D]),
                         ACT.Copy).then_inc(tr["doubled"], 1)

        def turn_chunk(e, tr, done, k, n):
            nb = len(tr["banks"])
            e.wait_ge(tr["low"], turned_by(tr, done, max(k + 1 - nb, 0)))
            e.wait_ge(tr["doubled"], turned_by(tr, done, k + 1))
            for t in range(n):
                mm = e.transpose(tr["banks"][k % nb][:, t * P:(t + 1) * P],
                                 tr["dup"][k % DUPS][:, t, :, :].rearrange("p a d -> p (a d)"), ident[:, :])
            mm.then_inc(tr["turned"], 1)

        def high_chunk(e, tr, done, k, n, hi):
            e.wait_ge(tr["turned"], turned_by(tr, done, k + 1))
            e.activation(hi, tr["banks"][k % len(tr["banks"])][:, 0:n * P], ACT.Copy).then_inc(tr["high"], 1)

        def low_chunk(e, tr, done, k, n, hi, lo):
            e.wait_ge(tr["high"], turned_by(tr, done, k + 1))
            e.tensor_tensor(lo, tr["banks"][k % len(tr["banks"])][:, 0:n * P], hi.bitcast(F32),
                            ALU.subtract).then_inc(tr["low"], 1)

        def product(e, out, weights, hi, lo, start=True, stop=True):
            e.matmul(out, weights, hi, start=start, stop=False)
            return e.matmul(out, weights, lo, start=False, stop=stop)

        def ffn(name, E, w2, kind, into):
            st = ExitStack()
            TURN = 5
            TURNS_A = NCH // TURN
            XH = [sb(f"{name}_XH{j}", [P, BANK], F32R, st) for j in range(2)]
            XL = [sb(f"{name}_XL{j}", [P, BANK], F32R, st) for j in range(2)]
            x_dup = sb(f"{name}_xdup", [P, TPC, 2, D], F32, st)
            LG = sb(f"{name}_LG", [P, T, E], F32, st)
            WH = sb(f"{name}_WH", [P, T, E], F32R, st)
            keep = ExitStack()
            tr = turner(name, keep, [bank[0], bank[1], bank[2]], NCH)
            LT = [sb(f"{name}_LT{j}", [P, BANK], F32, keep) for j in range(2)]
            g_logit, g_biased, g_turned, g_stored = (sem(f"{name}_{x}") for x in ("logit", "biased", "lturned", "lstored"))
            keep.close()
            keep = ExitStack()
            place = sb(f"{name}_place", [P, E], F32, keep)
            oh1 = sb(f"{name}_oh1", [P, T, E], F32, keep)
            oh2 = sb(f"{name}_oh2", [P, T, E], F32, keep)
            oh3 = sb(f"{name}_oh3", [P, T, E], F32, keep)
            red = sb(f"{name}_red", [P, 6, T], F32, keep)
            place_set, g_dve, g_act, g_exp = (sem(f"{name}_{x}") for x in ("place", "gdve", "gact", "gexp"))
            keep.close()
            RING = 4
            ext = [sb(f"{name}_ext{j}", [P, TPC, P], F32, st) for j in range(2)]
            GS = [sb(f"{name}_GS{j}", [P, BANK], F32R, st) for j in range(2)]
            hid = [sb(f"{name}_hid{j}", [P, BANK], F32, st) for j in range(RING)]
            hw = [sb(f"{name}_hw{j}", [P, BANK], F32, st) for j in range(RING)]
            ysb = sb(f"{name}_ysb", [P, BANK], F32, st)
            (ext_zeroed, ext_ready, w_turned, w_ready, h_ready, wb_ready, act_done, weighted, used, y_copied,
             y_turned, y_added, y_half, x_doubled, x_turned, x_high, x_low) = (sem(f"{name}_{x}") for x in (
                 "ext0", "ext", "wturned", "wready", "h", "wb", "act", "weighted", "used", "ycopied",
                 "yturned", "yadded", "yhalf", "xdoubled", "xturned", "xhigh", "xlow"))
            st.close()
            func = ACT.Relu if kind == "relu" else ACT.Gelu

            def tiles(t, c, n=TPC):
                return t[:, bass.ds(c * TPC, n), :] if not isinstance(c, int) else t[:, c * TPC:c * TPC + n, :]

            def a_tensor(e):
                with e.Fori(0, TURNS_A) as i:
                    for u in range(TURN + 2):
                        if u < TURN:
                            turn_chunk(e, tr, i * TURN, u, TPC)
                        if 1 <= u <= TURN:
                            v = u - 1
                            e.wait_ge(g_biased, i * TURN + max(v - 1, 0))
                            e.wait_ge(tr["low"], turned_by(tr, i * TURN, v + 1))
                            product(e, bank[3 + v % 2][:, :], W(name + "_g"), XH[v % 2][:, :], XL[v % 2][:, :]).then_inc(g_logit, 1)
                        if u >= 2:
                            v = u - 2
                            e.wait_ge(g_stored, i * TURN + max(v - 1, 0))
                            e.wait_ge(g_biased, i * TURN + (v + 1))
                            for t in range(TPC):
                                mm = e.transpose(bank[5 + v % 2][:, t * P:(t + 1) * P],
                                                 LT[v % 2][:, t * P:(t + 1) * P], ident[:, :])
                            mm.then_inc(g_turned, 1)

            def a_scalar(e):
                with e.Fori(0, TURNS_A) as i:
                    for u in range(TURN + 2):
                        if u < TURN:
                            double_chunk(e, tr, i * TURN, u, tiles(Y, i * TURN + u), TPC)
                            e.wait_ge(g_logit, i * TURN + max(u - 1, 0))
                            high_chunk(e, tr, i * TURN, u, TPC, XH[u % 2][:, :])
                        if 1 <= u <= TURN:
                            v = u - 1
                            e.wait_ge(g_turned, i * TURN + max(v - 1, 0))
                            e.wait_ge(g_logit, i * TURN + (v + 1))
                            e.activation(LT[v % 2][:, :], bank[3 + v % 2][:, :], ACT.Identity,
                                         bias=bcol(name + "_gb")).then_inc(g_biased, 1)

            def a_vector(e):
                with e.Fori(0, TURNS_A) as i:
                    for u in range(TURN + 2):
                        if u < TURN:
                            low_chunk(e, tr, i * TURN, u, TPC, XH[u % 2][:, :], XL[u % 2][:, :])
                        if u >= 2:
                            v = u - 2
                            e.wait_ge(g_turned, i * TURN + (v + 1))
                            e.tensor_copy(tiles(LG, i * TURN + v),
                                          bank[5 + v % 2][:, :].rearrange("p (t c) -> p t c", c=P)[:, :, 0:E]
                                          ).then_inc(g_stored, 1)

            def over_e(v):
                return v.unsqueeze(2).broadcast_to([P, T, E])

            def b_gpsimd(e):
                e.iota(place[:, :], pattern=[[1, E]], base=-99, channel_multiplier=0,
                       allow_small_or_imprecise_dtypes=True).then_inc(place_set, 1)

            def b_vector(e):
                ch = Chain(e, g_dve)
                L, top, pos, ex = LG[:, :, :], red[:, 0, :], red[:, 1, :], red[:, 2, :]
                places = place[:, :].unsqueeze(1).broadcast_to([P, T, E])
                e.wait_ge(place_set, 1)
                if kind == "gelu":
                    ch.link(e.tensor_reduce(top, L, X, ALU.max))
                    e.tensor_tensor(L, L, over_e(top), ALU.subtract).then_inc(g_exp, 1)
                    e.wait_ge(g_act, 1)
                    ch.link(e.tensor_reduce(top, L, X, ALU.add))
                    ch.link(e.reciprocal(top, top))
                    ch.link(e.tensor_tensor(L, L, over_e(top), ALU.mult))

                def best(oh, values, top):
                    ch.link(e.tensor_reduce(top, values, X, ALU.max))
                    ch.link(e.tensor_tensor(oh, values, over_e(top), ALU.is_equal))
                    ch.link(e.tensor_tensor(oh, oh, places, ALU.mult))
                    ch.link(e.tensor_reduce(pos, oh, X, ALU.min))
                    ch.link(e.tensor_tensor(oh, places, over_e(pos), ALU.is_equal))

                first, second, rest = oh1[:, :, :], oh2[:, :, :], oh3[:, :, :]
                best(first, L, top)
                ch.link(e.scalar_tensor_tensor(out=rest, in0=first, scalar=MASKED, in1=L, op0=ALU.mult, op1=ALU.add))
                best(second, rest, red[:, 3, :])
                if kind == "gelu":
                    ch.link(e.tensor_tensor(first, first, second, ALU.add))
                    ch.link(e.tensor_tensor(L, L, first, ALU.mult))
                else:
                    e.tensor_tensor(ex, red[:, 3, :], top, ALU.subtract).then_inc(g_exp, 1)
                    e.wait_ge(g_act, 1)
                    ch.link(e.tensor_scalar(red[:, 4, :], ex, 1.0, None, ALU.add))
                    ch.link(e.reciprocal(red[:, 4, :], red[:, 4, :]))
                    ch.link(e.tensor_tensor(red[:, 5, :], ex, red[:, 4, :], ALU.mult))
                    ch.link(e.tensor_tensor(first, first, over_e(red[:, 4, :]), ALU.mult))
                    ch.link(e.tensor_tensor(second, second, over_e(red[:, 5, :]), ALU.mult))
                    ch.link(e.tensor_tensor(L, first, second, ALU.add))
                ch.link(e.tensor_copy(WH[:, :, :], L))
                ch.link(e.tensor_tensor(L, L, WH[:, :, :].bitcast(F32), ALU.subtract))

            def b_scalar(e):
                e.wait_ge(g_exp, 1)
                v = LG[:, :, :] if kind == "gelu" else red[:, 2, :]
                e.activation(v, v, ACT.Exp).then_inc(g_act, 1)

            def loop_chunks(e, body):
                body(0, 0, True, False)
                with e.Fori(0, (NCH - 3) // 2) as i:
                    body(i * 2 + 1, 1, False, False)
                    body(i * 2 + 2, 0, False, False)
                body(NCH - 2, 1, False, False)
                body(NCH - 1, 0, False, True)

            def c_gpsimd(e):
                for j in range(2):
                    e.memset(ext[j][:, :, :], 0.0).then_inc(ext_zeroed, 1)
                e.wait_ge(ext_zeroed, 2)

                def body(c, par, fresh, last):
                    if not fresh:
                        e.wait_ge(w_turned, c - 1)
                    v = ext[par][:, :, :].rearrange("p t (g x) -> p g t x", g=4)
                    for g in range(4):
                        src = (WH[:, :, :].bitcast(F32), LG[:, :, :])[g % 2]
                        a = e.tensor_copy(v[:, g, :, 0:E], tiles(src, c))
                    a.then_inc(ext_ready, 1)
                loop_chunks(e, body)

            def c_tensor(e):
                def turn_tokens(c):
                    e.wait_ge(w_ready, c)
                    e.wait_ge(x_doubled, c + 1)
                    for t in range(TPC):
                        mm = e.transpose(bank[6][:, t * P:(t + 1) * P],
                                         x_dup[:, t, :, :].rearrange("p a d -> p (a d)"), ident[:, :])
                    mm.then_inc(x_turned, 1)

                def turn_weights(c, par):
                    e.wait_ge(x_low, c + 1)
                    e.wait_ge(ext_ready, c + 1)
                    for t in range(TPC):
                        mm = e.transpose(bank[6][:, t * P:(t + 1) * P], ext[par][:, t, :], ident[:, :])
                    mm.then_inc(w_turned, 1)

                def hidden(c, par, x):
                    n, r = c * E + x, x % 2
                    reused = not (isinstance(n, int) and n < 2)
                    if reused:
                        e.wait_ge(act_done, n - 1)
                    product(e, bank[r][:, :], W(name + "_w1", x), XH[par][:, :], XL[par][:, :]).then_inc(h_ready, 1)
                    if x == 0:
                        e.wait_ge(w_ready, c + 1)
                    if reused:
                        e.wait_ge(weighted, n - 1)
                    e.matmul(bank[2 + r][:, :], SEL[:, x, :], GS[par][:, :], start=True, stop=True).then_inc(wb_ready, 1)

                def output(c, par, x):
                    y = bank[4 + par]
                    n = c * E + x
                    if x == 0:
                        if not isinstance(c, int) or c >= 2:
                            e.wait_ge(y_copied, c - 1)
                        e.matmul(y[:, :], W(name + "_b2"), GS[par][:, :], start=True, stop=False, skip_group_check=True)
                    e.wait_ge(weighted, n + 1)
                    mm = e.matmul(y[(x % 2) * D:(x % 2 + 1) * D, :], w2[:, x, :], hw[x % RING][:, :],
                                  start=False, stop=(x >= E - 2), skip_group_check=True)
                    mm.then_inc(used, 1)

                def turn_out(c):
                    e.wait_ge(y_added, c)
                    e.wait_ge(y_copied, c + 1)
                    for t in range(TPC):
                        mm = e.transpose(bank[7][:, t * P:(t + 1) * P], ysb[:, t * P:(t + 1) * P], ident[:, :])
                    mm.then_inc(y_turned, 1)

                turn_tokens(0)
                turn_weights(0, 0)
                hidden(0, 0, 0)
                hidden(0, 0, 1)

                def body(c, par, fresh, last):
                    for x in range(E):
                        if x == 3 and not fresh:
                            turn_out(c - 1)
                        if x == E - 7 and not last:
                            turn_tokens(c + 1)
                        if x == E - 4 and not last:
                            turn_weights(c + 1, 1 - par)
                        if x + 2 < E:
                            hidden(c, par, x + 2)
                        elif not last:
                            hidden(c + 1, 1 - par, x + 2 - E)
                        output(c, par, x)
                loop_chunks(e, body)
                turn_out(NCH - 1)

            def c_scalar(e):
                def weights_in(c, par):
                    e.wait_ge(w_turned, c + 1)
                    if not isinstance(c, int) or c >= 2:
                        e.wait_ge(used, (c - 1) * E)
                    e.activation(GS[par][:, :], bank[6][:, :], ACT.Copy).then_inc(w_ready, 1)

                def copy_out(c, par):
                    e.wait_ge(used, (c + 1) * E)
                    if not isinstance(c, int) or c >= 1:
                        e.wait_ge(y_turned, c)
                    e.activation(ysb[:, :], bank[4 + par][:, :], ACT.Copy).then_inc(y_copied, 1)

                def double(c):
                    e.wait_ge(x_turned, c)
                    e.activation(x_dup[:, :, :, :], tiles(Y, c).unsqueeze(2).broadcast_to([P, TPC, 2, D]),
                                 ACT.Copy).then_inc(x_doubled, 1)

                def high(c, par):
                    if not isinstance(c, int) or c >= 2:
                        e.wait_ge(h_ready, (c - 1) * E)
                    e.wait_ge(x_turned, c + 1)
                    e.activation(XH[par][:, :], bank[6][:, :], ACT.Copy).then_inc(x_high, 1)

                double(0)
                high(0, 0)
                weights_in(0, 0)

                def body(c, par, fresh, last):
                    for x in range(E):
                        n = c * E + x
                        e.wait_ge(h_ready, n + 1)
                        if not isinstance(n, int) or n >= RING:
                            e.wait_ge(weighted, n - (RING - 1))
                        e.activation(hid[x % RING][:, :], bank[x % 2][:, :], func,
                                     bias=bcol(name + "_b1", x)).then_inc(act_done, 1)
                        if x == 1 and not fresh:
                            copy_out(c - 1, 1 - par)
                        if x == E - 8 and not last:
                            double(c + 1)
                        if x == E - 6 and not last:
                            high(c + 1, 1 - par)
                        if x == E - 3 and not last:
                            weights_in(c + 1, 1 - par)
                loop_chunks(e, body)
                copy_out(NCH - 1, (NCH - 1) % 2)

            def c_vector(e):
                def add_out(c):
                    e.wait_ge(y_turned, c + 1)
                    both = bank[7][:, :].rearrange("p (t a d) -> p t a d", a=2, d=D)
                    e.tensor_tensor(tiles(into, c), tiles(into, c), both[:, :, 0, :], ALU.add).then_inc(y_half, 1)
                    e.wait_ge(y_half, c + 1)
                    e.tensor_tensor(tiles(into, c), tiles(into, c), both[:, :, 1, :], ALU.add).then_inc(y_added, 1)

                def low(c, par):
                    e.wait_ge(x_high, c + 1)
                    e.tensor_tensor(XL[par][:, :], bank[6][:, :], XH[par][:, :].bitcast(F32),
                                    ALU.subtract).then_inc(x_low, 1)

                low(0, 0)

                def body(c, par, fresh, last):
                    for x in range(E):
                        if x == E - 5 and not last:
                            low(c + 1, 1 - par)
                        n = c * E + x
                        e.wait_ge(act_done, n + 1)
                        e.wait_ge(wb_ready, n + 1)
                        if not isinstance(n, int) or n >= RING:
                            e.wait_ge(used, n - (RING - 1))
                        e.tensor_tensor(hw[x % RING][:, :], hid[x % RING][:, :], bank[2 + x % 2][:, :],
                                        ALU.mult).then_inc(weighted, 1)
                        if x == 4 and not fresh:
                            add_out(c - 1)
                loop_chunks(e, body)
                add_out(NCH - 1)

            return {"a": (None, None, a_scalar, a_vector, a_tensor), "b": (None, b_gpsimd, b_scalar, b_vector, None),
                    "c": (None, c_gpsimd, c_scalar, c_vector, c_tensor)}

        ctx_a = ExitStack()
        AH = sb("a0_XH", [P, NPAD], F32R, ctx_a)
        AL = sb("a0_XL", [P, NPAD], F32R, ctx_a)
        a_tr = turner("a0", ctx_a, [bank[0], bank[1]], B * -(-NPAD // BANK))
        SPANS = [(c, min(BANK, NPAD - c)) for c in range(0, NPAD, BANK)]
        VSPANS = [(c, min(BANK, NPAD - c)) for c in range(BANK, NPAD, BANK)]
        NS, NV = len(SPANS), len(VSPANS)
        SCALE = float(DH) ** -0.5
        qf = sb("a0_qf", [P, BANK], F32, ctx_a)
        kf = sb("a0_kf", [P, BANK], F32, ctx_a)
        vf = sb("a0_vf", [P, BANK], F32, ctx_a)
        qh = sb("a0_qh", [P, BANK], F32R, ctx_a)
        ql = sb("a0_ql", [P, BANK], F32R, ctx_a)
        ks = sb("a0_ks", [P, BANK], F32R, ctx_a)
        kh = [sb(f"a0_kh{j}", [P, BANK], F32R, ctx_a) for j in range(2)]
        vx = sb("a0_vx", [P, TPC, HEADS, 32], F32, ctx_a)
        af = [sb(f"a0_af{j}", [P, BANK], F32, ctx_a) for j in range(2)]
        PR = 3
        prob = [sb(f"a0_prob{j}", [P, BANK], F32, ctx_a) for j in range(PR)]
        probT = [sb(f"a0_probT{j}", [P, TPC, BANK], F32, ctx_a) for j in range(2)]
        nmax = sb("a0_nmax", [P, TPC * HEADS], F32, ctx_a)
        oT = sb("a0_oT", [P, 2, BANK], F32, ctx_a)
        rsum = sb("a0_rsum", [P, TPC, HEADS], F32, ctx_a)
        att = [sb(f"a0_att{j}", [P, 2, D], F32, ctx_a) for j in range(2)]
        ot = [sb(f"a0_ot{j}", [P, BANK], F32, ctx_a) for j in range(2)]
        ctx_a.close()
        a_names = ("vx_set qkv_ready q_biased k_biased v_biased q_high q_low k_high k_low v_turned v_stored vv_ready "
                   "vv_biased vv_high vv_low kh_ready s_ready max_ready exp_ready p_turned p_copied_a p_copied_v o_ready "
                   "o_copied o_turned r_ready att_ready att_turned att_high att_low w_ready w_biased w_turned w_added")
        A = {n: sem("a0_" + n) for n in a_names.split()}
        TILES = HEADS * TPC

        def a0_gpsimd(e):
            e.memset(vx[:, :, :, :], 0.0).then_inc(A["vx_set"], 1)
            e.wait_ge(A["vx_set"], 1)
            e.memset(vx[:, :, :, DH:DH + 1], 1.0).then_inc(A["vx_set"], 1)

        def a0_tensor(e):
            with e.Fori(0, B) as i:
                for k, (c, w) in enumerate(SPANS):
                    turn_chunk(e, a_tr, i * NS, k, w // P)
                e.wait_ge(a_tr["low"], turned_by(a_tr, i * NS, NS))
                for j, name in enumerate("qkv"):
                    product(e, bank[2 + j][:, :], W("a0_" + name), AH[:, 0:BANK], AL[:, 0:BANK]).then_inc(A["qkv_ready"], 1)
                for k, (c, w) in enumerate(VSPANS):
                    e.wait_ge(A["vv_biased"], i * NV + max(k - 1, 0))
                    product(e, bank[5 + k % 2][:, 0:w], W("a0_v"), AH[:, c:c + w], AL[:, c:c + w]).then_inc(A["vv_ready"], 1)
                e.wait_ge(A["v_biased"], i + 1)
                for t in range(TPC):
                    mm = e.transpose(bank[7][:, t * P:(t + 1) * P], vf[:, t * P:(t + 1) * P], ident[:, :])
                mm.then_inc(A["v_turned"], 1)

                def scores(n):
                    h, t = divmod(n, TPC)
                    s = bank[n % 3]
                    e.wait_ge(A["kh_ready"], i * HEADS + (h + 1))
                    e.wait_ge(A["exp_ready"], i * TILES + max(n - 2, 0))
                    e.matmul(s[:, :], qh[:, t * P:(t + 1) * P], kh[h % 2][:, :], start=True, stop=False)
                    e.matmul(s[:, :], ql[:, t * P:(t + 1) * P], kh[h % 2][:, :], start=False, stop=False)
                    e.matmul(s[:, :], ident_bf[:, :], mask0[:, t, :], start=False, stop=True).then_inc(A["s_ready"], 1)

                def turn_probs(n):
                    b = bank[3 + n % 3]
                    e.wait_ge(A["p_copied_a"], i * (TILES // 2) + max((n - 3 + 2) // 2, 0))
                    e.wait_ge(A["p_copied_v"], i * (TILES // 2) + max((n - 3 + 1) // 2, 0))
                    e.wait_ge(A["exp_ready"], i * TILES + (n + 1))
                    for t in range(TPC):
                        mm = e.transpose(b[:, t * P:(t + 1) * P], prob[n % PR][:, t * P:(t + 1) * P], ident[:, :])
                    mm.then_inc(A["p_turned"], 1)

                def attend(h):
                    o = bank[6 + h // 4]
                    e.wait_ge(A["p_copied_a"], i * (TILES // 2) + (h + 1) * (TPC // 2))
                    e.wait_ge(A["p_copied_v"], i * (TILES // 2) + (h + 1) * (TPC // 2))
                    for t in range(TPC):
                        mm = e.matmul(o[(h % 4) * 32:(h % 4 + 1) * 32, :], vx[:, t, h, :], probT[h % 2][:, t, :],
                                      start=(t == 0), stop=(t == TPC - 1))
                    mm.then_inc(A["o_ready"], 1)

                e.wait_ge(A["q_low"], i + 1)
                e.wait_ge(A["k_low"], i + 1)
                e.wait_ge(A["vv_biased"], i * NV + NV)
                e.wait_ge(A["vx_set"], 2)
                e.wait_ge(A["v_stored"], i + 1)
                scores(0)
                scores(1)
                for n in range(TILES):
                    if n + 2 < TILES:
                        scores(n + 2)
                    turn_probs(n)
                    if n % TPC == 1 and n >= TPC:
                        attend(n // TPC - 1)
                attend(HEADS - 1)
                for t in range(TPC):
                    if t == 0:
                        e.wait_ge(A["o_copied"], i * 2 + 2)
                    if t >= 2:
                        e.wait_ge(A["att_ready"], i * TPC + (t - 1))
                    for g in range(2):
                        mm = e.transpose(bank[t % 2][:, g * P:(g + 1) * P], oT[:, g, t * P:(t + 1) * P], ident[:, :])
                    mm.then_inc(A["o_turned"], 1)
                    if t >= 1:
                        e.wait_ge(A["att_ready"], i * TPC + t)
                        e.transpose(bank[2][:, (t - 1) * P:t * P], att[(t - 1) % 2][:, :, :].rearrange("p a d -> p (a d)"),
                                    ident[:, :]).then_inc(A["att_turned"], 1)
                e.wait_ge(A["att_ready"], i * TPC + TPC)
                e.transpose(bank[2][:, (TPC - 1) * P:BANK], att[(TPC - 1) % 2][:, :, :].rearrange("p a d -> p (a d)"),
                            ident[:, :]).then_inc(A["att_turned"], 1)
                e.wait_ge(A["vv_low"], i * NV + NV)

                def project(m):
                    c, w = SPANS[A_ORDER[m]]
                    if A_ORDER[m] == 0:
                        e.wait_ge(A["att_low"], i + 1)
                    e.wait_ge(A["w_biased"], i * NS + max(m - 1, 0))
                    product(e, bank[3 + m % 2][:, 0:w], W("a0_o"), AH[:, c:c + w], AL[:, c:c + w]).then_inc(A["w_ready"], 1)

                def turn_back(m):
                    c, w = SPANS[A_ORDER[m]]
                    e.wait_ge(A["w_added"], i * NS + max(m - 1, 0))
                    e.wait_ge(A["w_biased"], i * NS + (m + 1))
                    for t in range(w // P):
                        mm = e.transpose(bank[5 + m % 2][:, t * P:(t + 1) * P], ot[m % 2][:, t * P:(t + 1) * P], ident[:, :])
                    mm.then_inc(A["w_turned"], 1)

                project(0)
                for m in range(NS):
                    if m + 1 < NS:
                        project(m + 1)
                    turn_back(m)
                e.wait_ge(A["w_added"], i * NS + NS)

        A_ORDER = list(range(1, NS)) + [0]

        def a0_scalar(e):
            with e.Fori(0, B) as i:
                e.wait_ge(A["w_ready"], i * NS)
                for k, (c, w) in enumerate(SPANS):
                    n = w // P
                    double_chunk(e, a_tr, i * NS, k, Y[:, bass.ds(i * TPB + k * TPC, n), :], n)
                    high_chunk(e, a_tr, i * NS, k, n, AH[:, c:c + w])
                e.wait_ge(A["qkv_ready"], i * 3 + 2)
                e.activation(kf[:, :], bank[3][:, :], ACT.Identity, bias=bcol("a0_bk")).then_inc(A["k_biased"], 1)
                e.wait_ge(A["qkv_ready"], i * 3 + 3)
                e.activation(vf[:, :], bank[4][:, :], ACT.Identity, bias=bcol("a0_bv")).then_inc(A["v_biased"], 1)
                for k, (c, w) in enumerate(VSPANS):
                    e.wait_ge(A["vv_low"], i * NV + max(k - 1, 0))
                    e.wait_ge(A["vv_ready"], i * NV + (k + 1))
                    e.activation(af[k % 2][:, 0:w], bank[5 + k % 2][:, 0:w], ACT.Identity,
                                 bias=bcol("a0_bv")).then_inc(A["vv_biased"], 1)
                    e.wait_ge(A["vv_biased"], i * NV + (k + 1))
                    e.activation(AH[:, c:c + w], af[k % 2][:, 0:w], ACT.Copy).then_inc(A["vv_high"], 1)
                for n in range(TILES + 1):
                    if n < TILES:
                        e.wait_ge(A["max_ready"], i * TILES + (n + 1))
                        e.wait_ge(A["p_turned"], i * TILES + max(n - PR + 1, 0))
                        e.activation(prob[n % PR][:, :], bank[n % 3][:, :], ACT.Exp,
                                     bias=nmax[:, n:n + 1]).then_inc(A["exp_ready"], 1)
                    if n >= 1 and (n - 1) % 2 == 0:
                        copy_probs(e, i, n - 1, "p_copied_a")
                for g in range(2):
                    e.wait_ge(A["o_ready"], i * HEADS + 4 * (g + 1))
                    e.activation(oT[:, g, :], bank[6 + g][:, :], ACT.Copy).then_inc(A["o_copied"], 1)
                e.wait_ge(A["att_turned"], i * TPC + TPC)
                e.activation(AH[:, 0:BANK], bank[2][:, :], ACT.Copy).then_inc(A["att_high"], 1)
                for m in range(NS):
                    c, w = SPANS[A_ORDER[m]]
                    e.wait_ge(A["w_turned"], i * NS + max(m - 1, 0))
                    e.wait_ge(A["w_ready"], i * NS + (m + 1))
                    e.activation(ot[m % 2][:, 0:w], bank[3 + m % 2][:, 0:w], ACT.Identity,
                                 bias=bcol("a0_bo")).then_inc(A["w_biased"], 1)

        def copy_probs(e, i, n, done):
            h, t = divmod(n, TPC)
            e.wait_ge(A["o_ready"], i * HEADS + max(h - 1, 0))
            e.wait_ge(A["p_turned"], i * TILES + (n + 1))
            dst = probT[h % 2][:, :, t * P:(t + 1) * P]
            src = bank[3 + n % 3][:, :].rearrange("p (k q) -> p k q", k=TPC)
            if done == "p_copied_a":
                e.activation(dst, src, ACT.Copy).then_inc(A[done], 1)
            else:
                e.tensor_copy(dst, src).then_inc(A[done], 1)

        def a0_vector(e):
            with e.Fori(0, B) as i:
                for k, (c, w) in enumerate(SPANS):
                    low_chunk(e, a_tr, i * NS, k, w // P, AH[:, c:c + w], AL[:, c:c + w])
                e.wait_ge(A["qkv_ready"], i * 3 + 1)
                e.tensor_scalar(qf[:, :], bank[2][:, :], bcol("a0_bq"), SCALE, ALU.add, ALU.mult).then_inc(A["q_biased"], 1)
                e.wait_ge(A["q_biased"], i + 1)
                e.tensor_copy(qh[:, :], qf[:, :]).then_inc(A["q_high"], 1)
                e.wait_ge(A["q_high"], i + 1)
                e.tensor_tensor(ql[:, :], qf[:, :], qh[:, :].bitcast(F32), ALU.subtract).then_inc(A["q_low"], 1)
                e.wait_ge(A["k_biased"], i + 1)
                e.tensor_copy(ks[:, :], kf[:, :]).then_inc(A["k_high"], 1)
                e.wait_ge(A["k_high"], i + 1)
                e.tensor_tensor(ks[D:P, :], kf[D:P, :], ks[D:P, :].bitcast(F32), ALU.subtract).then_inc(A["k_low"], 1)
                for k, (c, w) in enumerate(VSPANS):
                    e.wait_ge(A["vv_high"], i * NV + (k + 1))
                    e.tensor_tensor(AL[:, c:c + w], af[k % 2][:, 0:w], AH[:, c:c + w].bitcast(F32),
                                    ALU.subtract).then_inc(A["vv_low"], 1)
                e.wait_ge(A["vx_set"], 2)
                e.wait_ge(A["v_turned"], i + 1)
                e.tensor_copy(vx[:, :, :, 0:DH], bank[7][:, :].rearrange("p (t c) -> p t c", c=P)[:, :, 0:D]
                              .rearrange("p t (h d) -> p t h d", d=DH)).then_inc(A["v_stored"], 1)
                e.wait_ge(A["k_low"], i + 1)
                for n in range(TILES + 1):
                    h = n // TPC
                    if n < TILES:
                        if n % TPC == 0:
                            e.wait_ge(A["s_ready"], i * TILES + max((h - 1) * TPC, 0))
                            e.tensor_scalar(kh[h % 2][:, :], ks[:, :].bitcast(F32), head_rows[:, h:h + 1], None,
                                            ALU.mult).then_inc(A["kh_ready"], 1)
                        e.wait_ge(A["s_ready"], i * TILES + (n + 1))
                        e.tensor_reduce(nmax[:, n:n + 1], bank[n % 3][:, :], X, ALU.max, negate=True).then_inc(A["max_ready"], 1)
                    if n >= 1 and (n - 1) % 2 == 1:
                        copy_probs(e, i, n - 1, "p_copied_v")
                for t in range(TPC):
                    o = bank[t % 2][:, 0:2 * P].rearrange("p (h x) -> p h x", x=32)
                    e.wait_ge(A["o_turned"], i * TPC + (t + 1))
                    e.reciprocal(rsum[:, t, :], o[:, :, DH]).then_inc(A["r_ready"], 1)
                    e.wait_ge(A["r_ready"], i * TPC + (t + 1))
                    e.wait_ge(A["att_turned"], i * TPC + max(t - 1, 0))
                    for m in range(2):
                        a = e.tensor_tensor(att[t % 2][:, m, :].rearrange("p (h d) -> p h d", d=DH), o[:, :, 0:DH],
                                            rsum[:, t, :].unsqueeze(2).broadcast_to([P, HEADS, DH]), ALU.mult)
                    a.then_inc(A["att_ready"], 1)
                e.wait_ge(A["att_high"], i + 1)
                e.tensor_tensor(AL[:, 0:BANK], bank[2][:, :], AH[:, 0:BANK].bitcast(F32), ALU.subtract).then_inc(A["att_low"], 1)
                for m in range(NS):
                    k = A_ORDER[m]
                    n = SPANS[k][1] // P
                    e.wait_ge(A["w_turned"], i * NS + (m + 1))
                    yt = Y[:, bass.ds(i * TPB + k * TPC, n), :]
                    e.tensor_tensor(yt, yt, bank[5 + m % 2][:, :].rearrange("p (t c) -> p t c", c=P)[:, 0:n, 0:D],
                                    ALU.add).then_inc(A["w_added"], 1)

        f0 = ffn("f0", E0, f0_w2, "relu", Y)

        ctx_b = ExitStack()
        QH = sb("a1_QH", [P, NPAD], F32R, ctx_b)
        QL = sb("a1_QL", [P, NPAD], F32R, ctx_b)
        KS = sb("a1_KS", [P, NPAD], F32R, ctx_b)
        b_tr = turner("a1", ctx_b, [bank[0], bank[1]], B * NS)
        qf1 = [sb(f"a1_qf{j}", [P, BANK], F32, ctx_b) for j in range(2)]
        kf1 = sb("a1_kf", [P, BANK], F32, ctx_b)
        vf1 = sb("a1_vf", [P, BANK], F32, ctx_b)
        V = sb("a1_V", [P, TPB, D], F32, ctx_b)
        PB = 2
        pT = [sb(f"a1_pT{j}", [P, NS, BANK], F32, ctx_b) for j in range(PB)]
        vs = [sb(f"a1_vs{j}", [P, NS, D], F32, ctx_b) for j in range(2)]
        oS = sb("a1_oS", [P, 4, BANK], F32, ctx_b)
        nm = [sb(f"a1_nm{j}", [P, NS], F32, ctx_b) for j in range(2)]
        sm = [sb(f"a1_sm{j}", [P, NS], F32, ctx_b) for j in range(2)]
        fc = [sb(f"a1_fc{j}", [P, NS], F32, ctx_b) for j in range(2)]
        tot = [sb(f"a1_tot{j}", [P, 4], F32, ctx_b) for j in range(2)]
        later = sb("a1_later", [P, P], BF16, ctx_b)
        laterf = sb("a1_laterf", [P, BANK], F32, ctx_b)
        first_key = sb("a1_first", [P, 1], F32, ctx_b)
        ctx_b.close()
        b_names = ("set qkv_ready q_scaled k_copied v_copied q_high q_low k_high k_low v_turned v_stored s_ready masked "
                   "max_ready exp_ready min_ready f_ready dve scaled pv_done o_ready o_copied o_turned o_added")
        Z = {n: sem("a1_" + n) for n in b_names.split()}
        MASK_ALL = -1.0e10 / 8.0

        def widths(j):
            if j == 0:
                return [min(BANK, N - c * BANK) for c in range(NS)]
            end = min((j + 1) * P, N)
            return [min(BANK, end - c * BANK) for c in range(j // TPC + 1)]

        first_chunk, at_chunk = [], 0
        for j in range(TPB):
            first_chunk.append(at_chunk)
            at_chunk += len(widths(j))
        CHUNKS = at_chunk
        RS = 4
        SMALL = 4

        def a1_gpsimd(e):
            e.memset(V[:, :, :], 0.0).then_inc(Z["set"], 1)
            e.memset(oS[:, :, :], 0.0).then_inc(Z["set"], 1)
            e.memset(laterf[:, :], 0.0).then_inc(Z["set"], 1)
            e.memset(first_key[:, :], MASKED).then_inc(Z["set"], 1)
            e.wait_ge(Z["set"], 4)
            e.memset(first_key[0:1, :], MASK_ALL).then_inc(Z["set"], 1)
            e.affine_select(out=laterf[:, :], in_=laterf[:, :], compare_op=ALU.is_gt, fill=MASKED, base=0,
                            pattern=[[-1, BANK]], channel_multiplier=1).then_inc(Z["set"], 1)
            e.wait_ge(Z["set"], 6)
            e.tensor_copy(later[:, :], laterf[:, 0:P]).then_inc(Z["set"], 1)
            e.wait_ge(Z["set"], 7)
            e.memset(laterf[0:1, :], MASK_ALL).then_inc(Z["set"], 1)
            with e.Fori(0, B) as i:
                for j in range(TPB):
                    nc_ = len(widths(j))
                    e.wait_ge(Z["pv_done"], i * CHUNKS + (first_chunk[j - 1] if j >= 1 else 0))
                    e.wait_ge(Z["dve"], i * (TPB * SMALL) + (j + 1) * SMALL)
                    e.tensor_tensor(vs[j % 2][:, 0:nc_, :], V[:, j, :].unsqueeze(1).broadcast_to([P, nc_, D]),
                                    fc[j % 2][:, 0:nc_].unsqueeze(2).broadcast_to([P, nc_, D]),
                                    ALU.mult).then_inc(Z["scaled"], 1)

        def a1_tensor(e):
            e.wait_ge(Z["set"], 8)
            with e.Fori(0, B) as i:
                def projections(k):
                    c, w = SPANS[k]
                    hi, lo = QH[:, c:c + w], QL[:, c:c + w]
                    e.wait_ge(b_tr["low"], turned_by(b_tr, i * NS, k + 1))
                    e.wait_ge(Z["q_scaled"], i * NS + k)
                    product(e, bank[2][:, 0:w], W("a1_q"), hi, lo)
                    e.wait_ge(Z["k_copied"], i * NS + k)
                    product(e, bank[3][:, 0:w], W("a1_k"), hi, lo)
                    e.wait_ge(Z["v_copied"], i * NS + k)
                    product(e, bank[4][:, 0:w], W("a1_v"), hi, lo).then_inc(Z["qkv_ready"], 1)

                def values(k):
                    e.wait_ge(Z["v_stored"], i * NS + max(k - 1, 0))
                    e.wait_ge(Z["v_copied"], i * NS + (k + 1))
                    for t in range(SPANS[k][1] // P):
                        mm = e.transpose(bank[5 + k % 2][:, t * P:(t + 1) * P], vf1[:, t * P:(t + 1) * P], ident[:, :])
                    mm.then_inc(Z["v_turned"], 1)

                turn_chunk(e, b_tr, i * NS, 0, SPANS[0][1] // P)
                for k in range(NS):
                    if k + 1 < NS:
                        turn_chunk(e, b_tr, i * NS, k + 1, SPANS[k + 1][1] // P)
                    projections(k)
                    values(k)

                def scores(j, c):
                    n = first_chunk[j] + c
                    w = widths(j)[c]
                    s = bank[n % RS]
                    e.wait_ge(Z["exp_ready"], i * CHUNKS + max(n + 1 - RS, 0))
                    diagonal = j > 0 and c == len(widths(j)) - 1
                    k = KS[:, j * P:(j + 1) * P]
                    e.matmul(s[:, 0:w], k, QH[:, c * BANK:c * BANK + w], start=True, stop=False)
                    if diagonal:
                        lo = j * P - c * BANK
                        e.matmul(s[:, lo:w], ident_bf[:, :], later[:, 0:w - lo], start=False, stop=False,
                                 skip_group_check=True)
                    mm = e.matmul(s[:, 0:w], k, QL[:, c * BANK:c * BANK + w], start=False, stop=True)
                    mm.then_inc(Z["s_ready"], 1)

                def attend(j):
                    e.wait_ge(Z["scaled"], i * TPB + (j + 1))
                    for c, w in enumerate(widths(j)):
                        n = first_chunk[j] + c
                        r = c % 2
                        mm = e.matmul(bank[4 + c // 2][r * D:(r + 1) * D, 0:w], vs[j % 2][:, c, :], pT[j % PB][:, c, 0:w],
                                      start=(j == 0), stop=(j == TPB - 1), skip_group_check=True)
                        mm.then_inc(Z["pv_done"], 1)

                e.wait_ge(Z["q_low"], i * NS + NS)
                e.wait_ge(Z["k_low"], i * NS + NS)
                e.wait_ge(Z["v_stored"], i * NS + NS)
                for j in range(TPB + 1):
                    ahead = widths(j) if j < TPB else []
                    split = min(len(ahead), RS - 1)
                    for c in range(split):
                        scores(j, c)
                    if j >= 2:
                        attend(j - 2)
                    for c in range(split, len(ahead)):
                        scores(j, c)
                attend(TPB - 1)
                for q in range(4):
                    e.wait_ge(Z["o_added"], i * 4 + max(q - 1, 0))
                    e.wait_ge(Z["o_copied"], i * 4 + (q + 1))
                    for t in range(TPC if q < 3 else 1):
                        mm = e.transpose(bank[q % 2][:, t * P:(t + 1) * P], oS[:, q, t * P:(t + 1) * P], ident[:, :])
                    mm.then_inc(Z["o_turned"], 1)
                e.wait_ge(Z["o_added"], i * 4 + 4)

        def a1_scalar(e):
            with e.Fori(0, B) as i:
                e.wait_ge(Z["s_ready"], i * CHUNKS)

                def tokens(k):
                    c, w = SPANS[k]
                    n = w // P
                    double_chunk(e, b_tr, i * NS, k, Y[:, bass.ds(i * TPB + k * TPC, n), :], n)
                    high_chunk(e, b_tr, i * NS, k, n, QH[:, c:c + w])

                tokens(0)
                for k, (c, w) in enumerate(SPANS):
                    if k + 1 < NS:
                        tokens(k + 1)
                    e.wait_ge(Z["qkv_ready"], i * NS + (k + 1))
                    e.wait_ge(Z["q_low"], i * NS + max(k - 1, 0))
                    e.activation(qf1[k % 2][:, 0:w], bank[2][:, 0:w], ACT.Copy, scale=1.0 / 8.0).then_inc(Z["q_scaled"], 1)
                    e.wait_ge(Z["k_low"], i * NS + k)
                    e.activation(kf1[:, 0:w], bank[3][:, 0:w], ACT.Copy).then_inc(Z["k_copied"], 1)
                    e.wait_ge(Z["v_turned"], i * NS + k)
                    e.activation(vf1[:, 0:w], bank[4][:, 0:w], ACT.Copy).then_inc(Z["v_copied"], 1)
                for j in range(TPB):
                    for c, w in enumerate(widths(j)):
                        n = first_chunk[j] + c
                        p = pT[j % PB][:, c, 0:w]
                        e.wait_ge(Z["max_ready"], i * CHUNKS + (n + 1))
                        if j >= PB:
                            e.wait_ge(Z["pv_done"], i * CHUNKS + (first_chunk[j - PB] + min(c, len(widths(j - PB)) - 1) + 1))
                            if c == 0:
                                e.wait_ge(Z["dve"], i * (TPB * SMALL) + (j - 1) * SMALL)
                        src = p if j == 0 else bank[n % RS][:, 0:w]
                        e.activation(p, src, ACT.Exp, bias=nm[j % 2][:, c:c + 1],
                                     accum_out=sm[j % 2][:, c:c + 1]).then_inc(Z["exp_ready"], 1)
                    e.wait_ge(Z["min_ready"], i * TPB + (j + 1))
                    e.wait_ge(Z["scaled"], i * TPB + max(j - 1, 0))
                    nc_ = len(widths(j))
                    e.activation(fc[j % 2][:, 0:nc_], nm[j % 2][:, 0:nc_], ACT.Exp, bias=tot[j % 2][:, 0:1],
                                 scale=-1.0).then_inc(Z["f_ready"], 1)
                for q in range(4):
                    e.wait_ge(Z["pv_done"], i * CHUNKS + CHUNKS)
                    if q < 3:
                        a = e.activation(oS[:, q, :], bank[4 + q][:, :], ACT.Copy)
                    else:
                        a = e.activation(oS[0:D, q, 0:LAST], bank[4 + q][0:D, 0:LAST], ACT.Copy)
                    a.then_inc(Z["o_copied"], 1)

        def a1_vector(e):
            e.wait_ge(Z["set"], 8)
            with e.Fori(0, B) as i:
                low_chunk(e, b_tr, i * NS, 0, SPANS[0][1] // P, QH[:, 0:BANK], QL[:, 0:BANK])
                for k, (c, w) in enumerate(SPANS):
                    if k + 1 < NS:
                        c2, w2 = SPANS[k + 1]
                        low_chunk(e, b_tr, i * NS, k + 1, w2 // P, QH[:, c2:c2 + w2], QL[:, c2:c2 + w2])
                    e.wait_ge(Z["q_scaled"], i * NS + (k + 1))
                    e.tensor_copy(QH[:, c:c + w], qf1[k % 2][:, 0:w]).then_inc(Z["q_high"], 1)
                    e.wait_ge(Z["k_copied"], i * NS + (k + 1))
                    e.tensor_copy(KS[:, c:c + w], kf1[:, 0:w]).then_inc(Z["k_high"], 1)
                    e.wait_ge(Z["q_high"], i * NS + (k + 1))
                    e.tensor_tensor(QL[:, c:c + w], qf1[k % 2][:, 0:w], QH[:, c:c + w].bitcast(F32),
                                    ALU.subtract).then_inc(Z["q_low"], 1)
                    e.wait_ge(Z["k_high"], i * NS + (k + 1))
                    e.tensor_tensor(KS[D:P, c:c + w], kf1[D:P, 0:w], KS[D:P, c:c + w].bitcast(F32),
                                    ALU.subtract).then_inc(Z["k_low"], 1)
                    e.wait_ge(Z["v_turned"], i * NS + (k + 1))
                    n = w // P
                    hi = P if k < NS - 1 else LAST
                    e.tensor_copy(V[0:hi, k * TPC:k * TPC + n, :],
                                  bank[5 + k % 2][0:hi, :].rearrange("p (t c) -> p t c", c=P)[:, 0:n, 0:D]
                                  ).then_inc(Z["v_stored"], 1)

                def tile_sums(j):
                    nc_ = len(widths(j))
                    r = j % 2
                    ch = Chain(e, Z["dve"], j * SMALL, i, TPB * SMALL)
                    e.wait_ge(Z["f_ready"], i * TPB + (j + 1))
                    ch.link(e.tensor_tensor(sm[r][:, 0:nc_], sm[r][:, 0:nc_], fc[r][:, 0:nc_], ALU.mult))
                    ch.link(e.tensor_reduce(tot[r][:, 1:2], sm[r][:, 0:nc_], X, ALU.add))
                    ch.link(e.reciprocal(tot[r][:, 2:3], tot[r][:, 1:2]))
                    ch.mark(e.tensor_scalar(fc[r][:, 0:nc_], fc[r][:, 0:nc_], tot[r][:, 2:3], None, ALU.mult))

                for j in range(TPB):
                    ws = widths(j)
                    for c, w in enumerate(ws):
                        n = first_chunk[j] + c
                        src = bank[n % RS][:, 0:w]
                        e.wait_ge(Z["s_ready"], i * CHUNKS + (n + 1))
                        if j == 0:
                            src = pT[0][:, c, 0:w]
                            e.wait_ge(Z["pv_done"], i * CHUNKS)
                            if c == 0:
                                a = e.tensor_tensor(src, bank[n % RS][:, 0:w], laterf[:, 0:w], ALU.add)
                            else:
                                a = e.tensor_scalar(src, bank[n % RS][:, 0:w], first_key[:, :], None, ALU.add)
                            a.then_inc(Z["masked"], 1)
                            e.wait_ge(Z["masked"], i * NS + (n + 1))
                        e.tensor_reduce(nm[j % 2][:, c:c + 1], src, X, ALU.max, negate=True).then_inc(Z["max_ready"], 1)
                        if j >= 1 and c == min(1, len(ws) - 1):
                            tile_sums(j - 1)
                    e.wait_ge(Z["max_ready"], i * CHUNKS + (first_chunk[j] + len(ws)))
                    e.tensor_reduce(tot[j % 2][:, 0:1], nm[j % 2][:, 0:len(ws)], X, ALU.min).then_inc(Z["min_ready"], 1)
                tile_sums(TPB - 1)
                for q in range(4):
                    e.wait_ge(Z["o_turned"], i * 4 + (q + 1))
                    if q < 3:
                        h = H[:, bass.ds(i * TPB + 2 * q * TPC, 2 * TPC), :].rearrange("p (a t) d -> p t a d", a=2)
                        o = bank[q % 2][:, :].rearrange("p (t a d) -> p t a d", a=2, d=D)
                        e.tensor_tensor(h, h, o, ALU.add).then_inc(Z["o_added"], 1)
                    else:
                        h = H[0:LAST, bass.ds(i * TPB + 2 * q * TPC, 1), :].rearrange("p t d -> p (t d)")
                        e.tensor_tensor(h, h, bank[q % 2][0:LAST, 0:D], ALU.add).then_inc(Z["o_added"], 1)

        stages = [
            (weights_sync, weights_gpsimd, weights_scalar, weights_vector, weights_tensor),
            (tok_sync, tok_gpsimd, tok_scalar, tok_vector, tok_tensor),
        ]
        def norm(k, src, affine=None):
            return (None, (lambda e: norm_gpsimd(e, affine)) if affine is not None else None,
                    lambda e: norm_scalar(e, k), lambda e: norm_vector(e, k, src, affine), None)
        f1 = ffn("f1", E1, f1_w2, "gelu", H)
        stages += [norm(0, H), (None, a0_gpsimd, a0_scalar, a0_vector, a0_tensor), norm(1, Y, 0)]
        stages += [norm(2, H), f0["a"], f0["b"], f0["c"], norm(3, Y, 2)]
        stages += [norm(4, H), (None, a1_gpsimd, a1_scalar, a1_vector, a1_tensor)]
        stages += [norm(5, H), f1["a"], f1["b"], f1["c"]]

        block = ctx.enter_context(nc.Block())

        def run(e, which):
            for k, st in enumerate(stages):
                if st[which] is not None:
                    st[which](e)
                stage_end(e, k + 1)

        @block.sync
        def _(e):
            run(e, 0)
            for b in range(B):
                e.dma_start(out[b, 0:(TPB - 1) * P, :].rearrange("(t p) d -> p t d", p=P),
                            H[:, b * TPB:(b + 1) * TPB - 1, :]).then_inc(stored, 16)
                e.dma_start(out[b, (TPB - 1) * P:N, :], H[0:LAST, (b + 1) * TPB - 1, :]).then_inc(stored, 16)
            e.wait_ge(stored, 2 * B * 16)

        @block.gpsimd
        def _(e):
            run(e, 1)

        @block.scalar
        def _(e):
            run(e, 2)

        @block.vector
        def _(e):
            run(e, 3)

        @block.tensor
        def _(e):
            run(e, 4)


_INS = ["x", "txt", "L0_tok_W1", "L0_tok_b1", "L0_tok_W2", "L0_tok_b2", "L0_tok_W3", "L0_tok_b3",
        "L0_attn_edge_index", "L0_attn_Wq", "L0_attn_bq", "L0_attn_Wk", "L0_attn_bk", "L0_attn_Wv", "L0_attn_bv",
        "L0_attn_Wo", "L0_attn_bo", "L0_attn_gamma", "L0_attn_beta", "L0_ffn_gate_w", "L0_ffn_gate_b",
        "L0_ffn_w1", "L0_ffn_b1", "L0_ffn_w2", "L0_ffn_b2", "L0_ffn_gamma", "L0_ffn_beta", "L1_attn_Wq",
        "L1_attn_Wk", "L1_attn_Wv", "L1_ffn_gate_w", "L1_ffn_gate_b", "L1_ffn_W1", "L1_ffn_b1", "L1_ffn_W2",
        "L1_ffn_b2"]


def kernel(**inputs):
    import numpy as _np
    import concourse.bacc as _bacc
    from concourse import mybir as _mybir
    from concourse.bass_utils import run_bass_kernel_spmd as _run

    nc = _bacc.Bacc("TRN2", target_bir_lowering=False, num_devices=1)
    arrays, ins = {}, {}
    for name in _INS:
        a = _np.ascontiguousarray(inputs[name])
        arrays[f"in_{name}_dram"] = a
        ins[name] = nc.dram_tensor(f"in_{name}_dram", a.shape, _mybir.dt.from_np(a.dtype), kind="ExternalInput").ap()
    shape = (inputs["x"].shape[0], inputs["x"].shape[2] * inputs["x"].shape[3] + inputs["txt"].shape[1],
             inputs["x"].shape[1])
    out = nc.dram_tensor("out_0_dram", shape, _mybir.dt.float32, kind="ExternalOutput").ap()
    build(nc, ins, out)
    r = _run(nc, [arrays], core_ids=[0])
    return r.results[0]["out_0_dram"]
```

```python
from contextlib import ExitStack

import concourse.bass as bass
from concourse import mybir

F32 = mybir.dt.float32
F32R = mybir.dt.float32r
BF16 = mybir.dt.bfloat16
F16 = mybir.dt.float16
I32 = mybir.dt.int32
ALU = mybir.AluOpType
ACT = mybir.ActivationFunctionType
X = mybir.AxisListType.X

P = 128
BANK = 512
START = 1
MASKED = -1.0e30
LN_EPS = 1e-5


class Chain:

    def __init__(self, eng, sem, done=0, turn=None, per=0):
        self.eng, self.sem, self.done, self.turn, self.per, self.n = eng, sem, done, turn, per, 0

    def mark(self, ins):
        ins.then_inc(self.sem, 1)
        self.n += 1
        return ins

    def value(self):
        return self.done + self.n if self.turn is None else self.turn * self.per + (self.done + self.n)

    def wait(self):
        self.eng.wait_ge(self.sem, self.value())

    def link(self, ins):
        self.mark(ins)
        self.wait()

    def close(self):
        assert self.turn is None or self.n == self.per, (self.n, self.per)
        return self.n


def build(nc, I, out):
    B, C, IH, IW = I["x"].shape
    TXT = I["txt"].shape[1]
    D = C
    IMG = IH * IW
    N = IMG + TXT
    TPB = -(-N // P)
    LAST = N - (TPB - 1) * P
    NPAD = TPB * P
    T = B * TPB
    NCH = T * P // BANK
    TPC = BANK // P
    TAPS = 9
    G5 = 5
    PW = IW + 2
    PAIRS = [(0, 1), (3, 4), (6, 7), (2, 5), (8, None)]
    ROWS = 8
    CT = ROWS * IW
    HALF = CT // 2
    CPB = IH // ROWS
    E0, _, F = I["L0_ffn_w1"].shape
    E1 = I["L1_ffn_W1"].shape[0]
    HEADS = 8
    DH = D // HEADS
    assert T * P % BANK == 0 and F == P and D == 64

    def off(tap):
        return (tap // 3) * PW + tap % 3

    cols, at = {}, 0
    for name, n in (("tok_w2", G5 * P), ("a0_q", P), ("a0_k", P), ("a0_v", P), ("a0_o", P), ("f0_g", P),
                    ("f0_w1", E0 * P), ("a1_q", P), ("a1_k", P), ("a1_v", P), ("f1_g", P),
                    ("f1_w1", E1 * P)):
        cols[name] = at
        at += n
    WCOLS = at
    rows, at = {}, 0
    for name, n in (("f0_b1", E0), ("f1_b1", E1), ("tok_b1", 1), ("tok_b3", 1), ("a0_bq", 1), ("a0_bk", 1),
                    ("a0_bv", 1), ("a0_bo", 1), ("f0_gb", 1), ("f1_gb", 1), ("tok_b2", G5), ("f0_b2", E0 // 2),
                    ("f1_b2", E1 // 2)):
        rows[name] = at
        at += n
    NBIAS = at

    with ExitStack() as ctx:
        def sb(name, shape, dt=F32, stack=ctx):
            return stack.enter_context(nc.sbuf_tensor(name, shape, dt))

        def sem(name):
            return ctx.enter_context(nc.semaphore(name))

        bank = [ctx.enter_context(nc.psum_tensor(f"bank{i}", [P, BANK], F32)) for i in range(8)]

        H = sb("H", [P, T, D])
        WS = sb("WS", [P, WCOLS], F32R)
        tok_w1 = sb("tok_w1", [P, G5, D])
        tok_w3 = sb("tok_w3", [P, G5, D])
        f0_w2 = sb("f0_w2", [P, E0, D])
        f1_w2 = sb("f1_w2", [P, E1, D])
        bias = sb("bias", [P, NBIAS])
        gb = sb("gb", [P, 4, D])
        ident = sb("ident", [P, P])
        SEL = sb("SEL", [P, max(E0, E1), D], F32R)
        head_rows = sb("head_rows", [P, HEADS])
        ident_bf = sb("ident_bf", [P, P], BF16)
        mask0 = sb("mask0", [P, TPC, BANK], BF16)
        E_PER = I["L0_attn_edge_index"].shape[1] // P
        edges_f = sb("edges_f", [P, 2, E_PER])
        node = sb("node", [P, BANK], F16)
        row_bias = sb("row_bias", [P, 2, D])
        any_far = sb("any_far", [1, 1], I32)

        stage_done = sem("stage_done")
        stored = sem("stored")

        ln_dve = sem("ln_dve")
        ln_centred = sem("ln_centred")
        ln_squared = sem("ln_squared")
        ln_var = sem("ln_var")
        ln_std = sem("ln_std")

        def W(name, i=0, n=P):
            return WS[:, cols[name] + i * P:cols[name] + i * P + n]

        def bcol(name, i=0, lo=0, hi=P):
            return bias[lo:hi, rows[name] + i:rows[name] + i + 1]

        LOADS = [0]

        def stage_end(e, k):
            e.drain().then_inc(stage_done, 1)
            e.wait_ge(stage_done, 5 * k)

        ctx_w = ExitStack()
        WF = sb("WF", [P, WCOLS], F32, ctx_w)
        sel_f = sb("sel_f", [P, max(E0, E1), D], F32, ctx_w)
        tok_w2_raw = sb("tok_w2_raw", [P, D * TAPS], F32, ctx_w)
        brow = sb("brow", [P, P], F32, ctx_w)
        wt = sb("wt", [D, 3, P], F32, ctx_w)
        edges = sb("edges", [P, 2, E_PER], I32, ctx_w)
        negative = sb("negative", [P, 2, E_PER], F32, ctx_w)
        e_max = sb("e_max", [P, 1], F32, ctx_w)
        e_top = sb("e_top", [1, 2], F32, ctx_w)
        HOTS = 4
        hot = sb("hot", [P, HOTS, 2, BANK], BF16, ctx_w)
        w_zeroed = sem("w_zeroed")
        edges_loaded = sem("edges_loaded")
        w_loaded = sem("w_loaded")
        edges_cast = sem("edges_cast")
        w_sorted = sem("w_sorted")
        w_rounded = sem("w_rounded")
        ident_set = sem("ident_set")
        tables_turned = sem("tables_turned")
        tables_copied = sem("tables_copied")
        hot_ready = sem("hot_ready")
        hot_used = sem("hot_used")
        counts_zeroed = sem("counts_zeroed")
        mask_thresholded = sem("mask_thresholded")
        sel_set = sem("sel_set")
        heads_set = sem("heads_set")

        def weights_sync(e):
            def load(dst, src, **kw):
                e.dma_start(dst, src, **kw).then_inc(w_loaded, 16)
                LOADS[0] += 1

            e.dma_start(edges[:, :, :], I["L0_attn_edge_index"].rearrange("a (p j) -> p a j", p=P)).then_inc(edges_loaded, 16)
            load(gb[:, 0, :], I["L0_attn_gamma"].partition_broadcast(P))
            load(gb[:, 1, :], I["L0_attn_beta"].partition_broadcast(P))
            load(gb[:, 2, :], I["L0_ffn_gamma"].partition_broadcast(P))
            load(gb[:, 3, :], I["L0_ffn_beta"].partition_broadcast(P))
            load(row_bias[:, 0, :], I["L0_attn_bv"].partition_broadcast(P))
            load(row_bias[:, 1, :], I["L0_attn_bo"].partition_broadcast(P))
            load(f0_w2[:, :, :], I["L0_ffn_w2"].rearrange("e f n -> f e n"))
            load(f1_w2[:, :, :], I["L1_ffn_W2"].rearrange("e f n -> f e n"))
            for i, name in enumerate("qkv"):
                for m in (0, D):
                    load(wt[0:D, i, m:m + D], I["L1_attn_W" + name])
            e.wait_ge(w_zeroed, 5)
            for lo in (0, D):
                half = WF[lo:lo + D, :]
                load(half[:, cols["f0_w1"]:cols["f0_w1"] + E0 * P].rearrange("k (e m) -> k e m", e=E0),
                     I["L0_ffn_w1"].rearrange("e k m -> k e m"))
                load(half[:, cols["f1_w1"]:cols["f1_w1"] + E1 * P].rearrange("k (e m) -> k e m", e=E1),
                     I["L1_ffn_W1"].rearrange("e k m -> k e m"))
                load(half[:, cols["f0_g"]:cols["f0_g"] + E0], I["L0_ffn_gate_w"])
                load(half[:, cols["f1_g"]:cols["f1_g"] + E1], I["L1_ffn_gate_w"])
                for name in "qkvo":
                    for m in (0, D):
                        c = cols["a0_" + name] + m
                        load(half[:, c:c + D], I["L0_attn_W" + name])
                load(tok_w2_raw[lo:lo + D, :], I["L0_tok_W2"])
            for name, src, n in (("f0_b2", "L0_ffn_b2", E0), ("f1_b2", "L1_ffn_b2", E1)):
                load(brow[rows[name]:rows[name] + n // 2, :], I[src].rearrange("(p a) d -> p (a d)", a=2))
            w1_taps = I["L0_tok_W1"].rearrange("(c t) n -> t c n", t=TAPS)
            w3_taps = I["L0_tok_W3"].rearrange("(c t) n -> t c n", t=TAPS)
            b2_taps = I["L0_tok_b2"].rearrange("(o c t) -> t o c", t=TAPS, o=1)
            for g, pair in enumerate(PAIRS):
                for h, tap in enumerate(pair):
                    if tap is not None:
                        load(tok_w1[h * D:(h + 1) * D, g, :], w1_taps[tap])
                        load(tok_w3[h * D:(h + 1) * D, g, :], w3_taps[tap])
                        r = rows["tok_b2"] + g
                        load(brow[r:r + 1, h * D:(h + 1) * D], b2_taps[tap], allow_slow_non_contiguous=True)
            load(brow[rows["f0_b1"]:rows["f0_b1"] + E0, :], I["L0_ffn_b1"])
            load(brow[rows["f1_b1"]:rows["f1_b1"] + E1, :], I["L1_ffn_b1"])
            for name, src in (("tok_b1", "L0_tok_b1"), ("tok_b3", "L0_tok_b3"), ("a0_bq", "L0_attn_bq"),
                              ("a0_bk", "L0_attn_bk"), ("a0_bv", "L0_attn_bv"), ("a0_bo", "L0_attn_bo")):
                for m in (0, D):
                    load(brow[rows[name]:rows[name] + 1, m:m + D], I[src].rearrange("(o n) -> o n", o=1))
            load(brow[rows["f0_gb"]:rows["f0_gb"] + 1, 0:E0], I["L0_ffn_gate_b"].rearrange("(o n) -> o n", o=1))
            load(brow[rows["f1_gb"]:rows["f1_gb"] + 1, 0:E1], I["L1_ffn_gate_b"].rearrange("(o n) -> o n", o=1))
            for b in range(B):
                load(H[IMG % P:IMG % P + TXT, b * TPB + TPB - 1, :], I["txt"][b])
            e.wait_ge(w_loaded, 16 * LOADS[0])

        def weights_gpsimd(e):
            e.iota(node[:, :], pattern=[[1, BANK]], base=0, channel_multiplier=0,
                   allow_small_or_imprecise_dtypes=True).then_inc(ident_set, 1)
            e.memset(brow[:, :], 0.0).then_inc(w_zeroed, 1)
            e.memset(tok_w1[:, :, :], 0.0).then_inc(w_zeroed, 1)
            e.memset(tok_w3[:, :, :], 0.0).then_inc(w_zeroed, 1)
            e.memset(WF[:, :], 0.0).then_inc(w_zeroed, 1)
            e.memset(H[:, :, :], 0.0).then_inc(w_zeroed, 1)
            e.memset(ident[:, :], 0.0).then_inc(ident_set, 1)
            e.wait_ge(ident_set, 2)
            e.affine_select(out=ident[:, :], in_=ident[:, :], compare_op=ALU.not_equal, fill=1.0, base=0,
                            pattern=[[-1, P]], channel_multiplier=1).then_inc(ident_set, 1)
            e.wait_ge(ident_set, 3)
            e.tensor_copy(ident_bf[:, :], ident[:, :]).then_inc(ident_set, 1)
            for s in started():
                e.sem_inc(s, START)
            e.memset(sel_f[:, :, :], 0.0).then_inc(sel_set, 1)
            for k in range(2):
                e.wait_ge(sel_set, k + 1)
                e.affine_select(out=sel_f[:, :, :], in_=sel_f[:, :, :], compare_op=ALU.not_equal, fill=1.0,
                                base=-32 * k, pattern=[[-1, max(E0, E1)], [0, D]],
                                channel_multiplier=1).then_inc(sel_set, 1)
            e.memset(head_rows[:, :], 0.0).then_inc(heads_set, 1)
            for k, r in enumerate(range(2 * DH)):
                e.wait_ge(heads_set, k + 1)
                e.affine_select(out=head_rows[:, :], in_=head_rows[:, :], compare_op=ALU.not_equal, fill=1.0,
                                base=-(r // DH) * D - r % DH, pattern=[[-DH, HEADS]],
                                channel_multiplier=1).then_inc(heads_set, 1)
            for t in range(TPC):
                e.wait_ge(mask_thresholded, t + 1)
                e.affine_select(out=mask0[:, t, :], in_=mask0[:, t, :], compare_op=ALU.not_equal, fill=0.0,
                                base=t * P, pattern=[[-1, BANK]], channel_multiplier=1).then_inc(ident_set, 1)

        def weights_scalar(e):
            e.wait_ge(w_sorted, 1)
            e.activation(WS[:, :], WF[:, :], ACT.Copy).then_inc(w_rounded, 1)
            e.wait_ge(sel_set, 3)
            e.activation(SEL[:, :, :], sel_f[:, :, :], ACT.Copy).then_inc(w_rounded, 1)
            e.wait_ge(tables_turned, 1)
            e.activation(bias[:, :], bank[4][:, 0:NBIAS], ACT.Copy).then_inc(tables_copied, 1)

        def weights_vector(e):
            for t in range(TPC):
                e.memset(bank[t][:, :], 0.0).then_inc(counts_zeroed, 1)
            e.wait_ge(edges_loaded, 16)
            ids = Chain(e, edges_cast)
            ids.link(e.tensor_copy(edges_f[:, :, :], edges[:, :, :]))
            ids.link(e.tensor_scalar(negative[:, :, :], edges_f[:, :, :], 0.0, float(N), ALU.is_lt, ALU.mult))
            ids.link(e.tensor_tensor(edges_f[:, :, :], edges_f[:, :, :], negative[:, :, :], ALU.add))
            ids.link(e.tensor_reduce(e_max[:, :], edges_f[:, :, :].rearrange("p a j -> p (a j)"), X, ALU.max))
            e.wait_ge(ident_set, 1)
            with e.Fori(0, E_PER // HOTS) as i:
                for u in range(HOTS):
                    e.wait_ge(hot_used, i * HOTS + (u + 1))
                    for a in range(2):
                        e.tensor_scalar(hot[:, u, a, :], node[:, :],
                                        edges_f[:, a, bass.ds(i * HOTS + u, 1)], None,
                                        ALU.is_equal).then_inc(hot_ready, 1)
            for t in range(TPC):
                e.wait_ge(hot_used, HOTS + E_PER)
                e.tensor_scalar(mask0[:, t, :], bank[t][:, :], 0.5, MASKED, ALU.is_lt,
                                ALU.mult).then_inc(mask_thresholded, 1)
            e.wait_ge(w_loaded, 16 * LOADS[0])
            for i, name in enumerate(("a1_q", "a1_k", "a1_v")):
                e.wait_ge(tables_turned, 2)
                for m in (0, D):
                    c = cols[name] + m
                    e.tensor_copy(WF[:, c:c + D], bank[5][:, i * D:(i + 1) * D]).then_inc(edges_cast, 1)
            for g, pair in enumerate(PAIRS):
                for h, tap in enumerate(pair):
                    if tap is not None:
                        c = cols["tok_w2"] + g * P + h * D
                        e.tensor_copy(WF[:, c:c + D], tok_w2_raw[:, :].rearrange("p (c t) -> p t c", t=TAPS)[:, tap, :]
                                      ).then_inc(edges_cast, 1)
            e.wait_ge(edges_cast, 4 + 6 + TAPS)
            e.sem_inc(w_sorted, 1)
            e.wait_ge(w_rounded, 1)
            e.tensor_tensor(WS[D:P, :], WF[D:P, :], WS[D:P, :].bitcast(F32), ALU.subtract).then_inc(w_rounded, 1)
            top = Chain(e, edges_cast, 4 + 6 + TAPS)
            e.wait_ge(tables_turned, 3)
            top.link(e.tensor_reduce(e_top[:, 0:1], bank[6][0:1, 0:P], X, ALU.max))
            top.link(e.tensor_scalar(e_top[:, 1:2], e_top[:, 0:1], float(BANK), None, ALU.is_ge))
            top.link(e.tensor_copy(any_far[:, :], e_top[:, 1:2]))

        def weights_tensor(e):
            e.sem_inc(hot_used, HOTS)
            e.wait_ge(counts_zeroed, TPC)
            with e.Fori(0, E_PER // HOTS) as i:
                for u in range(HOTS):
                    e.wait_ge(hot_ready, i * (2 * HOTS) + 2 * (u + 1))
                    for t in range(TPC):
                        mm = e.matmul(bank[t][:, :], hot[:, u, 0, t * P:(t + 1) * P], hot[:, u, 1, :],
                                      start=False, stop=False, skip_group_check=True)
                    mm.then_inc(hot_used, 1)
            e.wait_ge(ident_set, 3)
            e.wait_ge(w_loaded, 16 * LOADS[0])
            e.transpose(bank[4][:, 0:P], brow[:, :], ident[:, :]).then_inc(tables_turned, 1)
            for i in range(3):
                last = e.transpose(bank[5][:, i * D:(i + 1) * D], wt[:, i, :], ident[0:D, 0:D])
            last.then_inc(tables_turned, 1)
            e.wait_ge(edges_cast, 4)
            e.transpose(bank[6][0:1, 0:P], e_max[:, :], ident[:, :]).then_inc(tables_turned, 1)

        ctx_w.close()

        ctx_t = ExitStack()
        PIX = PW * PW
        img = [[sb(f"img_{n}{b}", [P, PIX + PW], F32, ctx_t) for b in range(2)] for n in ("col", "row")]
        tokT = [sb(f"tokT{b}", [P, NPAD], F32, ctx_t) for b in range(2)]
        h1 = [sb(f"h1_{b}", [P, CT], F32, ctx_t) for b in range(2)]
        h1_hi = [sb(f"h1_hi{b}", [P, CT], F32R, ctx_t) for b in range(2)]
        h1_lo = [sb(f"h1_lo{b}", [P, CT], F32R, ctx_t) for b in range(2)]
        NG = 3
        gate = [sb(f"gate{b}", [P, CT], F32, ctx_t) for b in range(NG)]
        gated = [sb(f"gated{b}", [P, G5, CT], F32, ctx_t) for b in range(2)]
        GROUP = [(0, off(0)), (0, off(3)), (0, off(6)), (1, off(2)), (0, off(8))]
        UB = 2
        UC = UB * CPB
        TURNS = B // UB
        TGROUPS = -(-TPB // TPC)
        img_zeroed = sem("img_zeroed")
        img_loaded = [sem(f"img_loaded{b}") for b in range(UB)]
        img_copied = [sem(f"img_copied{b}") for b in range(UB)]
        t_h = sem("t_h")
        t_relu = sem("t_relu")
        t_split = sem("t_split")
        t_halves = sem("t_halves")
        t_logit = sem("t_logit")
        t_gate = sem("t_gate")
        t_gated = sem("t_gated")
        t_out = sem("t_out")
        t_stored = sem("t_stored")
        t_turned = sem("t_turned")
        t_inH = sem("t_inH")

        def tok_sync(e):
            e.wait_ge(img_zeroed, 2 * UB)
            for b in range(B):
                u = b % UB
                col, row = img[0][u], img[1][u]
                if b >= UB:
                    e.wait_ge(t_gated, (b - UB + 1) * CPB * G5 + START)
                e.dma_start(col[0:D, 0:PIX].rearrange("c (h w) -> c h w", w=PW)[:, 1:IH + 1, 1:IW + 1],
                            I["x"][b]).then_inc(img_loaded[u], 16)
                e.wait_ge(img_loaded[u], (b // UB + 1) * 16)
                e.dma_start(col[D:P, 0:PIX - 1], col[0:D, 1:PIX]).then_inc(img_copied[u], 16)
                e.dma_start(row[0:D, 0:PIX], col[0:D, 0:PIX]).then_inc(img_copied[u], 16)
                e.dma_start(row[D:P, 0:PIX - PW], col[0:D, PW:PIX]).then_inc(img_copied[u], 16)

        def taps(g, u, j, lo=0, hi=ROWS):
            which, o = GROUP[g]
            o += (j * ROWS + lo) * PW
            n = hi - lo
            return img[which][u][:, o:o + n * PW].rearrange("p (h w) -> p h w", w=PW)[:, :, 0:IW]

        def tok_gpsimd(e):
            for which in range(2):
                for u in range(UB):
                    e.memset(img[which][u][:, :], 0.0).then_inc(img_zeroed, 1)
            for u in range(UB):
                e.memset(tokT[u][:, :], 0.0).then_inc(img_zeroed, 1)

        def tok_tensor(e):
            with e.Fori(0, TURNS) as i:
                def at(n, per=1):
                    return i * (UC * per) + n

                def first_product(c):
                    u, j = divmod(c, CPB)
                    if j == 0:
                        e.wait_ge(img_copied[u], i * 48 + 48)
                    e.wait_ge(t_relu, at(c + 1))
                    for g in range(G5):
                        for h in range(2):
                            mm = e.matmul(bank[c % 2][h * D:(h + 1) * D, 0:HALF], tok_w1[:, g, :],
                                          taps(g, u, j, h * ROWS // 2, (h + 1) * ROWS // 2),
                                          start=(g == 0), stop=(g == G5 - 1))
                    mm.then_inc(t_h, 1)

                def gate_logits(c):
                    if c == 0:
                        e.wait_ge(t_inH, i * (UB * TGROUPS) + 2)
                    e.wait_ge(t_split, at(c + 1) + START)
                    for g in range(G5):
                        k = c * G5 + g
                        b = bank[2 + k % 4]
                        e.wait_ge(t_gate, i * (UC * G5) + (k + 1))
                        e.matmul(b[:, 0:CT], W("tok_w2", g), h1_hi[c % 2][:, :], start=True, stop=False)
                        e.matmul(b[:, 0:CT], W("tok_w2", g), h1_lo[c % 2][:, :], start=False, stop=True).then_inc(t_logit, 1)

                def last_product(c):
                    e.wait_ge(t_gated, i * (UC * G5) + (c + 1) * G5 + START)
                    e.wait_ge(t_stored, at(c + 1))
                    for g in range(G5):
                        for h in range(2):
                            mm = e.matmul(bank[6 + c % 2][h * D:(h + 1) * D, 0:HALF], tok_w3[:, g, :],
                                          gated[c % 2][:, g, h * HALF:(h + 1) * HALF],
                                          start=(g == 0), stop=(g == G5 - 1))
                    mm.then_inc(t_out, 1)

                first_product(0)
                for c in range(UC):
                    if c + 1 < UC:
                        first_product(c + 1)
                    gate_logits(c)
                    if c >= 1:
                        last_product(c - 1)
                last_product(UC - 1)
                for u in range(UB):
                    for k in range(0, TPB, TPC):
                        r = u * TGROUPS + k // TPC
                        if r == 0:
                            e.wait_ge(t_stored, at(UC + 2))
                            e.wait_ge(t_gate, i * (UC * G5) + (UC * G5 + 4))
                        e.wait_ge(t_inH, i * (UB * TGROUPS) + (r + 1))
                        for t in range(k, min(k + TPC, TPB)):
                            mm = e.transpose(bank[2 + r % 2][:, (t - k) * P:(t - k + 1) * P],
                                             tokT[u][:, t * P:(t + 1) * P], ident[:, :])
                        mm.then_inc(t_turned, 1)

        def tok_scalar(e):
            e.sem_inc(t_relu, 2)
            e.sem_inc(t_gate, 4)
            with e.Fori(0, TURNS) as i:
                for c in range(UC + 1):
                    if c < UC:
                        e.wait_ge(t_h, i * UC + (c + 1))
                        e.wait_ge(t_split, i * UC + max(c - 1, 0) + START)
                        for h in range(2):
                            for m in range(2):
                                a = e.activation(h1[c % 2][m * D:(m + 1) * D, h * HALF:(h + 1) * HALF],
                                                 bank[c % 2][h * D:(h + 1) * D, 0:HALF], ACT.Relu,
                                                 bias=bcol("tok_b1", 0, h * D, (h + 1) * D))
                        a.then_inc(t_relu, 1)
                    if c >= 1:
                        for g in range(G5):
                            k = (c - 1) * G5 + g
                            e.wait_ge(t_logit, i * (UC * G5) + (k + 1 + START))
                            e.wait_ge(t_gated, i * (UC * G5) + max(k + 1 - NG, 0) + START)
                            e.activation(gate[k % NG][:, :], bank[2 + k % 4][:, 0:CT], ACT.Sigmoid,
                                         bias=bcol("tok_b2", g)).then_inc(t_gate, 1)

        def tok_vector(e):
            e.sem_inc(t_stored, 2)
            e.sem_inc(t_inH, 2)
            e.wait_ge(img_zeroed, 3 * UB)
            with e.Fori(0, TURNS) as i:
                def split(c):
                    e.wait_ge(t_relu, i * UC + (c + 3))
                    e.wait_ge(t_logit, i * (UC * G5) + max(c - 1, 0) * G5 + START)
                    hi = h1_hi[c % 2]
                    e.tensor_copy(hi[:, :], h1[c % 2][:, :]).then_inc(t_halves, 1)
                    e.wait_ge(t_halves, i * UC + (c + 1))
                    e.tensor_tensor(h1_lo[c % 2][:, :], h1[c % 2][:, :], hi[:, :].bitcast(F32),
                                    ALU.subtract).then_inc(t_split, 1)

                def store(c):
                    u, j = divmod(c, CPB)
                    e.wait_ge(t_out, i * UC + (c + 1 + START))
                    if j == 0:
                        e.wait_ge(t_turned, i * (UB * TGROUPS) + START)
                    for h in range(2):
                        o = j * CT + h * HALF
                        a = e.tensor_scalar(tokT[u][0:D, o:o + HALF], bank[6 + c % 2][h * D:(h + 1) * D, 0:HALF],
                                            bcol("tok_b3", 0, h * D, (h + 1) * D), None, ALU.add)
                    a.then_inc(t_stored, 1)

                split(0)
                for c in range(UC):
                    u, j = divmod(c, CPB)
                    if c + 1 < UC:
                        split(c + 1)
                    e.wait_ge(t_out, i * UC + max(c - 1, 0) + START)
                    for g in range(G5):
                        e.wait_ge(t_gate, i * (UC * G5) + (c * G5 + g + 1 + 4))
                        e.tensor_tensor(gated[c % 2][:, g, :].rearrange("p (h w) -> p h w", w=IW),
                                        gate[(c * G5 + g) % NG][:, :].rearrange("p (h w) -> p h w", w=IW),
                                        taps(g, u, j), ALU.mult).then_inc(t_gated, 1)
                    if c >= 1:
                        store(c - 1)
                store(UC - 1)
                for u in range(UB):
                    for k in range(0, TPB, TPC):
                        r = u * TGROUPS + k // TPC
                        e.wait_ge(t_turned, i * (UB * TGROUPS) + (r + 1 + START))
                        whole = k + TPC < TPB
                        n, hi = (TPC, P) if whole else (1, IMG % P)
                        e.tensor_copy(H[0:hi, bass.ds(i * (UB * TPB) + (u * TPB + k), n), :],
                                      bank[2 + r % 2][0:hi, :].rearrange("p (t c) -> p t c", c=P)[:, 0:n, 0:D]
                                      ).then_inc(t_inH, 1)

        ctx_t.close()
        assert TPB % TPC == 1

        Y = sb("Y", [P, T, D])
        stat = sb("stat", [P, 4, T])
        NORMS = 4
        LN_LINKS = B + 1 + B + 1

        def rows_of(t, b):
            return t[:, b * TPB:(b + 1) * TPB, :]

        def over_d(t2, b):
            return t2[:, b * TPB:(b + 1) * TPB].unsqueeze(2).broadcast_to([P, TPB, D])

        def over_t(v):
            return v.unsqueeze(1).broadcast_to([P, TPB, D])

        def norm_vector(e, k, src, affine=None):
            ch = Chain(e, ln_dve, k * LN_LINKS)
            for b in range(B):
                ch.mark(e.tensor_reduce(stat[:, 0, b * TPB:(b + 1) * TPB], rows_of(src, b), X, ALU.add))
            ch.wait()
            ch.link(e.tensor_scalar(stat[:, 1, :], stat[:, 0, :], 1.0 / D, None, ALU.mult))
            for b in range(B):
                e.tensor_tensor(rows_of(Y, b), rows_of(src, b), over_d(stat[:, 1, :], b),
                                ALU.subtract).then_inc(ln_centred, 1)
            for b in range(B):
                e.wait_ge(ln_squared, k * B + b + 1)
                ch.mark(e.tensor_reduce(stat[:, 2, b * TPB:(b + 1) * TPB], squares[k][b % 2][:, :, :], X, ALU.add))
            ch.wait()
            e.tensor_scalar(stat[:, 3, :], stat[:, 2, :], 1.0 / D, LN_EPS, ALU.mult, ALU.add).then_inc(ln_var, 1)
            e.wait_ge(ln_std, k + 1)
            ch.link(e.reciprocal(stat[:, 3, :], stat[:, 3, :]))
            for b in range(B):
                e.tensor_tensor(rows_of(Y, b), rows_of(Y, b), over_d(stat[:, 3, :], b), ALU.mult).then_inc(ln_scaled, 1)
            if affine is not None:
                for b in range(B):
                    e.wait_ge(ln_scaled, k * B + b + 1)
                    e.tensor_tensor(rows_of(Y, b), rows_of(Y, b), over_t(gb[:, affine, :]), ALU.mult).then_inc(ln_gamma, 1)
                for b in range(B):
                    e.wait_ge(ln_gamma, (affine // 2) * B + b + 1)
                    e.wait_ge(ln_beta, (affine // 2) * B + b + 1)
                    e.tensor_tensor(rows_of(H, b), rows_of(H, b), rows_of(Y, b), ALU.add).then_inc(ln_gamma_in, 1)

        def norm_scalar(e, k):
            for b in range(B):
                e.wait_ge(ln_centred, k * B + b + 1)
                if b >= 2:
                    e.wait_ge(ln_dve, k * LN_LINKS + B + 1 + b - 1)
                e.activation(squares[k][b % 2][:, :, :], rows_of(Y, b), ACT.Square).then_inc(ln_squared, 1)
            e.wait_ge(ln_var, k + 1)
            e.activation(stat[:, 3, :], stat[:, 3, :], ACT.Sqrt).then_inc(ln_std, 1)

        def norm_gpsimd(e, affine):
            for b in range(B):
                e.tensor_tensor(rows_of(H, b), rows_of(H, b), over_t(gb[:, affine + 1, :]), ALU.add).then_inc(ln_beta, 1)

        ln_scaled = sem("ln_scaled")
        ln_gamma = sem("ln_gamma")
        ln_gamma_in = sem("ln_gamma_in")
        ln_beta = sem("ln_beta")
        squares = []
        ctx_n = ExitStack()
        squares_now = [sb(f"squares{j}", [P, TPB, D], F32, ctx_n) for j in range(2)]
        for k in range(NORMS):
            squares.append(squares_now)
        ctx_n.close()

        DUPS = 2

        CHUNKS_TURNED = [START]
        t_sems = {n: sem("x_" + n) for n in ("doubled", "turned", "high", "low")}

        def turner(name, stack, banks, chunks):
            CHUNKS_TURNED[0] += chunks
            return {"dup": [sb(f"{name}_dup{j}", [P, TPC, 2, D], F32, stack) for j in range(DUPS)],
                    "banks": banks, "before": CHUNKS_TURNED[0] - chunks, **t_sems}

        def turned_by(tr, done, n):
            return done + (tr["before"] + n)

        def double_chunk(e, tr, done, k, tokens, n):
            e.wait_ge(tr["turned"], turned_by(tr, done, max(k + 1 - DUPS, 0)))
            e.activation(tr["dup"][k % DUPS][:, 0:n, :, :], tokens.unsqueeze(2).broadcast_to([P, n, 2, D]),
                         ACT.Copy).then_inc(tr["doubled"], 1)

        def turn_chunk(e, tr, done, k, n):
            nb = len(tr["banks"])
            e.wait_ge(tr["low"], turned_by(tr, done, max(k + 1 - nb, 0)))
            e.wait_ge(tr["doubled"], turned_by(tr, done, k + 1))
            for t in range(n):
                mm = e.transpose(tr["banks"][k % nb][:, t * P:(t + 1) * P],
                                 tr["dup"][k % DUPS][:, t, :, :].rearrange("p a d -> p (a d)"), ident[:, :])
            mm.then_inc(tr["turned"], 1)

        def high_chunk(e, tr, done, k, n, hi):
            e.wait_ge(tr["turned"], turned_by(tr, done, k + 1))
            e.activation(hi, tr["banks"][k % len(tr["banks"])][:, 0:n * P], ACT.Copy).then_inc(tr["high"], 1)

        def low_chunk(e, tr, done, k, n, hi, lo):
            e.wait_ge(tr["high"], turned_by(tr, done, k + 1))
            e.tensor_tensor(lo, tr["banks"][k % len(tr["banks"])][:, 0:n * P], hi.bitcast(F32),
                            ALU.subtract).then_inc(tr["low"], 1)

        def product(e, out, weights, hi, lo, start=True, stop=True):
            e.matmul(out, weights, hi, start=start, stop=False)
            return e.matmul(out, weights, lo, start=False, stop=stop)

        g_names = ("logit lt_biased lt_turned stored place_set dve act exp ext_zeroed ext_ready w_turned w_ready h_ready "
                   "wb_ready wb_copied act_done weighted used summed y_turned y_added y_half x_doubled x_turned x_high x_low "
                   "n0_dve n1_dve n0_var n1_var n0_std n1_std n_beta")
        G = {n: sem("ffn_" + n) for n in g_names.split()}
        GATE_LINKS = 19

        def ffn(name, E, w2, kind, into, k, C0, N0, P0, L0, norms):
            st = ExitStack()
            TURN = 5
            TURNS_A = NCH // TURN
            XH = [sb(f"{name}_XH{j}", [P, BANK], F32R, st) for j in range(2)]
            XL = [sb(f"{name}_XL{j}", [P, BANK], F32R, st) for j in range(2)]
            x_dup = sb(f"{name}_xdup", [P, TPC, 2, D], F32, st)
            LG = sb(f"{name}_LG", [P, T, E], F32, st)
            WH = sb(f"{name}_WH", [P, T, E], F32R, st)
            keep = ExitStack()
            tr = turner(name, keep, [bank[0], bank[1], bank[2]], NCH)
            LT = [sb(f"{name}_LT{j}", [P, BANK], F32, keep) for j in range(2)]
            g_logit, g_biased, g_turned, g_stored = G["logit"], G["lt_biased"], G["lt_turned"], G["stored"]
            keep.close()
            keep = ExitStack()
            place = sb(f"{name}_place", [P, E], F32, keep)
            oh1 = sb(f"{name}_oh1", [P, T, E], F32, keep)
            oh2 = sb(f"{name}_oh2", [P, T, E], F32, keep)
            oh3 = sb(f"{name}_oh3", [P, T, E], F32, keep)
            red = sb(f"{name}_red", [P, 6, T], F32, keep)
            place_set, g_dve, g_act, g_exp = G["place_set"], G["dve"], G["act"], G["exp"]
            keep.close()
            RING = 4
            TR = 3
            PAIRS_E = E // 2
            ext = [sb(f"{name}_ext{j}", [P, TPC, P], F32, st) for j in range(2)]
            GS = [sb(f"{name}_GS{j}", [P, BANK], F32R, st) for j in range(2)]
            hid = [sb(f"{name}_hid{j}", [P, BANK], F32, st) for j in range(RING)]
            term = [sb(f"{name}_term{j}", [P, BANK], F32, st) for j in range(TR)]
            wb = [sb(f"{name}_wb{j}", [P, BANK], F32, st) for j in range(2)]
            total = [sb(f"{name}_total{j}", [P, BANK], F32, st) for j in range(2)]
            cs = [sb(f"{name}_cs{j}", [P, 4, TPC], F32, st) for j in range(2)]
            csq = sb(f"{name}_csq", [P, TPC, D], F32, st)
            copier_is_vector = kind == "gelu"
            (ext_zeroed, ext_ready, w_turned, w_ready, h_ready, wb_ready, wb_copied, act_done, weighted, used, summed,
             y_turned, y_added, y_half, x_doubled, x_turned, x_high, x_low) = (G[x] for x in (
                 "ext_zeroed ext_ready w_turned w_ready h_ready wb_ready wb_copied act_done weighted used summed y_turned "
                 "y_added y_half x_doubled x_turned x_high x_low").split())
            st.close()
            func = ACT.Relu if kind == "relu" else ACT.Gelu

            def tiles(t, c, n=TPC):
                return t[:, bass.ds(c * TPC, n), :] if not isinstance(c, int) else t[:, c * TPC:c * TPC + n, :]

            def a_tensor(e):
                with e.Fori(0, TURNS_A) as i:
                    for u in range(TURN + 2):
                        if u < TURN:
                            turn_chunk(e, tr, i * TURN, u, TPC)
                        if 1 <= u <= TURN:
                            v = u - 1
                            e.wait_ge(g_biased, i * TURN + (C0 + max(v - 1, 0) + START))
                            e.wait_ge(tr["low"], turned_by(tr, i * TURN, v + 1))
                            product(e, bank[3 + v % 2][:, :], W(name + "_g"), XH[v % 2][:, :], XL[v % 2][:, :]).then_inc(g_logit, 1)
                        if u >= 2:
                            v = u - 2
                            e.wait_ge(g_stored, i * TURN + (C0 + max(v - 1, 0) + START))
                            e.wait_ge(g_biased, i * TURN + (C0 + v + 1 + START))
                            for t in range(TPC):
                                mm = e.transpose(bank[5 + v % 2][:, t * P:(t + 1) * P],
                                                 LT[v % 2][:, t * P:(t + 1) * P], ident[:, :])
                            mm.then_inc(g_turned, 1)

            def a_scalar(e):
                with e.Fori(0, TURNS_A) as i:
                    for u in range(TURN + 2):
                        if u < TURN:
                            double_chunk(e, tr, i * TURN, u, tiles(Y, i * TURN + u), TPC)
                            e.wait_ge(g_logit, i * TURN + (C0 + max(u - 1, 0) + START))
                            high_chunk(e, tr, i * TURN, u, TPC, XH[u % 2][:, :])
                        if 1 <= u <= TURN:
                            v = u - 1
                            e.wait_ge(g_turned, i * TURN + (C0 + max(v - 1, 0) + START))
                            e.wait_ge(g_logit, i * TURN + (C0 + v + 1 + START))
                            e.activation(LT[v % 2][:, :], bank[3 + v % 2][:, :], ACT.Identity,
                                         bias=bcol(name + "_gb")).then_inc(g_biased, 1)

            def a_vector(e):
                with e.Fori(0, TURNS_A) as i:
                    for u in range(TURN + 2):
                        if u < TURN:
                            low_chunk(e, tr, i * TURN, u, TPC, XH[u % 2][:, :], XL[u % 2][:, :])
                        if u >= 2:
                            v = u - 2
                            e.wait_ge(g_turned, i * TURN + (C0 + v + 1 + START))
                            e.tensor_copy(tiles(LG, i * TURN + v),
                                          bank[5 + v % 2][:, :].rearrange("p (t c) -> p t c", c=P)[:, :, 0:E]
                                          ).then_inc(g_stored, 1)

            def over_e(v):
                return v.unsqueeze(2).broadcast_to([P, T, E])

            def b_gpsimd(e):
                e.iota(place[:, :], pattern=[[1, E]], base=-99, channel_multiplier=0,
                       allow_small_or_imprecise_dtypes=True).then_inc(place_set, 1)

            def b_vector(e):
                ch = Chain(e, g_dve, L0)
                L, top, pos, ex = LG[:, :, :], red[:, 0, :], red[:, 1, :], red[:, 2, :]
                places = place[:, :].unsqueeze(1).broadcast_to([P, T, E])
                e.wait_ge(place_set, k + 1)
                if kind == "gelu":
                    ch.link(e.tensor_reduce(top, L, X, ALU.max))
                    e.tensor_tensor(L, L, over_e(top), ALU.subtract).then_inc(g_exp, 1)
                    e.wait_ge(g_act, k + 1)
                    ch.link(e.tensor_reduce(top, L, X, ALU.add))
                    ch.link(e.reciprocal(top, top))
                    ch.link(e.tensor_tensor(L, L, over_e(top), ALU.mult))

                def best(oh, values, top):
                    ch.link(e.tensor_reduce(top, values, X, ALU.max))
                    ch.link(e.tensor_tensor(oh, values, over_e(top), ALU.is_equal))
                    ch.link(e.tensor_tensor(oh, oh, places, ALU.mult))
                    ch.link(e.tensor_reduce(pos, oh, X, ALU.min))
                    ch.link(e.tensor_tensor(oh, places, over_e(pos), ALU.is_equal))

                first, second, rest = oh1[:, :, :], oh2[:, :, :], oh3[:, :, :]
                best(first, L, top)
                ch.link(e.scalar_tensor_tensor(out=rest, in0=first, scalar=MASKED, in1=L, op0=ALU.mult, op1=ALU.add))
                best(second, rest, red[:, 3, :])
                if kind == "gelu":
                    ch.link(e.tensor_tensor(first, first, second, ALU.add))
                    ch.link(e.tensor_tensor(L, L, first, ALU.mult))
                else:
                    e.tensor_tensor(ex, red[:, 3, :], top, ALU.subtract).then_inc(g_exp, 1)
                    e.wait_ge(g_act, k + 1)
                    ch.link(e.tensor_scalar(red[:, 4, :], ex, 1.0, None, ALU.add))
                    ch.link(e.reciprocal(red[:, 4, :], red[:, 4, :]))
                    ch.link(e.tensor_tensor(red[:, 5, :], ex, red[:, 4, :], ALU.mult))
                    ch.link(e.tensor_tensor(first, first, over_e(red[:, 4, :]), ALU.mult))
                    ch.link(e.tensor_tensor(second, second, over_e(red[:, 5, :]), ALU.mult))
                    ch.link(e.tensor_tensor(L, first, second, ALU.add))
                ch.link(e.tensor_copy(WH[:, :, :], L))
                ch.link(e.tensor_tensor(L, L, WH[:, :, :].bitcast(F32), ALU.subtract))
                assert ch.close() == GATE_LINKS, ch.n

            def b_scalar(e):
                e.wait_ge(g_exp, k + 1)
                v = LG[:, :, :] if kind == "gelu" else red[:, 2, :]
                e.activation(v, v, ACT.Exp).then_inc(g_act, 1)

            def loop_chunks(e, body):
                body(0, 0, 0, False)
                body(1, 1, 1, False)
                with e.Fori(0, (NCH - 3) // 2) as i:
                    body(i * 2 + 2, 0, 2, False)
                    body(i * 2 + 3, 1, 2, False)
                body(NCH - 1, 0, 2, True)

            ADDS = PAIRS_E - 1

            def c_gpsimd(e):
                for j in range(2):
                    e.memset(ext[j][:, :, :], 0.0).then_inc(ext_zeroed, 1)
                e.wait_ge(ext_zeroed, 2 * k + 2)

                def widen(c, par, fresh):
                    if not fresh:
                        e.wait_ge(w_turned, c + (C0 - 1))
                    v = ext[par][:, :, :].rearrange("p t (g x) -> p g t x", g=4)
                    for g in range(4):
                        src = (WH[:, :, :].bitcast(F32), LG[:, :, :])[g % 2]
                        a = e.tensor_copy(v[:, g, :, 0:E], tiles(src, c))
                    a.then_inc(ext_ready, 1)

                def beta(c):
                    h = tiles(H, c)
                    e.tensor_tensor(h, h, gb[:, 3, :].unsqueeze(1).broadcast_to([P, TPC, D]), ALU.add).then_inc(G["n_beta"], 1)

                widen(0, 0, True)

                def body(c, par, past, last):
                    if not last:
                        widen(c + 1, 1 - par, not past)
                    for p in range(1, PAIRS_E):
                        e.wait_ge(weighted, c * PAIRS_E + (P0 + p + 1))
                        e.wait_ge(summed, c * ADDS + (P0 - C0 + p - 1))
                        e.tensor_tensor(total[par][:, :], total[par][:, :], term[p % TR][:, :], ALU.add).then_inc(summed, 1)
                        if p == 2 and norms:
                            beta(c)
                loop_chunks(e, body)

            def c_tensor(e):
                def turn_tokens(c):
                    e.wait_ge(w_ready, c + C0)
                    e.wait_ge(x_doubled, c + (C0 + 1))
                    for t in range(TPC):
                        mm = e.transpose(bank[6][:, t * P:(t + 1) * P],
                                         x_dup[:, t, :, :].rearrange("p a d -> p (a d)"), ident[:, :])
                    mm.then_inc(x_turned, 1)

                def turn_weights(c, par):
                    e.wait_ge(x_low, c + (C0 + 1))
                    e.wait_ge(ext_ready, c + (C0 + 1))
                    for t in range(TPC):
                        mm = e.transpose(bank[6][:, t * P:(t + 1) * P], ext[par][:, t, :], ident[:, :])
                    mm.then_inc(w_turned, 1)

                def hidden(c, par, x):
                    n, r = c * E + x, x % 2
                    if not (isinstance(n, int) and n < 2):
                        e.wait_ge(act_done, n + (N0 - 1))
                    product(e, bank[r][:, :], W(name + "_w1", x), XH[par][:, :], XL[par][:, :]).then_inc(h_ready, 1)

                def spread(c, par, p):
                    m = c * PAIRS_E + p
                    if p == 0:
                        e.wait_ge(w_ready, c + (C0 + 1))
                    if not (isinstance(m, int) and m < 2):
                        e.wait_ge(wb_copied, m + (P0 - 1))
                    e.matmul(bank[2 + p % 2][:, :], SEL[:, 2 * p:2 * p + 2, :].rearrange("k a m -> k (a m)"), GS[par][:, :],
                             start=True, stop=True).then_inc(wb_ready, 1)

                def output(c, x):
                    m = c * PAIRS_E + x // 2
                    if x % 2 == 0 and not (isinstance(m, int) and m < 2):
                        e.wait_ge(weighted, m + (P0 - 1))
                    e.wait_ge(act_done, c * E + (N0 + x + 1))
                    y = bank[4 + (x // 2) % 2]
                    e.matmul(y[(x % 2) * D:(x % 2 + 1) * D, :], w2[:, x, :], hid[x % RING][:, :],
                             start=True, stop=True, skip_group_check=True).then_inc(used, 1)

                def turn_out(c, par):
                    e.wait_ge(y_added, c + C0)
                    e.wait_ge(summed, c * ADDS + (P0 - C0 + ADDS))
                    for t in range(TPC):
                        mm = e.transpose(bank[7][:, t * P:(t + 1) * P], total[par][:, t * P:(t + 1) * P], ident[:, :])
                    mm.then_inc(y_turned, 1)

                turn_tokens(0)
                turn_weights(0, 0)
                hidden(0, 0, 0)
                hidden(0, 0, 1)
                spread(0, 0, 0)

                def body(c, par, past, last):
                    for x in range(E):
                        if x == min(4, E // 2 - 1) and past:
                            turn_out(c - 1, 1 - par)
                        if x == E - 7 and not last:
                            turn_tokens(c + 1)
                        if x == E - 3 and not last:
                            turn_weights(c + 1, 1 - par)
                        if x % 2 == 1 and x + 1 < E:
                            spread(c, par, x // 2 + 1)
                        elif x % 2 == 1 and not last:
                            spread(c + 1, 1 - par, 0)
                        if x + 2 < E:
                            hidden(c, par, x + 2)
                        elif not last:
                            hidden(c + 1, 1 - par, x + 2 - E)
                        output(c, x)
                loop_chunks(e, body)
                turn_out(NCH - 1, (NCH - 1) % 2)

            def copy_spread(e, c, p):
                m = c * PAIRS_E + p
                e.wait_ge(wb_ready, m + (P0 + 1))
                if not isinstance(m, int) or m >= 2:
                    e.wait_ge(weighted, m + (P0 - 1))
                if copier_is_vector:
                    e.tensor_copy(wb[p % 2][:, :], bank[2 + p % 2][:, :]).then_inc(wb_copied, 1)
                else:
                    e.activation(wb[p % 2][:, :], bank[2 + p % 2][:, :], ACT.Copy).then_inc(wb_copied, 1)

            N_LINKS = (9, 7)

            def norm_step(e, c, w, step):
                y, src = tiles(Y, c), tiles((Y, H)[w], c)
                s = cs[w]
                ch = Chain(e, G[f"n{w}_dve"], (0, 2, 3, 5)[step], c, N_LINKS[w])
                if step == 0:
                    ch.link(e.tensor_reduce(s[:, 0, :], src, X, ALU.add))
                    ch.link(e.tensor_scalar(s[:, 1, :], s[:, 0, :], 1.0 / D, None, ALU.mult))
                elif step == 1:
                    ch.link(e.tensor_tensor(y, src, s[:, 1, :].unsqueeze(2).broadcast_to([P, TPC, D]), ALU.subtract))
                elif step == 2:
                    ch.link(e.tensor_tensor(csq[:, :, :], y, y, ALU.mult))
                    ch.link(e.tensor_reduce(s[:, 2, :], csq[:, :, :], X, ALU.add))
                    e.tensor_scalar(s[:, 3, :], s[:, 2, :], 1.0 / D, LN_EPS, ALU.mult, ALU.add).then_inc(G[f"n{w}_var"], 1)
                else:
                    e.wait_ge(G[f"n{w}_std"], c + 1)
                    ch.link(e.reciprocal(s[:, 3, :], s[:, 3, :]))
                    ch.link(e.tensor_tensor(y, y, s[:, 3, :].unsqueeze(2).broadcast_to([P, TPC, D]), ALU.mult))
                    if w == 0:
                        ch.link(e.tensor_tensor(y, y, gb[:, 2, :].unsqueeze(1).broadcast_to([P, TPC, D]), ALU.mult))
                        e.wait_ge(G["n_beta"], c + 1)
                        ch.link(e.tensor_tensor(tiles(H, c), tiles(H, c), y, ALU.add))

            def deviation(e, c, w):
                e.wait_ge(G[f"n{w}_var"], c + 1)
                e.activation(cs[w][:, 3, :], cs[w][:, 3, :], ACT.Sqrt).then_inc(G[f"n{w}_std"], 1)

            def c_scalar(e):
                def weights_in(c, par):
                    e.wait_ge(w_turned, c + (C0 + 1))
                    if not isinstance(c, int) or c >= 2:
                        e.wait_ge(wb_ready, (c - 1) * PAIRS_E + P0)
                    e.activation(GS[par][:, :], bank[6][:, :], ACT.Copy).then_inc(w_ready, 1)

                def double(c):
                    e.wait_ge(x_turned, c + C0)
                    e.activation(x_dup[:, :, :, :], tiles(Y, c).unsqueeze(2).broadcast_to([P, TPC, 2, D]),
                                 ACT.Copy).then_inc(x_doubled, 1)

                def high(c, par):
                    if not isinstance(c, int) or c >= 2:
                        e.wait_ge(h_ready, (c - 1) * E + N0)
                    e.wait_ge(x_turned, c + (C0 + 1))
                    e.activation(XH[par][:, :], bank[6][:, :], ACT.Copy).then_inc(x_high, 1)

                double(0)
                high(0, 0)
                weights_in(0, 0)
                if not copier_is_vector:
                    copy_spread(e, 0, 0)

                def body(c, par, past, last):
                    for x in range(E):
                        n = c * E + x
                        e.wait_ge(h_ready, n + (N0 + 1))
                        if not isinstance(n, int) or n >= RING:
                            e.wait_ge(used, n + (N0 - RING + 1))
                        e.activation(hid[x % RING][:, :], bank[x % 2][:, :], func,
                                     bias=bcol(name + "_b1", x)).then_inc(act_done, 1)
                        if x % 2 == 0 and x >= 2 and not copier_is_vector:
                            copy_spread(e, c, x // 2)
                        if x == 0 and not copier_is_vector and past:
                            copy_spread(e, c, 0)
                        if norms and past == 2 and x == 7:
                            deviation(e, c - 2, 1)
                        if norms and past and x == 13:
                            deviation(e, c - 1, 0)
                        if x == E - 8 and not last:
                            double(c + 1)
                        if x == E - 6 and not last:
                            high(c + 1, 1 - par)
                        if x == E - 2 and not last:
                            weights_in(c + 1, 1 - par)
                loop_chunks(e, body)
                if norms:
                    for c, w in ((NCH - 2, 1), (NCH - 1, 0), (NCH - 1, 1)):
                        deviation(e, c, w)

            def c_vector(e):
                def add_out(c):
                    e.wait_ge(y_turned, c + (C0 + 1))
                    both = bank[7][:, :].rearrange("p (t a d) -> p t a d", a=2, d=D)
                    e.tensor_tensor(tiles(into, c), tiles(into, c), both[:, :, 0, :], ALU.add).then_inc(y_half, 1)
                    e.wait_ge(y_half, c + (C0 + 1))
                    e.tensor_tensor(tiles(into, c), tiles(into, c), both[:, :, 1, :], ALU.add).then_inc(y_added, 1)
                    e.wait_ge(y_added, c + (C0 + 1))

                def low(c, par):
                    e.wait_ge(x_high, c + (C0 + 1))
                    e.tensor_tensor(XL[par][:, :], bank[6][:, :], XH[par][:, :].bitcast(F32),
                                    ALU.subtract).then_inc(x_low, 1)

                low(0, 0)
                if copier_is_vector:
                    copy_spread(e, 0, 0)

                def body(c, par, past, last):
                    for p in range(PAIRS_E):
                        m = c * PAIRS_E + p
                        if p == PAIRS_E - 3 and not last:
                            low(c + 1, 1 - par)
                        e.wait_ge(used, c * E + (N0 + 2 * p + 2))
                        e.wait_ge(wb_copied, m + (P0 + 1))
                        if p == 0:
                            if not isinstance(c, int) or c >= 2:
                                e.wait_ge(y_turned, c + (C0 - 1))
                            dst = total[par]
                        else:
                            dst = term[p % TR]
                            if p >= TR:
                                e.wait_ge(summed, c * ADDS + (P0 - C0 + p - TR))
                            elif past:
                                e.wait_ge(summed, c * ADDS + (P0 - C0))
                        e.scalar_tensor_tensor(out=dst[:, :], in0=bank[4 + p % 2][:, :], scalar=bcol(name + "_b2", p),
                                               in1=wb[p % 2][:, :], op0=ALU.add, op1=ALU.mult).then_inc(weighted, 1)
                        if copier_is_vector and not (last and p == PAIRS_E - 1):
                            copy_spread(e, c, p + 1)
                        if norms and past == 2:
                            for step in SECOND_NORM_AT[p]:
                                norm_step(e, c - 2, 1, step)
                        if p == min(2, PAIRS_E // 2 - 1) and past:
                            add_out(c - 1)
                        if norms and past:
                            for step in FIRST_NORM_AT[p]:
                                norm_step(e, c - 1, 0, step)
                loop_chunks(e, body)
                add_out(NCH - 1)
                if norms:
                    for c, w in ((NCH - 2, 1), (NCH - 1, 0), (NCH - 1, 1)):
                        for step in range(NORM_STEPS):
                            norm_step(e, c, w, step)

            NORM_STEPS = 4
            FIRST_NORM_AT = ((), (), (), (0, 1), (2,), (), (), (3,))
            SECOND_NORM_AT = ((0, 1), (2,), (), (), (), (3,), (), ())

            return {"a": (None, None, a_scalar, a_vector, a_tensor), "b": (None, b_gpsimd, b_scalar, b_vector, None),
                    "c": (None, c_gpsimd, c_scalar, c_vector, c_tensor)}

        SPANS = [(c, min(BANK, NPAD - c)) for c in range(0, NPAD, BANK)]
        NS = len(SPANS)
        LATER = [(c // P, w // P) for c, w in SPANS[1:]]
        NV = len(LATER)
        VB = 2
        VT = VB * NV
        ctx_v = ExitStack()
        v_tr = turner("v0", ctx_v, [bank[0], bank[1]], B * NV)
        vXH = [sb(f"v0_XH{j}", [P, BANK], F32R, ctx_v) for j in range(2)]
        vXL = [sb(f"v0_XL{j}", [P, BANK], F32R, ctx_v) for j in range(2)]
        af = [sb(f"v0_af{j}", [P, BANK], F32, ctx_v) for j in range(2)]
        vVH = [sb(f"v0_VH{j}", [P, BANK], F32R, ctx_v) for j in range(2)]
        vVL = [sb(f"v0_VL{j}", [P, BANK], F32R, ctx_v) for j in range(2)]
        vot = [sb(f"v0_ot{j}", [P, BANK], F32, ctx_v) for j in range(2)]
        ctx_v.close()
        VS = {n: sem("v0_" + n) for n in "v_ready v_biased v_high v_low o_ready o_biased o_turned o_added".split()}

        def later_tokens(i, s):
            t, n = LATER[s % NV]
            return Y[:, bass.ds(i * (VB * TPB) + (s // NV * TPB + t), n), :], n

        def later_tensor(e):
            with e.Fori(0, B // VB) as i:
                for u in range(VT + 3):
                    if u < VT:
                        turn_chunk(e, v_tr, i * VT, u, LATER[u % NV][1])
                    if 1 <= u <= VT:
                        s = u - 1
                        w = LATER[s % NV][1] * P
                        e.wait_ge(v_tr["low"], turned_by(v_tr, i * VT, s + 1))
                        e.wait_ge(VS["v_biased"], i * VT + max(s - 1, 0) + START)
                        product(e, bank[2 + s % 2][:, 0:w], W("a0_v"), vXH[s % 2][:, 0:w], vXL[s % 2][:, 0:w]
                                ).then_inc(VS["v_ready"], 1)
                    if 2 <= u <= VT + 1:
                        s = u - 2
                        w = LATER[s % NV][1] * P
                        e.wait_ge(VS["v_low"], i * VT + (s + 1 + START))
                        e.wait_ge(VS["o_biased"], i * VT + max(s - 1, 0) + START)
                        product(e, bank[4 + s % 2][:, 0:w], W("a0_o"), vVH[s % 2][:, 0:w], vVL[s % 2][:, 0:w]
                                ).then_inc(VS["o_ready"], 1)
                    if u >= 3:
                        s = u - 3
                        e.wait_ge(VS["o_biased"], i * VT + (s + 1 + START))
                        e.wait_ge(VS["o_added"], i * VT + max(s - 1, 0) + START)
                        for t in range(LATER[s % NV][1]):
                            mm = e.transpose(bank[6 + s % 2][:, t * P:(t + 1) * P], vot[s % 2][:, t * P:(t + 1) * P], ident[:, :])
                        mm.then_inc(VS["o_turned"], 1)

        def later_scalar(e):
            with e.Fori(0, B // VB) as i:
                for u in range(VT + 2):
                    if u < VT:
                        tokens, n = later_tokens(i, u)
                        double_chunk(e, v_tr, i * VT, u, tokens, n)
                        e.wait_ge(VS["v_ready"], i * VT + max(u - 1, 0) + START)
                        high_chunk(e, v_tr, i * VT, u, n, vXH[u % 2][:, 0:n * P])
                    if 1 <= u <= VT:
                        s = u - 1
                        w = LATER[s % NV][1] * P
                        e.wait_ge(VS["v_ready"], i * VT + (s + 1 + START))
                        e.wait_ge(VS["v_low"], i * VT + max(s - 1, 0) + START)
                        e.activation(af[s % 2][:, 0:w], bank[2 + s % 2][:, 0:w], ACT.Identity,
                                     bias=bcol("a0_bv")).then_inc(VS["v_biased"], 1)
                    if u >= 2:
                        s = u - 2
                        w = LATER[s % NV][1] * P
                        e.wait_ge(VS["o_ready"], i * VT + (s + 1 + START))
                        e.wait_ge(VS["o_turned"], i * VT + max(s - 1, 0) + START)
                        e.activation(vot[s % 2][:, 0:w], bank[4 + s % 2][:, 0:w], ACT.Identity,
                                     bias=bcol("a0_bo")).then_inc(VS["o_biased"], 1)

        def later_vector(e):
            with e.Fori(0, B // VB) as i:
                for u in range(VT + 3):
                    if u < VT:
                        w = LATER[u % NV][1] * P
                        low_chunk(e, v_tr, i * VT, u, w // P, vXH[u % 2][:, 0:w], vXL[u % 2][:, 0:w])
                    if 1 <= u <= VT:
                        s = u - 1
                        w = LATER[s % NV][1] * P
                        e.wait_ge(VS["v_biased"], i * VT + (s + 1 + START))
                        e.wait_ge(VS["o_ready"], i * VT + max(s - 1, 0) + START)
                        e.tensor_copy(vVH[s % 2][:, 0:w], af[s % 2][:, 0:w]).then_inc(VS["v_high"], 1)
                        e.wait_ge(VS["v_high"], i * VT + (s + 1 + START))
                        e.tensor_tensor(vVL[s % 2][:, 0:w], af[s % 2][:, 0:w], vVH[s % 2][:, 0:w].bitcast(F32),
                                        ALU.subtract).then_inc(VS["v_low"], 1)
                    if u >= 3:
                        s = u - 3
                        e.wait_ge(VS["o_turned"], i * VT + (s + 1 + START))
                        tokens, n = later_tokens(i, s)
                        e.tensor_tensor(tokens, tokens, bank[6 + s % 2][:, :].rearrange("p (t c) -> p t c", c=P)[:, 0:n, 0:D],
                                        ALU.add).then_inc(VS["o_added"], 1)

        ctx_a = ExitStack()
        AH = sb("a0_XH", [P, BANK], F32R, ctx_a)
        AL = sb("a0_XL", [P, BANK], F32R, ctx_a)
        a_tr = turner("a0", ctx_a, [bank[0], bank[1]], B)
        SCALE = float(DH) ** -0.5
        qf = sb("a0_qf", [P, BANK], F32, ctx_a)
        kf = sb("a0_kf", [P, BANK], F32, ctx_a)
        vf = sb("a0_vf", [P, BANK], F32, ctx_a)
        qh = sb("a0_qh", [P, BANK], F32R, ctx_a)
        ql = sb("a0_ql", [P, BANK], F32R, ctx_a)
        ks = sb("a0_ks", [P, BANK], F32R, ctx_a)
        kh = [sb(f"a0_kh{j}", [P, BANK], F32R, ctx_a) for j in range(2)]
        vx = sb("a0_vx", [P, TPC, HEADS, 32], F32, ctx_a)
        PR = 3
        prob = [sb(f"a0_prob{j}", [P, BANK], F32, ctx_a) for j in range(PR)]
        probT = [sb(f"a0_probT{j}", [P, TPC, BANK], F32, ctx_a) for j in range(2)]
        nmax = sb("a0_nmax", [P, TPC * HEADS], F32, ctx_a)
        oT = sb("a0_oT", [P, 2, BANK], F32, ctx_a)
        rsum = sb("a0_rsum", [P, TPC, HEADS], F32, ctx_a)
        att = [sb(f"a0_att{j}", [P, 2, D], F32, ctx_a) for j in range(2)]
        ot = sb("a0_ot", [P, BANK], F32, ctx_a)
        ctx_a.close()
        a_names = ("vx_set qkv_ready q_biased k_biased v_biased q_high q_low k_high k_low v_turned v_stored "
                   "kh_ready s_ready max_ready exp_ready p_turned p_copied_a p_copied_v o_ready "
                   "o_copied o_turned r_ready att_ready att_turned att_high att_low w_ready w_biased w_turned w_added")
        A = {n: sem("a0_" + n) for n in a_names.split()}
        TILES = HEADS * TPC

        def a0_gpsimd(e):
            e.memset(vx[:, :, :, :], 0.0).then_inc(A["vx_set"], 1)
            e.wait_ge(A["vx_set"], 1 + START)
            e.memset(vx[:, :, :, DH:DH + 1], 1.0).then_inc(A["vx_set"], 1)

        def a0_tensor(e):
            with e.Fori(0, B) as i:
                turn_chunk(e, a_tr, i, 0, TPC)
                e.wait_ge(a_tr["low"], turned_by(a_tr, i, 1))
                for j, name in enumerate("qkv"):
                    product(e, bank[2 + j][:, :], W("a0_" + name), AH[:, 0:BANK], AL[:, 0:BANK]).then_inc(A["qkv_ready"], 1)
                e.wait_ge(A["v_biased"], i + (1 + START))
                for t in range(TPC):
                    mm = e.transpose(bank[7][:, t * P:(t + 1) * P], vf[:, t * P:(t + 1) * P], ident[:, :])
                mm.then_inc(A["v_turned"], 1)

                def scores(n):
                    h, t = divmod(n, TPC)
                    s = bank[n % 3]
                    e.wait_ge(A["kh_ready"], i * HEADS + (h + 1 + START))
                    e.wait_ge(A["exp_ready"], i * TILES + max(n - 2, 0) + START)
                    e.matmul(s[:, :], qh[:, t * P:(t + 1) * P], kh[h % 2][:, :], start=True, stop=False)
                    e.matmul(s[:, :], ql[:, t * P:(t + 1) * P], kh[h % 2][:, :], start=False, stop=False)
                    e.matmul(s[:, :], ident_bf[:, :], mask0[:, t, :], start=False, stop=True).then_inc(A["s_ready"], 1)

                def turn_probs(n):
                    b = bank[3 + n % 3]
                    e.wait_ge(A["p_copied_a"], i * (TILES // 2) + max((n - 3 + 2) // 2, 0) + START)
                    e.wait_ge(A["p_copied_v"], i * (TILES // 2) + max((n - 3 + 1) // 2, 0) + START)
                    e.wait_ge(A["exp_ready"], i * TILES + (n + 1 + START))
                    for t in range(TPC):
                        mm = e.transpose(b[:, t * P:(t + 1) * P], prob[n % PR][:, t * P:(t + 1) * P], ident[:, :])
                    mm.then_inc(A["p_turned"], 1)

                def attend(h):
                    o = bank[6 + h // 4]
                    e.wait_ge(A["p_copied_a"], i * (TILES // 2) + (h + 1) * (TPC // 2) + START)
                    e.wait_ge(A["p_copied_v"], i * (TILES // 2) + (h + 1) * (TPC // 2) + START)
                    for t in range(TPC):
                        mm = e.matmul(o[(h % 4) * 32:(h % 4 + 1) * 32, :], vx[:, t, h, :], probT[h % 2][:, t, :],
                                      start=(t == 0), stop=(t == TPC - 1))
                    mm.then_inc(A["o_ready"], 1)

                e.wait_ge(A["w_added"], i + START)
                e.wait_ge(A["q_low"], i + (1 + START))
                e.wait_ge(A["k_low"], i + (1 + START))
                e.wait_ge(A["vx_set"], 2 + START)
                e.wait_ge(A["v_stored"], i + (1 + START))
                scores(0)
                scores(1)
                for n in range(TILES):
                    if n + 2 < TILES:
                        scores(n + 2)
                    turn_probs(n)
                    if n % TPC == 1 and n >= TPC:
                        attend(n // TPC - 1)
                attend(HEADS - 1)
                for t in range(TPC):
                    if t == 0:
                        e.wait_ge(A["o_copied"], i * 2 + (2 + START))
                    if t >= 2:
                        e.wait_ge(A["att_ready"], i * TPC + (t - 1 + START))
                    for g in range(2):
                        mm = e.transpose(bank[t % 2][:, g * P:(g + 1) * P], oT[:, g, t * P:(t + 1) * P], ident[:, :])
                    mm.then_inc(A["o_turned"], 1)
                    if t >= 1:
                        e.wait_ge(A["att_ready"], i * TPC + (t + START))
                        e.transpose(bank[2][:, (t - 1) * P:t * P], att[(t - 1) % 2][:, :, :].rearrange("p a d -> p (a d)"),
                                    ident[:, :]).then_inc(A["att_turned"], 1)
                e.wait_ge(A["att_ready"], i * TPC + (TPC + START))
                e.transpose(bank[2][:, (TPC - 1) * P:BANK], att[(TPC - 1) % 2][:, :, :].rearrange("p a d -> p (a d)"),
                            ident[:, :]).then_inc(A["att_turned"], 1)
                e.wait_ge(A["att_low"], i + (1 + START))
                product(e, bank[3][:, :], W("a0_o"), AH[:, :], AL[:, :]).then_inc(A["w_ready"], 1)
                e.wait_ge(A["w_biased"], i + (1 + START))
                for t in range(TPC):
                    mm = e.transpose(bank[5][:, t * P:(t + 1) * P], ot[:, t * P:(t + 1) * P], ident[:, :])
                mm.then_inc(A["w_turned"], 1)

        def a0_scalar(e):
            with e.Fori(0, B) as i:
                e.wait_ge(A["w_ready"], i + START)
                double_chunk(e, a_tr, i, 0, Y[:, bass.ds(i * TPB, TPC), :], TPC)
                high_chunk(e, a_tr, i, 0, TPC, AH[:, :])
                e.wait_ge(A["qkv_ready"], i * 3 + (2 + START))
                e.activation(kf[:, :], bank[3][:, :], ACT.Identity, bias=bcol("a0_bk")).then_inc(A["k_biased"], 1)
                e.wait_ge(A["qkv_ready"], i * 3 + (3 + START))
                e.activation(vf[:, :], bank[4][:, :], ACT.Identity, bias=bcol("a0_bv")).then_inc(A["v_biased"], 1)
                for n in range(TILES + 1):
                    if n < TILES:
                        e.wait_ge(A["max_ready"], i * TILES + (n + 1 + START))
                        e.wait_ge(A["p_turned"], i * TILES + max(n - PR + 1, 0) + START)
                        e.activation(prob[n % PR][:, :], bank[n % 3][:, :], ACT.Exp,
                                     bias=nmax[:, n:n + 1]).then_inc(A["exp_ready"], 1)
                    if n >= 1 and (n - 1) % 2 == 0:
                        copy_probs(e, i, n - 1, "p_copied_a")
                for g in range(2):
                    e.wait_ge(A["o_ready"], i * HEADS + 4 * (g + 1) + START)
                    e.activation(oT[:, g, :], bank[6 + g][:, :], ACT.Copy).then_inc(A["o_copied"], 1)
                e.wait_ge(A["att_turned"], i * TPC + (TPC + START))
                e.activation(AH[:, 0:BANK], bank[2][:, :], ACT.Copy).then_inc(A["att_high"], 1)
                e.wait_ge(A["w_ready"], i + (1 + START))
                e.activation(ot[:, :], bank[3][:, :], ACT.Identity, bias=bcol("a0_bo")).then_inc(A["w_biased"], 1)

        def copy_probs(e, i, n, done):
            h, t = divmod(n, TPC)
            e.wait_ge(A["o_ready"], i * HEADS + max(h - 1, 0) + START)
            e.wait_ge(A["p_turned"], i * TILES + (n + 1 + START))
            dst = probT[h % 2][:, :, t * P:(t + 1) * P]
            src = bank[3 + n % 3][:, :].rearrange("p (k q) -> p k q", k=TPC)
            if done == "p_copied_a":
                e.activation(dst, src, ACT.Copy).then_inc(A[done], 1)
            else:
                e.tensor_copy(dst, src).then_inc(A[done], 1)

        def a0_vector(e):
            with e.Fori(0, B) as i:
                low_chunk(e, a_tr, i, 0, TPC, AH[:, :], AL[:, :])
                e.wait_ge(A["qkv_ready"], i * 3 + (1 + START))
                e.tensor_scalar(qf[:, :], bank[2][:, :], bcol("a0_bq"), SCALE, ALU.add, ALU.mult).then_inc(A["q_biased"], 1)
                e.wait_ge(A["q_biased"], i + (1 + START))
                e.tensor_copy(qh[:, :], qf[:, :]).then_inc(A["q_high"], 1)
                e.wait_ge(A["q_high"], i + (1 + START))
                e.tensor_tensor(ql[:, :], qf[:, :], qh[:, :].bitcast(F32), ALU.subtract).then_inc(A["q_low"], 1)
                e.wait_ge(A["k_biased"], i + (1 + START))
                e.tensor_copy(ks[:, :], kf[:, :]).then_inc(A["k_high"], 1)
                e.wait_ge(A["k_high"], i + (1 + START))
                e.tensor_tensor(ks[D:P, :], kf[D:P, :], ks[D:P, :].bitcast(F32), ALU.subtract).then_inc(A["k_low"], 1)
                e.wait_ge(A["vx_set"], 2 + START)
                e.wait_ge(A["v_turned"], i + (1 + START))
                e.tensor_copy(vx[:, :, :, 0:DH], bank[7][:, :].rearrange("p (t c) -> p t c", c=P)[:, :, 0:D]
                              .rearrange("p t (h d) -> p t h d", d=DH)).then_inc(A["v_stored"], 1)
                e.wait_ge(A["k_low"], i + (1 + START))
                for n in range(TILES + 1):
                    h = n // TPC
                    if n < TILES:
                        if n % TPC == 0:
                            e.wait_ge(A["s_ready"], i * TILES + max((h - 1) * TPC, 0) + START)
                            e.tensor_scalar(kh[h % 2][:, :], ks[:, :].bitcast(F32), head_rows[:, h:h + 1], None,
                                            ALU.mult).then_inc(A["kh_ready"], 1)
                        e.wait_ge(A["s_ready"], i * TILES + (n + 1 + START))
                        e.tensor_reduce(nmax[:, n:n + 1], bank[n % 3][:, :], X, ALU.max, negate=True).then_inc(A["max_ready"], 1)
                    if n >= 1 and (n - 1) % 2 == 1:
                        copy_probs(e, i, n - 1, "p_copied_v")
                for t in range(TPC):
                    o = bank[t % 2][:, 0:2 * P].rearrange("p (h x) -> p h x", x=32)
                    e.wait_ge(A["o_turned"], i * TPC + (t + 1 + START))
                    e.reciprocal(rsum[:, t, :], o[:, :, DH]).then_inc(A["r_ready"], 1)
                    e.wait_ge(A["r_ready"], i * TPC + (t + 1 + START))
                    e.wait_ge(A["att_turned"], i * TPC + max(t - 1, 0) + START)
                    for m in range(2):
                        a = e.tensor_tensor(att[t % 2][:, m, :].rearrange("p (h d) -> p h d", d=DH), o[:, :, 0:DH],
                                            rsum[:, t, :].unsqueeze(2).broadcast_to([P, HEADS, DH]), ALU.mult)
                    a.then_inc(A["att_ready"], 1)
                e.wait_ge(A["att_high"], i + (1 + START))
                e.tensor_tensor(AL[:, 0:BANK], bank[2][:, :], AH[:, 0:BANK].bitcast(F32), ALU.subtract).then_inc(A["att_low"], 1)
                e.wait_ge(A["w_turned"], i + (1 + START))
                yt = Y[:, bass.ds(i * TPB, TPC), :]
                e.tensor_tensor(yt, yt, bank[5][:, :].rearrange("p (t c) -> p t c", c=P)[:, :, 0:D],
                                ALU.add).then_inc(A["w_added"], 1)

        ctx_f = ExitStack()
        fmask = sb("far_mask", [P, NPAD], BF16, ctx_f)
        hotq = [sb(f"far_hotq{j}", [P, P], BF16, ctx_f) for j in range(2)]
        hotk = [sb(f"far_hotk{j}", [P, NPAD], BF16, ctx_f) for j in range(2)]
        eq = sb("far_eq", [P, E_PER], F32, ctx_f)
        ekr = sb("far_ekr", [P, NS, E_PER], F32, ctx_f)
        selfk = sb("far_self", [P, NS], F32, ctx_f)
        f_dup = sb("far_dup", [P, TPC, 2, D], F32, ctx_f)
        f_xh = sb("far_xh", [P, BANK], F32R, ctx_f)
        f_xl = sb("far_xl", [P, BANK], F32R, ctx_f)
        f_kf = sb("far_kf", [P, BANK], F32, ctx_f)
        f_ks = sb("far_ks", [P, NPAD], F32R, ctx_f)
        f_kh = sb("far_kh", [P, NPAD], F32R, ctx_f)
        f_vt = sb("far_vt", [P, TPB, HEADS, DH + 1], F32, ctx_f)
        f_vh = sb("far_vh", [P, TPB, DH + 1], F32, ctx_f)
        f_qf = sb("far_qf", [P, P], F32, ctx_f)
        f_qh = sb("far_qh", [P, P], F32R, ctx_f)
        f_ql = sb("far_ql", [P, P], F32R, ctx_f)
        f_nm = sb("far_nm", [P, NS + 1], F32, ctx_f)
        f_prob = sb("far_prob", [P, NPAD], F32, ctx_f)
        f_rs = sb("far_rs", [P, 1], F32, ctx_f)
        f_att = sb("far_att", [P, 2, D], F32, ctx_f)
        f_ah = sb("far_ah", [P, P], F32R, ctx_f)
        f_al = sb("far_al", [P, P], F32R, ctx_f)
        far_out = sb("far_out", [P, T, D], F32, ctx_f)
        ctx_f.close()
        f_names = ("set dve zeroed hot_ready hot_used mask_ready unit_done job_done doubled turned high low projected "
                   "unit_dve kh_ready scored max_ready head_dve expd p_turned copied attended att_ready att_turned "
                   "att_high att_low out_ready")
        FS = dict(zip(f_names.split(), A.values()))
        SLOTS = E_PER + 1
        JOBS = NS + 1
        JOB_LINKS, QUERY_LINKS, OUT_LINKS, HEAD_LINKS = 4, 3, 2, 3
        UNIT_LINKS = NS * JOB_LINKS + QUERY_LINKS + OUT_LINKS

        def far_gpsimd(e):
            e.memset(f_vt[:, :, :, :], 1.0).then_inc(FS["set"], 1)
            e.iota(selfk[:, :], pattern=[[-BANK, NS]], base=0, channel_multiplier=1,
                   allow_small_or_imprecise_dtypes=True).then_inc(FS["set"], 1)
            for n in t_sems:
                e.sem_inc(t_sems[n], B * NS)

        def far_tensor(e):
            e.sem_inc(FS["hot_used"], 2)
            with e.Fori(0, TPB) as q:
                with e.Fori(0, E_PER // 2) as j:
                    e.wait_ge(FS["zeroed"], q + (1 + START))
                    for u in range(2):
                        e.wait_ge(FS["hot_ready"], q * SLOTS + j * 2 + (u + 1 + START))
                        for k, (c, w) in enumerate(SPANS):
                            mm = e.matmul(bank[k][:, 0:w], hotq[u][:, :], hotk[u][:, c:c + w],
                                          start=False, stop=False, skip_group_check=True)
                        mm.then_inc(FS["hot_used"], 1)
                e.wait_ge(FS["hot_ready"], q * SLOTS + (SLOTS + START))
                for k, (c, w) in enumerate(SPANS):
                    mm = e.matmul(bank[k][:, 0:w], ident_bf[:, :], hotk[0][:, c:c + w],
                                  start=False, stop=False, skip_group_check=True)
                mm.then_inc(FS["hot_used"], 1)
                with e.Fori(0, B) as b:
                    r = q * B + b
                    e.wait_ge(FS["mask_ready"], q + (1 + START))
                    e.wait_ge(FS["unit_done"], r + (1 + START))
                    for m in range(JOBS):
                        n = SPANS[m][1] // P if m < NS else 1
                        e.wait_ge(FS["job_done"], r * JOBS + (m + 1 + START))
                        e.wait_ge(FS["doubled"], r * JOBS + (m + 1 + START))
                        for t in range(n):
                            mm = e.transpose(bank[0][:, t * P:(t + 1) * P],
                                             f_dup[:, t, :, :].rearrange("p a d -> p (a d)"), ident[:, :])
                        mm.then_inc(FS["turned"], 1)
                        e.wait_ge(FS["low"], r * JOBS + (m + 1 + START))
                        mm = product(e, bank[1][:, 0:n * P], W("a0_k" if m < NS else "a0_q"), f_xh[:, 0:n * P], f_xl[:, 0:n * P])
                        if m < NS:
                            for t in range(n):
                                v = bank[2][:, t * D:(t + 1) * D]
                                e.matmul(v, f_xh[:, t * P:(t + 1) * P], W("a0_v", 0, D), start=True, stop=False)
                                mm = e.matmul(v, f_xl[:, t * P:(t + 1) * P], W("a0_v", 0, D), start=False, stop=True)
                        mm.then_inc(FS["projected"], 1)
                    with e.Fori(0, HEADS) as h:
                        u = r * HEADS + h
                        e.wait_ge(FS["kh_ready"], u * 2 + (2 + START))
                        for k, (c, w) in enumerate(SPANS):
                            e.matmul(bank[k][:, 0:w], f_qh[:, :], f_kh[:, c:c + w], start=True, stop=False)
                            e.matmul(bank[k][:, 0:w], f_ql[:, :], f_kh[:, c:c + w], start=False, stop=False)
                            e.matmul(bank[k][:, 0:w], ident_bf[:, :], fmask[:, c:c + w],
                                     start=False, stop=True).then_inc(FS["scored"], 1)
                        for k, (c, w) in enumerate(SPANS):
                            e.wait_ge(FS["expd"], u * NS + (k + 1 + START))
                            for t in range(w // P):
                                mm = e.transpose(bank[k][:, t * P:(t + 1) * P], f_prob[:, c + t * P:c + (t + 1) * P], ident[:, :])
                            mm.then_inc(FS["p_turned"], 1)
                        e.wait_ge(FS["copied"], u * NS + (NS + START))
                        for t in range(TPB):
                            mm = e.matmul(bank[7][:, 0:DH + 1], f_prob[:, t * P:(t + 1) * P], f_vh[:, t, :],
                                          start=(t == 0), stop=(t == TPB - 1))
                        mm.then_inc(FS["attended"], 1)
                    e.wait_ge(FS["att_ready"], r + (1 + START))
                    e.transpose(bank[0][:, 0:P], f_att[:, :, :].rearrange("p a d -> p (a d)"), ident[:, :]
                                ).then_inc(FS["att_turned"], 1)
                    e.wait_ge(FS["att_low"], r + (1 + START))
                    e.matmul(bank[1][:, 0:D], f_ah[:, :], W("a0_o", 0, D), start=True, stop=False)
                    e.matmul(bank[1][:, 0:D], f_al[:, :], W("a0_o", 0, D), start=False, stop=True).then_inc(FS["out_ready"], 1)

        def far_scalar(e):
            with e.Fori(0, TPB) as q:
                with e.Fori(0, B) as b:
                    r = q * B + b
                    for m in range(JOBS):
                        e.wait_ge(FS["job_done"], r * JOBS + (m + 1 + START))
                        n = SPANS[m][1] // P if m < NS else 1
                        first = b * TPB + m * TPC if m < NS else b * TPB + q
                        e.activation(f_dup[:, 0:n, :, :], Y[:, bass.ds(first, n), :].unsqueeze(2).broadcast_to([P, n, 2, D]),
                                     ACT.Copy).then_inc(FS["doubled"], 1)
                        e.wait_ge(FS["turned"], r * JOBS + (m + 1 + START))
                        e.activation(f_xh[:, 0:n * P], bank[0][:, 0:n * P], ACT.Copy).then_inc(FS["high"], 1)
                    with e.Fori(0, HEADS) as h:
                        u = r * HEADS + h
                        e.wait_ge(FS["max_ready"], u + (1 + START))
                        for k, (c, w) in enumerate(SPANS):
                            e.activation(f_prob[:, c:c + w], bank[k][:, 0:w], ACT.Exp, bias=f_nm[:, NS:NS + 1]
                                         ).then_inc(FS["expd"], 1)
                        for k, (c, w) in enumerate(SPANS):
                            e.wait_ge(FS["p_turned"], u * NS + (k + 1 + START))
                            e.activation(f_prob[:, c:c + w], bank[k][:, 0:w], ACT.Copy).then_inc(FS["copied"], 1)
                    e.wait_ge(FS["att_turned"], r + (1 + START))
                    e.activation(f_ah[:, :], bank[0][:, 0:P], ACT.Copy).then_inc(FS["att_high"], 1)

        def far_vector(e):
            e.wait_ge(FS["set"], 2 + START)
            s = Chain(e, FS["dve"], START)
            s.mark(e.tensor_copy(eq[:, :], edges_f[:, 0, :]))
            for k, (c, w) in enumerate(SPANS):
                s.mark(e.tensor_scalar(ekr[:, k, :], edges_f[:, 1, :], float(-c), None, ALU.add))
            s.wait()
            e.sem_inc(FS["unit_done"], 1)
            e.sem_inc(FS["job_done"], 1)
            with e.Fori(0, TPB) as q:
                for k in range(NS):
                    a = e.memset(bank[k][:, :], 0.0)
                a.then_inc(FS["zeroed"], 1)

                def hot_keys(buf, ids):
                    for k, (c, w) in enumerate(SPANS):
                        a = e.tensor_scalar(buf[:, c:c + w], node[:, 0:w], ids(k), None, ALU.is_equal)
                    a.then_inc(FS["hot_ready"], 1)

                with e.Fori(0, E_PER // 2) as j:
                    for u in range(2):
                        e.wait_ge(FS["hot_used"], q * SLOTS + j * 2 + (u + 1 + START))
                        e.tensor_scalar(hotq[u][:, :], node[:, 0:P], eq[:, bass.ds(j * 2 + u, 1)], None, ALU.is_equal)
                        hot_keys(hotk[u], lambda k: ekr[:, k, bass.ds(j * 2 + u, 1)])
                e.wait_ge(FS["hot_used"], q * SLOTS + (SLOTS + 1 + START))
                hot_keys(hotk[0], lambda k: selfk[:, k:k + 1])
                e.wait_ge(FS["hot_used"], q * SLOTS + (SLOTS + 2 + START))
                s = Chain(e, FS["dve"], START + 1 + NS, q, NS + 1)
                for k, (c, w) in enumerate(SPANS):
                    s.mark(e.tensor_scalar(fmask[:, c:c + w], bank[k][:, 0:w], 0.5, MASKED, ALU.is_lt, ALU.mult))
                s.wait()
                s.link(e.memset(fmask[:, N:NPAD], MASKED))
                s.close()
                e.tensor_scalar(eq[:, :], eq[:, :], float(-P), None, ALU.add)
                e.tensor_scalar(selfk[:, :], selfk[:, :], float(P), None, ALU.add).then_inc(FS["mask_ready"], 1)
                with e.Fori(0, B) as b:
                    r = q * B + b
                    e.wait_ge(FS["mask_ready"], q + (1 + START))
                    s = Chain(e, FS["unit_dve"], START, r, UNIT_LINKS)
                    for m in range(JOBS):
                        n = SPANS[m][1] // P if m < NS else 1
                        w = n * P
                        e.wait_ge(FS["high"], r * JOBS + (m + 1 + START))
                        e.tensor_tensor(f_xl[:, 0:w], bank[0][:, 0:w], f_xh[:, 0:w].bitcast(F32), ALU.subtract
                                        ).then_inc(FS["low"], 1)
                        e.wait_ge(FS["projected"], r * JOBS + (m + 1 + START))
                        if m < NS:
                            c = SPANS[m][0]
                            s.link(e.tensor_scalar(f_kf[:, 0:w], bank[1][:, 0:w], bcol("a0_bk"), None, ALU.add))
                            s.link(e.tensor_copy(f_ks[:, c:c + w], f_kf[:, 0:w]))
                            s.mark(e.tensor_tensor(f_ks[D:P, c:c + w], f_kf[D:P, 0:w], f_ks[D:P, c:c + w].bitcast(F32),
                                                   ALU.subtract))
                            for t in range(n):
                                a = e.tensor_tensor(f_vt[:, m * TPC + t, :, 0:DH],
                                                    bank[2][:, t * D:(t + 1) * D].rearrange("p (h d) -> p h d", d=DH),
                                                    row_bias[:, 0, :].rearrange("p (h d) -> p h d", d=DH), ALU.add)
                            s.link(a)
                        else:
                            s.link(e.tensor_scalar(f_qf[:, :], bank[1][:, 0:P], bcol("a0_bq"), SCALE, ALU.add, ALU.mult))
                            s.link(e.tensor_copy(f_qh[:, :], f_qf[:, :]))
                            s.link(e.tensor_tensor(f_ql[:, :], f_qf[:, :], f_qh[:, :].bitcast(F32), ALU.subtract))
                        e.sem_inc(FS["job_done"], 1)
                    with e.Fori(0, HEADS) as h:
                        u = r * HEADS + h
                        e.tensor_scalar(f_kh[:, :], f_ks[:, :].bitcast(F32), head_rows[:, bass.ds(h, 1)], None, ALU.mult
                                        ).then_inc(FS["kh_ready"], 1)
                        e.tensor_copy(f_vh[:, :, :], f_vt[:, :, bass.ds(h, 1), :].rearrange("p t h d -> p t (h d)")
                                      ).then_inc(FS["kh_ready"], 1)
                        ch = Chain(e, FS["head_dve"], START, u, HEAD_LINKS)
                        for k, (c, w) in enumerate(SPANS):
                            e.wait_ge(FS["scored"], u * NS + (k + 1 + START))
                            a = e.tensor_reduce(f_nm[:, k:k + 1], bank[k][:, 0:w], X, ALU.max, negate=True)
                        ch.link(a)
                        e.tensor_reduce(f_nm[:, NS:NS + 1], f_nm[:, 0:NS], X, ALU.min).then_inc(FS["max_ready"], 1)
                        e.wait_ge(FS["attended"], u + (1 + START))
                        ch.link(e.reciprocal(f_rs[:, :], bank[7][:, DH:DH + 1]))
                        for g in range(2):
                            a = e.tensor_scalar(f_att[:, g, bass.ds(h * DH, DH)], bank[7][:, 0:DH], f_rs[:, :], None, ALU.mult)
                        ch.link(a)
                        ch.close()
                    e.sem_inc(FS["att_ready"], 1)
                    e.wait_ge(FS["att_high"], r + (1 + START))
                    e.tensor_tensor(f_al[:, :], bank[0][:, 0:P], f_ah[:, :].bitcast(F32), ALU.subtract).then_inc(FS["att_low"], 1)
                    e.wait_ge(FS["out_ready"], r + (1 + START))
                    o = far_out[:, bass.ds(b * TPB + q, 1), :].rearrange("p t d -> p (t d)")
                    y = Y[:, bass.ds(b * TPB + q, 1), :].rearrange("p t d -> p (t d)")
                    s.link(e.tensor_tensor(o, y, bank[1][:, 0:D], ALU.add))
                    s.link(e.tensor_tensor(o, o, row_bias[:, 1, :], ALU.add))
                    s.close()
                    e.sem_inc(FS["unit_done"], 1)
            for b in range(B):
                a = e.tensor_copy(rows_of(Y, b), rows_of(far_out, b))
            a.then_inc(FS["zeroed"], 1)
            e.wait_ge(FS["zeroed"], TPB + (1 + START))

        def near_only(e, stage):
            beyond = e.value_load(any_far[0:1, 0:1])
            with e.If(beyond <= 0):
                stage(e)

        def near_or_far(e, near, far_):
            beyond = e.value_load(any_far[0:1, 0:1])
            with e.If(beyond <= 0):
                near(e)
            with e.If(beyond > 0):
                far_(e)

        f0 = ffn("f0", E0, f0_w2, "relu", Y, 0, 0, 0, 0, 0, True)

        ctx_b = ExitStack()
        QH = sb("a1_QH", [P, NPAD], F32R, ctx_b)
        QL = sb("a1_QL", [P, NPAD], F32R, ctx_b)
        KS = sb("a1_KS", [P, NPAD], F32R, ctx_b)
        b_tr = turner("a1", ctx_b, [bank[0], bank[1]], B * NS)
        qf1 = [sb(f"a1_qf{j}", [P, BANK], F32, ctx_b) for j in range(2)]
        kf1 = sb("a1_kf", [P, BANK], F32, ctx_b)
        vf1 = sb("a1_vf", [P, BANK], F32, ctx_b)
        V = sb("a1_V", [P, TPB, D], F32, ctx_b)
        PB = 2
        pT = [sb(f"a1_pT{j}", [P, NS, BANK], F32, ctx_b) for j in range(PB)]
        vs = [sb(f"a1_vs{j}", [P, NS, D], F32, ctx_b) for j in range(2)]
        oS = sb("a1_oS", [P, 4, BANK], F32, ctx_b)
        nm = [sb(f"a1_nm{j}", [P, NS], F32, ctx_b) for j in range(2)]
        sm = [sb(f"a1_sm{j}", [P, NS], F32, ctx_b) for j in range(2)]
        fc = [sb(f"a1_fc{j}", [P, NS], F32, ctx_b) for j in range(2)]
        tot = [sb(f"a1_tot{j}", [P, 4], F32, ctx_b) for j in range(2)]
        later = sb("a1_later", [P, P], BF16, ctx_b)
        laterf = sb("a1_laterf", [P, BANK], F32, ctx_b)
        first_key = sb("a1_first", [P, 1], F32, ctx_b)
        ctx_b.close()
        b_names = ("set qkv_ready q_scaled k_copied v_copied q_high q_low k_high k_low v_turned v_stored s_ready masked "
                   "max_ready exp_ready min_ready f_ready dve scaled pv_done o_ready o_copied o_turned o_added")
        Z = {n: sem("a1_" + n) for n in b_names.split()}
        MASK_ALL = -1.0e10 / 8.0

        def widths(j):
            if j == 0:
                return [min(BANK, N - c * BANK) for c in range(NS)]
            end = min((j + 1) * P, N)
            return [min(BANK, end - c * BANK) for c in range(j // TPC + 1)]

        first_chunk, at_chunk = [], 0
        for j in range(TPB):
            first_chunk.append(at_chunk)
            at_chunk += len(widths(j))
        CHUNKS = at_chunk
        RS = 4
        SMALL = 4

        def a1_gpsimd(e):
            e.memset(V[:, :, :], 0.0).then_inc(Z["set"], 1)
            e.memset(oS[:, :, :], 0.0).then_inc(Z["set"], 1)
            e.memset(laterf[:, :], 0.0).then_inc(Z["set"], 1)
            e.memset(first_key[:, :], MASKED).then_inc(Z["set"], 1)
            e.wait_ge(Z["set"], 4 + START)
            e.memset(first_key[0:1, :], MASK_ALL).then_inc(Z["set"], 1)
            e.affine_select(out=laterf[:, :], in_=laterf[:, :], compare_op=ALU.is_gt, fill=MASKED, base=0,
                            pattern=[[-1, BANK]], channel_multiplier=1).then_inc(Z["set"], 1)
            e.wait_ge(Z["set"], 6 + START)
            e.tensor_copy(later[:, :], laterf[:, 0:P]).then_inc(Z["set"], 1)
            e.wait_ge(Z["set"], 7 + START)
            e.memset(laterf[0:1, :], MASK_ALL).then_inc(Z["set"], 1)
            with e.Fori(0, B) as i:
                for j in range(TPB):
                    nc_ = len(widths(j))
                    e.wait_ge(Z["pv_done"], i * CHUNKS + (first_chunk[j - 1] if j >= 1 else 0 + START))
                    e.wait_ge(Z["dve"], i * (TPB * SMALL) + (j + 1) * SMALL + START)
                    e.tensor_tensor(vs[j % 2][:, 0:nc_, :], V[:, j, :].unsqueeze(1).broadcast_to([P, nc_, D]),
                                    fc[j % 2][:, 0:nc_].unsqueeze(2).broadcast_to([P, nc_, D]),
                                    ALU.mult).then_inc(Z["scaled"], 1)

        def a1_tensor(e):
            e.wait_ge(Z["set"], 8 + START)
            with e.Fori(0, B) as i:
                def projections(k):
                    c, w = SPANS[k]
                    hi, lo = QH[:, c:c + w], QL[:, c:c + w]
                    e.wait_ge(b_tr["low"], turned_by(b_tr, i * NS, k + 1))
                    e.wait_ge(Z["q_scaled"], i * NS + (k + START))
                    product(e, bank[2][:, 0:w], W("a1_q"), hi, lo)
                    e.wait_ge(Z["k_copied"], i * NS + (k + START))
                    product(e, bank[3][:, 0:w], W("a1_k"), hi, lo)
                    e.wait_ge(Z["v_copied"], i * NS + (k + START))
                    product(e, bank[4][:, 0:w], W("a1_v"), hi, lo).then_inc(Z["qkv_ready"], 1)

                def values(k):
                    e.wait_ge(Z["v_stored"], i * NS + max(k - 1, 0) + START)
                    e.wait_ge(Z["v_copied"], i * NS + (k + 1 + START))
                    for t in range(SPANS[k][1] // P):
                        mm = e.transpose(bank[5 + k % 2][:, t * P:(t + 1) * P], vf1[:, t * P:(t + 1) * P], ident[:, :])
                    mm.then_inc(Z["v_turned"], 1)

                turn_chunk(e, b_tr, i * NS, 0, SPANS[0][1] // P)
                for k in range(NS):
                    if k + 1 < NS:
                        turn_chunk(e, b_tr, i * NS, k + 1, SPANS[k + 1][1] // P)
                    projections(k)
                    values(k)

                def scores(j, c):
                    n = first_chunk[j] + c
                    w = widths(j)[c]
                    s = bank[n % RS]
                    e.wait_ge(Z["exp_ready"], i * CHUNKS + max(n + 1 - RS, 0) + START)
                    diagonal = j > 0 and c == len(widths(j)) - 1
                    k = KS[:, j * P:(j + 1) * P]
                    e.matmul(s[:, 0:w], k, QH[:, c * BANK:c * BANK + w], start=True, stop=False)
                    if diagonal:
                        lo = j * P - c * BANK
                        e.matmul(s[:, lo:w], ident_bf[:, :], later[:, 0:w - lo], start=False, stop=False,
                                 skip_group_check=True)
                    mm = e.matmul(s[:, 0:w], k, QL[:, c * BANK:c * BANK + w], start=False, stop=True)
                    mm.then_inc(Z["s_ready"], 1)

                def attend(j):
                    e.wait_ge(Z["scaled"], i * TPB + (j + 1 + START))
                    for c, w in enumerate(widths(j)):
                        n = first_chunk[j] + c
                        r = c % 2
                        mm = e.matmul(bank[4 + c // 2][r * D:(r + 1) * D, 0:w], vs[j % 2][:, c, :], pT[j % PB][:, c, 0:w],
                                      start=(j == 0), stop=(j == TPB - 1), skip_group_check=True)
                        mm.then_inc(Z["pv_done"], 1)

                e.wait_ge(Z["q_low"], i * NS + (NS + START))
                e.wait_ge(Z["k_low"], i * NS + (NS + START))
                e.wait_ge(Z["v_stored"], i * NS + (NS + START))
                for j in range(TPB + 1):
                    ahead = widths(j) if j < TPB else []
                    split = min(len(ahead), RS - 1)
                    for c in range(split):
                        scores(j, c)
                    if j >= 2:
                        attend(j - 2)
                    for c in range(split, len(ahead)):
                        scores(j, c)
                attend(TPB - 1)
                for q in range(4):
                    e.wait_ge(Z["o_added"], i * 4 + max(q - 1, 0) + START)
                    e.wait_ge(Z["o_copied"], i * 4 + (q + 1 + START))
                    for t in range(TPC if q < 3 else 1):
                        mm = e.transpose(bank[q % 2][:, t * P:(t + 1) * P], oS[:, q, t * P:(t + 1) * P], ident[:, :])
                    mm.then_inc(Z["o_turned"], 1)
                e.wait_ge(Z["o_added"], i * 4 + (4 + START))

        def a1_scalar(e):
            with e.Fori(0, B) as i:
                e.wait_ge(Z["s_ready"], i * CHUNKS + START)

                def tokens(k):
                    c, w = SPANS[k]
                    n = w // P
                    double_chunk(e, b_tr, i * NS, k, Y[:, bass.ds(i * TPB + k * TPC, n), :], n)
                    high_chunk(e, b_tr, i * NS, k, n, QH[:, c:c + w])

                tokens(0)
                for k, (c, w) in enumerate(SPANS):
                    if k + 1 < NS:
                        tokens(k + 1)
                    e.wait_ge(Z["qkv_ready"], i * NS + (k + 1 + START))
                    e.wait_ge(Z["q_low"], i * NS + max(k - 1, 0) + START)
                    e.activation(qf1[k % 2][:, 0:w], bank[2][:, 0:w], ACT.Copy, scale=1.0 / 8.0).then_inc(Z["q_scaled"], 1)
                    e.wait_ge(Z["k_low"], i * NS + (k + START))
                    e.activation(kf1[:, 0:w], bank[3][:, 0:w], ACT.Copy).then_inc(Z["k_copied"], 1)
                    e.wait_ge(Z["v_turned"], i * NS + (k + START))
                    e.activation(vf1[:, 0:w], bank[4][:, 0:w], ACT.Copy).then_inc(Z["v_copied"], 1)
                for j in range(TPB):
                    for c, w in enumerate(widths(j)):
                        n = first_chunk[j] + c
                        p = pT[j % PB][:, c, 0:w]
                        e.wait_ge(Z["max_ready"], i * CHUNKS + (n + 1 + START))
                        if j >= PB:
                            e.wait_ge(Z["pv_done"], i * CHUNKS + (first_chunk[j - PB] + min(c, len(widths(j - PB)) - 1) + 1 + START))
                            if c == 0:
                                e.wait_ge(Z["dve"], i * (TPB * SMALL) + (j - 1) * SMALL + START)
                        src = p if j == 0 else bank[n % RS][:, 0:w]
                        e.activation(p, src, ACT.Exp, bias=nm[j % 2][:, c:c + 1],
                                     accum_out=sm[j % 2][:, c:c + 1]).then_inc(Z["exp_ready"], 1)
                    e.wait_ge(Z["min_ready"], i * TPB + (j + 1 + START))
                    e.wait_ge(Z["scaled"], i * TPB + max(j - 1, 0) + START)
                    nc_ = len(widths(j))
                    e.activation(fc[j % 2][:, 0:nc_], nm[j % 2][:, 0:nc_], ACT.Exp, bias=tot[j % 2][:, 0:1],
                                 scale=-1.0).then_inc(Z["f_ready"], 1)
                for q in range(4):
                    e.wait_ge(Z["pv_done"], i * CHUNKS + (CHUNKS + START))
                    if q < 3:
                        a = e.activation(oS[:, q, :], bank[4 + q][:, :], ACT.Copy)
                    else:
                        a = e.activation(oS[0:D, q, 0:LAST], bank[4 + q][0:D, 0:LAST], ACT.Copy)
                    a.then_inc(Z["o_copied"], 1)

        def a1_vector(e):
            e.wait_ge(Z["set"], 8 + START)
            with e.Fori(0, B) as i:
                low_chunk(e, b_tr, i * NS, 0, SPANS[0][1] // P, QH[:, 0:BANK], QL[:, 0:BANK])
                for k, (c, w) in enumerate(SPANS):
                    if k + 1 < NS:
                        c2, w2 = SPANS[k + 1]
                        low_chunk(e, b_tr, i * NS, k + 1, w2 // P, QH[:, c2:c2 + w2], QL[:, c2:c2 + w2])
                    e.wait_ge(Z["q_scaled"], i * NS + (k + 1 + START))
                    e.tensor_copy(QH[:, c:c + w], qf1[k % 2][:, 0:w]).then_inc(Z["q_high"], 1)
                    e.wait_ge(Z["k_copied"], i * NS + (k + 1 + START))
                    e.tensor_copy(KS[:, c:c + w], kf1[:, 0:w]).then_inc(Z["k_high"], 1)
                    e.wait_ge(Z["q_high"], i * NS + (k + 1 + START))
                    e.tensor_tensor(QL[:, c:c + w], qf1[k % 2][:, 0:w], QH[:, c:c + w].bitcast(F32),
                                    ALU.subtract).then_inc(Z["q_low"], 1)
                    e.wait_ge(Z["k_high"], i * NS + (k + 1 + START))
                    e.tensor_tensor(KS[D:P, c:c + w], kf1[D:P, 0:w], KS[D:P, c:c + w].bitcast(F32),
                                    ALU.subtract).then_inc(Z["k_low"], 1)
                    e.wait_ge(Z["v_turned"], i * NS + (k + 1 + START))
                    n = w // P
                    hi = P if k < NS - 1 else LAST
                    e.tensor_copy(V[0:hi, k * TPC:k * TPC + n, :],
                                  bank[5 + k % 2][0:hi, :].rearrange("p (t c) -> p t c", c=P)[:, 0:n, 0:D]
                                  ).then_inc(Z["v_stored"], 1)

                def tile_sums(j):
                    nc_ = len(widths(j))
                    r = j % 2
                    ch = Chain(e, Z["dve"], START + j * SMALL, i, TPB * SMALL)
                    e.wait_ge(Z["f_ready"], i * TPB + (j + 1 + START))
                    ch.link(e.tensor_tensor(sm[r][:, 0:nc_], sm[r][:, 0:nc_], fc[r][:, 0:nc_], ALU.mult))
                    ch.link(e.tensor_reduce(tot[r][:, 1:2], sm[r][:, 0:nc_], X, ALU.add))
                    ch.link(e.reciprocal(tot[r][:, 2:3], tot[r][:, 1:2]))
                    ch.mark(e.tensor_scalar(fc[r][:, 0:nc_], fc[r][:, 0:nc_], tot[r][:, 2:3], None, ALU.mult))

                for j in range(TPB):
                    ws = widths(j)
                    for c, w in enumerate(ws):
                        n = first_chunk[j] + c
                        src = bank[n % RS][:, 0:w]
                        e.wait_ge(Z["s_ready"], i * CHUNKS + (n + 1 + START))
                        if j == 0:
                            src = pT[0][:, c, 0:w]
                            e.wait_ge(Z["pv_done"], i * CHUNKS + START)
                            if c == 0:
                                a = e.tensor_tensor(src, bank[n % RS][:, 0:w], laterf[:, 0:w], ALU.add)
                            else:
                                a = e.tensor_scalar(src, bank[n % RS][:, 0:w], first_key[:, :], None, ALU.add)
                            a.then_inc(Z["masked"], 1)
                            e.wait_ge(Z["masked"], i * NS + (n + 1 + START))
                        e.tensor_reduce(nm[j % 2][:, c:c + 1], src, X, ALU.max, negate=True).then_inc(Z["max_ready"], 1)
                        if j >= 1 and c == min(1, len(ws) - 1):
                            tile_sums(j - 1)
                    e.wait_ge(Z["max_ready"], i * CHUNKS + (first_chunk[j] + len(ws) + START))
                    e.tensor_reduce(tot[j % 2][:, 0:1], nm[j % 2][:, 0:len(ws)], X, ALU.min).then_inc(Z["min_ready"], 1)
                tile_sums(TPB - 1)
                for q in range(4):
                    e.wait_ge(Z["o_turned"], i * 4 + (q + 1 + START))
                    if q < 3:
                        h = H[:, bass.ds(i * TPB + 2 * q * TPC, 2 * TPC), :].rearrange("p (a t) d -> p t a d", a=2)
                        o = bank[q % 2][:, :].rearrange("p (t a d) -> p t a d", a=2, d=D)
                        e.tensor_tensor(h, h, o, ALU.add).then_inc(Z["o_added"], 1)
                    else:
                        h = H[0:LAST, bass.ds(i * TPB + 2 * q * TPC, 1), :].rearrange("p t d -> p (t d)")
                        e.tensor_tensor(h, h, bank[q % 2][0:LAST, 0:D], ALU.add).then_inc(Z["o_added"], 1)

        def started():
            return [t_split, t_logit, t_out, t_turned, t_gated, *t_sems.values(), *VS.values(), *A.values(),
                    *(G[n] for n in ("logit", "lt_biased", "lt_turned", "stored")), *Z.values()]

        stages = [
            (weights_sync, weights_gpsimd, weights_scalar, weights_vector, weights_tensor),
            (tok_sync, tok_gpsimd, tok_scalar, tok_vector, tok_tensor),
        ]
        def norm(k, src, affine=None):
            return (None, (lambda e: norm_gpsimd(e, affine)) if affine is not None else None,
                    lambda e: norm_scalar(e, k), lambda e: norm_vector(e, k, src, affine), None)
        f1 = ffn("f1", E1, f1_w2, "gelu", H, 1, NCH, NCH * E0, NCH * E0 // 2, GATE_LINKS, False)
        stages += [norm(0, H), (None, None, lambda e: near_only(e, later_scalar), lambda e: near_only(e, later_vector),
                                  lambda e: near_only(e, later_tensor)),
                   (None, lambda e: near_or_far(e, a0_gpsimd, far_gpsimd), lambda e: near_or_far(e, a0_scalar, far_scalar),
                    lambda e: near_or_far(e, a0_vector, far_vector), lambda e: near_or_far(e, a0_tensor, far_tensor)),
                   norm(1, Y, 0)]
        stages += [norm(2, H), f0["a"], f0["b"], f0["c"]]
        stages += [(None, a1_gpsimd, a1_scalar, a1_vector, a1_tensor)]
        stages += [norm(3, H), f1["a"], f1["b"], f1["c"]]

        block = ctx.enter_context(nc.Block())

        def run(e, which):
            for k, st in enumerate(stages):
                if st[which] is not None:
                    st[which](e)
                stage_end(e, k + 1)

        @block.sync
        def _(e):
            run(e, 0)
            for b in range(B):
                e.dma_start(out[b, 0:(TPB - 1) * P, :].rearrange("(t p) d -> p t d", p=P),
                            H[:, b * TPB:(b + 1) * TPB - 1, :]).then_inc(stored, 16)
                e.dma_start(out[b, (TPB - 1) * P:N, :], H[0:LAST, (b + 1) * TPB - 1, :]).then_inc(stored, 16)
            e.wait_ge(stored, 2 * B * 16)

        @block.gpsimd
        def _(e):
            run(e, 1)

        @block.scalar
        def _(e):
            run(e, 2)

        @block.vector
        def _(e):
            run(e, 3)

        @block.tensor
        def _(e):
            run(e, 4)


_INS = ["x", "txt", "L0_tok_W1", "L0_tok_b1", "L0_tok_W2", "L0_tok_b2", "L0_tok_W3", "L0_tok_b3",
        "L0_attn_edge_index", "L0_attn_Wq", "L0_attn_bq", "L0_attn_Wk", "L0_attn_bk", "L0_attn_Wv", "L0_attn_bv",
        "L0_attn_Wo", "L0_attn_bo", "L0_attn_gamma", "L0_attn_beta", "L0_ffn_gate_w", "L0_ffn_gate_b",
        "L0_ffn_w1", "L0_ffn_b1", "L0_ffn_w2", "L0_ffn_b2", "L0_ffn_gamma", "L0_ffn_beta", "L1_attn_Wq",
        "L1_attn_Wk", "L1_attn_Wv", "L1_ffn_gate_w", "L1_ffn_gate_b", "L1_ffn_W1", "L1_ffn_b1", "L1_ffn_W2",
        "L1_ffn_b2"]


def kernel(**inputs):
    import numpy as _np
    import concourse.bacc as _bacc
    from concourse import mybir as _mybir
    from concourse.bass_utils import run_bass_kernel_spmd as _run

    nc = _bacc.Bacc("TRN2", target_bir_lowering=False, num_devices=1)
    arrays, ins = {}, {}
    for name in _INS:
        a = _np.ascontiguousarray(inputs[name])
        arrays[f"in_{name}_dram"] = a
        ins[name] = nc.dram_tensor(f"in_{name}_dram", a.shape, _mybir.dt.from_np(a.dtype), kind="ExternalInput").ap()
    shape = (inputs["x"].shape[0], inputs["x"].shape[2] * inputs["x"].shape[3] + inputs["txt"].shape[1],
             inputs["x"].shape[1])
    out = nc.dram_tensor("out_0_dram", shape, _mybir.dt.float32, kind="ExternalOutput").ap()
    build(nc, ins, out)
    r = _run(nc, [arrays], core_ids=[0])
    return r.results[0]["out_0_dram"]
```

```python
from contextlib import ExitStack

import concourse.bass as bass
from concourse import mybir

F32 = mybir.dt.float32
F32R = mybir.dt.float32r
BF16 = mybir.dt.bfloat16
F16 = mybir.dt.float16
I32 = mybir.dt.int32
ALU = mybir.AluOpType
ACT = mybir.ActivationFunctionType
X = mybir.AxisListType.X

P = 128
BANK = 512
START = 1
MASKED = -1.0e30
LN_EPS = 1e-5


class Chain:

    def __init__(self, eng, sem, done=0, turn=None, per=0):
        self.eng, self.sem, self.done, self.turn, self.per, self.n = eng, sem, done, turn, per, 0

    def mark(self, ins):
        ins.then_inc(self.sem, 1)
        self.n += 1
        return ins

    def value(self):
        return self.done + self.n if self.turn is None else self.turn * self.per + (self.done + self.n)

    def wait(self):
        self.eng.wait_ge(self.sem, self.value())

    def link(self, ins):
        self.mark(ins)
        self.wait()

    def close(self):
        assert self.turn is None or self.n == self.per, (self.n, self.per)
        return self.n


def build(nc, I, out):
    B, C, IH, IW = I["x"].shape
    TXT = I["txt"].shape[1]
    D = C
    IMG = IH * IW
    N = IMG + TXT
    TPB = -(-N // P)
    LAST = N - (TPB - 1) * P
    NPAD = TPB * P
    T = B * TPB
    NCH = T * P // BANK
    TPC = BANK // P
    TAPS = 9
    G5 = 5
    PW = IW + 2
    PAIRS = [(0, 1), (3, 4), (6, 7), (2, 5), (8, None)]
    ROWS = 8
    CT = ROWS * IW
    HALF = CT // 2
    CPB = IH // ROWS
    E0, _, F = I["L0_ffn_w1"].shape
    E1 = I["L1_ffn_W1"].shape[0]
    HEADS = 8
    DH = D // HEADS
    assert T * P % BANK == 0 and F == P and D == 64

    def off(tap):
        return (tap // 3) * PW + tap % 3

    cols, at = {}, 0
    for name, n in (("tok_w2", G5 * P), ("a0_q", P), ("a0_k", P), ("a0_v", P), ("a0_o", P), ("f0_g", P),
                    ("f0_w1", E0 * P), ("a1_q", P), ("a1_k", P), ("a1_v", P), ("f1_g", P),
                    ("f1_w1", E1 * P)):
        cols[name] = at
        at += n
    WCOLS = at
    rows, at = {}, 0
    for name, n in (("f0_b1", E0), ("f1_b1", E1), ("tok_b1", 1), ("tok_b3", 1), ("a0_bq", 1), ("a0_bk", 1),
                    ("a0_bv", 1), ("a0_bo", 1), ("f0_gb", 1), ("f1_gb", 1), ("tok_b2", G5), ("f0_b2", E0 // 2),
                    ("f1_b2", E1 // 2)):
        rows[name] = at
        at += n
    NBIAS = at

    with ExitStack() as ctx:
        def sb(name, shape, dt=F32, stack=ctx):
            return stack.enter_context(nc.sbuf_tensor(name, shape, dt))

        def sem(name):
            return ctx.enter_context(nc.semaphore(name))

        bank = [ctx.enter_context(nc.psum_tensor(f"bank{i}", [P, BANK], F32)) for i in range(8)]

        H = sb("H", [P, T, D])
        WS = sb("WS", [P, WCOLS], F32R)
        tok_w1 = sb("tok_w1", [P, G5, D])
        tok_w3 = sb("tok_w3", [P, G5, D])
        f0_w2 = sb("f0_w2", [P, E0, D])
        f1_w2 = sb("f1_w2", [P, E1, D])
        bias = sb("bias", [P, NBIAS])
        gb = sb("gb", [P, 4, D])
        ident = sb("ident", [P, P])
        SEL = sb("SEL", [P, max(E0, E1), D], F32R)
        head_rows = sb("head_rows", [P, HEADS])
        ident_bf = sb("ident_bf", [P, P], BF16)
        mask0 = sb("mask0", [P, TPC, BANK], BF16)
        E_PER = I["L0_attn_edge_index"].shape[1] // P
        edges_f = sb("edges_f", [P, 2, E_PER])
        node = sb("node", [P, BANK], F16)
        row_bias = sb("row_bias", [P, 2, D])
        any_far = sb("any_far", [1, 1], I32)

        stage_done = sem("stage_done")
        stored = sem("stored")
        STAGES = 15

        ln_dve = sem("ln_dve")
        ln_centred = sem("ln_centred")
        ln_squared = sem("ln_squared")
        ln_var = sem("ln_var")
        ln_std = sem("ln_std")
        ln_scaled = sem("ln_scaled")
        ln_gamma = sem("ln_gamma")
        ln_beta = sem("ln_beta")
        ln_added = sem("ln_added")
        ln_pool = sem("ln_pool")

        def W(name, i=0, n=P):
            return WS[:, cols[name] + i * P:cols[name] + i * P + n]

        def bcol(name, i=0, lo=0, hi=P):
            return bias[lo:hi, rows[name] + i:rows[name] + i + 1]

        LOADS = [0]

        def stage_end(e, k):
            e.drain().then_inc(stage_done, 1)
            e.wait_ge(stage_done, 5 * k)

        ctx_i = ExitStack()
        PIX = PW * PW
        UB = 2
        img = [[sb(f"img_{n}{b}", [P, PIX + PW], F32, ctx_i) for b in range(UB)] for n in ("col", "row")]
        img_zeroed = sem("img_zeroed")
        img_loaded = [sem(f"img_loaded{b}") for b in range(UB)]
        img_copied = [sem(f"img_copied{b}") for b in range(UB)]
        ctx_w = ExitStack()
        WF = sb("WF", [P, WCOLS], F32, ctx_w)
        sel_f = sb("sel_f", [P, max(E0, E1), D], F32, ctx_w)
        tok_w2_raw = sb("tok_w2_raw", [P, D * TAPS], F32, ctx_w)
        brow = sb("brow", [P, P], F32, ctx_w)
        wt = sb("wt", [D, 3, P], F32, ctx_w)
        edges = sb("edges", [P, 2, E_PER], I32, ctx_w)
        negative = sb("negative", [P, 2, E_PER], F32, ctx_w)
        e_max = sb("e_max", [P, 1], F32, ctx_w)
        e_top = sb("e_top", [1, 2], F32, ctx_w)
        HOTS = 4
        hot = sb("hot", [P, HOTS, 2, BANK], BF16, ctx_w)
        w_zeroed = sem("w_zeroed")
        edges_loaded = sem("edges_loaded")
        w_loaded = sem("w_loaded")
        edges_cast = sem("edges_cast")
        w_sorted = sem("w_sorted")
        w_rounded = sem("w_rounded")
        ident_set = sem("ident_set")
        tables_turned = sem("tables_turned")
        tables_copied = sem("tables_copied")
        hot_ready = sem("hot_ready")
        hot_used = sem("hot_used")
        counts_zeroed = sem("counts_zeroed")
        mask_thresholded = sem("mask_thresholded")
        sel_set = sem("sel_set")
        heads_set = sem("heads_set")

        def load_image(e, b):
            u = b % UB
            col, row = img[0][u], img[1][u]
            e.dma_start(col[0:D, 0:PIX].rearrange("c (h w) -> c h w", w=PW)[:, 1:IH + 1, 1:IW + 1],
                        I["x"][b]).then_inc(img_loaded[u], 16)
            e.wait_ge(img_loaded[u], (b // UB + 1) * 16)
            e.dma_start(col[D:P, 0:PIX - 1], col[0:D, 1:PIX]).then_inc(img_copied[u], 16)
            e.dma_start(row[0:D, 0:PIX], col[0:D, 0:PIX]).then_inc(img_copied[u], 16)
            e.dma_start(row[D:P, 0:PIX - PW], col[0:D, PW:PIX]).then_inc(img_copied[u], 16)

        def weights_sync(e):
            def load(dst, src, **kw):
                e.dma_start(dst, src, **kw).then_inc(w_loaded, 16)
                LOADS[0] += 1

            e.dma_start(edges[:, :, :], I["L0_attn_edge_index"].rearrange("a (p j) -> p a j", p=P)).then_inc(edges_loaded, 16)
            load(gb[:, 0, :], I["L0_attn_gamma"].partition_broadcast(P))
            load(gb[:, 1, :], I["L0_attn_beta"].partition_broadcast(P))
            load(gb[:, 2, :], I["L0_ffn_gamma"].partition_broadcast(P))
            load(gb[:, 3, :], I["L0_ffn_beta"].partition_broadcast(P))
            load(row_bias[:, 0, :], I["L0_attn_bv"].partition_broadcast(P))
            load(row_bias[:, 1, :], I["L0_attn_bo"].partition_broadcast(P))
            load(f0_w2[:, :, :], I["L0_ffn_w2"].rearrange("e f n -> f e n"))
            load(f1_w2[:, :, :], I["L1_ffn_W2"].rearrange("e f n -> f e n"))
            for i, name in enumerate("qkv"):
                for m in (0, D):
                    load(wt[0:D, i, m:m + D], I["L1_attn_W" + name])
            e.wait_ge(w_zeroed, 6 + B)
            for lo in (0, D):
                half = WF[lo:lo + D, :]
                load(half[:, cols["f0_w1"]:cols["f0_w1"] + E0 * P].rearrange("k (e m) -> k e m", e=E0),
                     I["L0_ffn_w1"].rearrange("e k m -> k e m"))
                load(half[:, cols["f1_w1"]:cols["f1_w1"] + E1 * P].rearrange("k (e m) -> k e m", e=E1),
                     I["L1_ffn_W1"].rearrange("e k m -> k e m"))
                load(half[:, cols["f0_g"]:cols["f0_g"] + E0], I["L0_ffn_gate_w"])
                load(half[:, cols["f1_g"]:cols["f1_g"] + E1], I["L1_ffn_gate_w"])
                for name in "qkvo":
                    for m in (0, D):
                        c = cols["a0_" + name] + m
                        load(half[:, c:c + D], I["L0_attn_W" + name])
                load(tok_w2_raw[lo:lo + D, :], I["L0_tok_W2"])
            for name, src, n in (("f0_b2", "L0_ffn_b2", E0), ("f1_b2", "L1_ffn_b2", E1)):
                load(brow[rows[name]:rows[name] + n // 2, :], I[src].rearrange("(p a) d -> p (a d)", a=2))
            w1_taps = I["L0_tok_W1"].rearrange("(c t) n -> t c n", t=TAPS)
            w3_taps = I["L0_tok_W3"].rearrange("(c t) n -> t c n", t=TAPS)
            b2_taps = I["L0_tok_b2"].rearrange("(o c t) -> t o c", t=TAPS, o=1)
            for g, pair in enumerate(PAIRS):
                for h, tap in enumerate(pair):
                    if tap is not None:
                        load(tok_w1[h * D:(h + 1) * D, g, :], w1_taps[tap])
                        load(tok_w3[h * D:(h + 1) * D, g, :], w3_taps[tap])
                        r = rows["tok_b2"] + g
                        load(brow[r:r + 1, h * D:(h + 1) * D], b2_taps[tap], allow_slow_non_contiguous=True)
            load(brow[rows["f0_b1"]:rows["f0_b1"] + E0, :], I["L0_ffn_b1"])
            load(brow[rows["f1_b1"]:rows["f1_b1"] + E1, :], I["L1_ffn_b1"])
            for name, src in (("tok_b1", "L0_tok_b1"), ("tok_b3", "L0_tok_b3"), ("a0_bq", "L0_attn_bq"),
                              ("a0_bk", "L0_attn_bk"), ("a0_bv", "L0_attn_bv"), ("a0_bo", "L0_attn_bo")):
                for m in (0, D):
                    load(brow[rows[name]:rows[name] + 1, m:m + D], I[src].rearrange("(o n) -> o n", o=1))
            load(brow[rows["f0_gb"]:rows["f0_gb"] + 1, 0:E0], I["L0_ffn_gate_b"].rearrange("(o n) -> o n", o=1))
            load(brow[rows["f1_gb"]:rows["f1_gb"] + 1, 0:E1], I["L1_ffn_gate_b"].rearrange("(o n) -> o n", o=1))
            for b in range(B):
                load(H[IMG % P:IMG % P + TXT, b * TPB + TPB - 1, :], I["txt"][b])
            e.wait_ge(img_zeroed, 2 * UB)
            for b in range(UB):
                load_image(e, b)
            e.wait_ge(w_loaded, 16 * LOADS[0])

        def weights_gpsimd(e):
            e.iota(node[:, :], pattern=[[1, BANK]], base=0, channel_multiplier=0,
                   allow_small_or_imprecise_dtypes=True).then_inc(ident_set, 1)
            e.memset(brow[:, :], 0.0).then_inc(w_zeroed, 1)
            e.memset(tok_w1[:, :, :], 0.0).then_inc(w_zeroed, 1)
            e.memset(tok_w3[:, :, :], 0.0).then_inc(w_zeroed, 1)
            for c, n in ((cols["f0_g"], P), (cols["f1_g"], P), (cols["tok_w2"] + (G5 - 1) * P + D, D)):
                e.memset(WF[:, c:c + n], 0.0).then_inc(w_zeroed, 1)
            for b in range(B):
                e.memset(H[:, (b + 1) * TPB - 1, :], 0.0).then_inc(w_zeroed, 1)
            e.memset(ident[:, :], 0.0).then_inc(ident_set, 1)
            e.wait_ge(ident_set, 2)
            e.affine_select(out=ident[:, :], in_=ident[:, :], compare_op=ALU.not_equal, fill=1.0, base=0,
                            pattern=[[-1, P]], channel_multiplier=1).then_inc(ident_set, 1)
            e.wait_ge(ident_set, 3)
            e.tensor_copy(ident_bf[:, :], ident[:, :]).then_inc(ident_set, 1)
            for which in range(2):
                for u in range(UB):
                    e.memset(img[which][u][:, :], 0.0).then_inc(img_zeroed, 1)
            for s in started():
                e.sem_inc(s, START)
            e.memset(sel_f[:, :, :], 0.0).then_inc(sel_set, 1)
            for k in range(2):
                e.wait_ge(sel_set, k + 1)
                e.affine_select(out=sel_f[:, :, :], in_=sel_f[:, :, :], compare_op=ALU.not_equal, fill=1.0,
                                base=-32 * k, pattern=[[-1, max(E0, E1)], [0, D]],
                                channel_multiplier=1).then_inc(sel_set, 1)
            e.memset(head_rows[:, :], 0.0).then_inc(heads_set, 1)
            for k, r in enumerate(range(2 * DH)):
                e.wait_ge(heads_set, k + 1)
                e.affine_select(out=head_rows[:, :], in_=head_rows[:, :], compare_op=ALU.not_equal, fill=1.0,
                                base=-(r // DH) * D - r % DH, pattern=[[-DH, HEADS]],
                                channel_multiplier=1).then_inc(heads_set, 1)
            e.wait_ge(heads_set, 2 * DH + 1)
            e.wait_ge(w_rounded, 1)
            e.tensor_tensor(WS[D:P, :], WF[D:P, :], WS[D:P, :].bitcast(F32), ALU.subtract).then_inc(w_rounded, 1)
            e.wait_ge(w_rounded, 3)
            for t in range(TPC):
                e.wait_ge(mask_thresholded, t + 1)
                e.affine_select(out=mask0[:, t, :], in_=mask0[:, t, :], compare_op=ALU.not_equal, fill=0.0,
                                base=t * P, pattern=[[-1, BANK]], channel_multiplier=1).then_inc(ident_set, 1)

        def weights_scalar(e):
            e.wait_ge(w_loaded, 16 * LOADS[0])
            e.wait_ge(tables_turned, 2)
            for i, name in enumerate(("a1_q", "a1_k", "a1_v")):
                for m in (0, D):
                    c = cols[name] + m
                    e.activation(WF[:, c:c + D], bank[5][:, i * D:(i + 1) * D], ACT.Copy).then_inc(w_sorted, 1)
            for g, pair in enumerate(PAIRS):
                for h, tap in enumerate(pair):
                    if tap is not None:
                        c = cols["tok_w2"] + g * P + h * D
                        e.activation(WF[:, c:c + D], tok_w2_raw[:, :].rearrange("p (c t) -> p t c", t=TAPS)[:, tap, :],
                                     ACT.Copy).then_inc(w_sorted, 1)
            e.wait_ge(w_sorted, 6 + TAPS)
            e.activation(WS[:, :], WF[:, :], ACT.Copy).then_inc(w_rounded, 1)
            e.wait_ge(sel_set, 3)
            e.activation(SEL[:, :, :], sel_f[:, :, :], ACT.Copy).then_inc(w_rounded, 1)
            e.wait_ge(tables_turned, 1)
            e.activation(bias[:, :], bank[4][:, 0:NBIAS], ACT.Copy).then_inc(tables_copied, 1)

        def weights_vector(e):
            for t in range(TPC):
                e.memset(bank[t][:, :], 0.0).then_inc(counts_zeroed, 1)
            e.wait_ge(edges_loaded, 16)
            ids = Chain(e, edges_cast)
            ids.link(e.tensor_copy(edges_f[:, :, :], edges[:, :, :]))
            ids.link(e.tensor_scalar(negative[:, :, :], edges_f[:, :, :], 0.0, float(N), ALU.is_lt, ALU.mult))
            ids.link(e.tensor_tensor(edges_f[:, :, :], edges_f[:, :, :], negative[:, :, :], ALU.add))
            ids.link(e.tensor_reduce(e_max[:, :], edges_f[:, :, :].rearrange("p a j -> p (a j)"), X, ALU.max))
            e.wait_ge(ident_set, 1)
            with e.Fori(0, E_PER // HOTS) as i:
                for u in range(HOTS):
                    e.wait_ge(hot_used, i * HOTS + (u + 1))
                    for a in range(2):
                        e.tensor_scalar(hot[:, u, a, :], node[:, :],
                                        edges_f[:, a, bass.ds(i * HOTS + u, 1)], None,
                                        ALU.is_equal).then_inc(hot_ready, 1)
            for t in range(TPC):
                e.wait_ge(hot_used, HOTS + E_PER)
                e.tensor_scalar(mask0[:, t, :], bank[t][:, :], 0.5, MASKED, ALU.is_lt,
                                ALU.mult).then_inc(mask_thresholded, 1)
            top = Chain(e, edges_cast, 4)
            e.wait_ge(tables_turned, 3)
            top.link(e.tensor_reduce(e_top[:, 0:1], bank[6][0:1, 0:P], X, ALU.max))
            top.link(e.tensor_scalar(e_top[:, 1:2], e_top[:, 0:1], float(BANK), None, ALU.is_ge))
            top.link(e.tensor_copy(any_far[:, :], e_top[:, 1:2]))

        def weights_tensor(e):
            e.sem_inc(hot_used, HOTS)
            e.wait_ge(counts_zeroed, TPC)
            def count(first, last):
                with e.Fori(first, last) as i:
                    for u in range(HOTS):
                        e.wait_ge(hot_ready, i * (2 * HOTS) + 2 * (u + 1))
                        for t in range(TPC):
                            mm = e.matmul(bank[t][:, :], hot[:, u, 0, t * P:(t + 1) * P], hot[:, u, 1, :],
                                          start=False, stop=False, skip_group_check=True)
                        mm.then_inc(hot_used, 1)

            turn_at = E_PER // HOTS * 3 // 4
            count(0, turn_at)
            e.wait_ge(ident_set, 3)
            e.wait_ge(w_loaded, 16 * LOADS[0])
            e.transpose(bank[4][:, 0:P], brow[:, :], ident[:, :]).then_inc(tables_turned, 1)
            for i in range(3):
                last = e.transpose(bank[5][:, i * D:(i + 1) * D], wt[:, i, :], ident[0:D, 0:D])
            last.then_inc(tables_turned, 1)
            e.wait_ge(edges_cast, 4)
            e.transpose(bank[6][0:1, 0:P], e_max[:, :], ident[:, :]).then_inc(tables_turned, 1)
            count(turn_at, E_PER // HOTS)

        ctx_w.close()

        ctx_t = ExitStack()
        tokT = [sb(f"tokT{b}", [P, NPAD], F32, ctx_t) for b in range(2)]
        h1 = [sb(f"h1_{b}", [P, CT], F32, ctx_t) for b in range(2)]
        h1_hi = [sb(f"h1_hi{b}", [P, CT], F32R, ctx_t) for b in range(2)]
        h1_lo = [sb(f"h1_lo{b}", [P, CT], F32R, ctx_t) for b in range(2)]
        NG = 3
        gate = [sb(f"gate{b}", [P, CT], F32, ctx_t) for b in range(NG)]
        gated = [sb(f"gated{b}", [P, G5, CT], F32, ctx_t) for b in range(2)]
        GROUP = [(0, off(0)), (0, off(3)), (0, off(6)), (1, off(2)), (0, off(8))]
        UC = UB * CPB
        TURNS = B // UB
        TGROUPS = -(-TPB // TPC)
        t_h = sem("t_h")
        t_relu = sem("t_relu")
        t_split = sem("t_split")
        t_halves = sem("t_halves")
        t_logit = sem("t_logit")
        t_gate = sem("t_gate")
        t_gated = sem("t_gated")
        t_out = sem("t_out")
        t_stored = sem("t_stored")
        t_turned = sem("t_turned")
        t_inH = sem("t_inH")

        def tok_sync(e):
            for b in range(UB, B):
                e.wait_ge(t_gated, (b - UB + 1) * CPB * G5 + START)
                load_image(e, b)

        def taps(g, u, j, lo=0, hi=ROWS):
            which, o = GROUP[g]
            o += (j * ROWS + lo) * PW
            n = hi - lo
            return img[which][u][:, o:o + n * PW].rearrange("p (h w) -> p h w", w=PW)[:, :, 0:IW]

        def tok_gpsimd(e):
            for u in range(UB):
                e.memset(tokT[u][:, :], 0.0).then_inc(img_zeroed, 1)

        def tok_tensor(e):
            with e.Fori(0, TURNS) as i:
                def at(n, per=1):
                    return i * (UC * per) + n

                def first_product(c):
                    u, j = divmod(c, CPB)
                    if j == 0:
                        e.wait_ge(img_copied[u], i * 48 + 48)
                    e.wait_ge(t_relu, at(c + 1))
                    for g in range(G5):
                        for h in range(2):
                            mm = e.matmul(bank[c % 2][h * D:(h + 1) * D, 0:HALF], tok_w1[:, g, :],
                                          taps(g, u, j, h * ROWS // 2, (h + 1) * ROWS // 2),
                                          start=(g == 0), stop=(g == G5 - 1))
                    mm.then_inc(t_h, 1)

                def gate_logits(c):
                    if c == 0:
                        e.wait_ge(t_inH, i * (UB * TGROUPS) + 2)
                    e.wait_ge(t_split, at(c + 1) + START)
                    for g in range(G5):
                        k = c * G5 + g
                        b = bank[2 + k % 4]
                        e.wait_ge(t_gate, i * (UC * G5) + (k + 1))
                        e.matmul(b[:, 0:CT], W("tok_w2", g), h1_hi[c % 2][:, :], start=True, stop=False)
                        e.matmul(b[:, 0:CT], W("tok_w2", g), h1_lo[c % 2][:, :], start=False, stop=True).then_inc(t_logit, 1)

                def last_product(c):
                    e.wait_ge(t_gated, i * (UC * G5) + (c + 1) * G5 + START)
                    e.wait_ge(t_stored, at(c + 1))
                    for g in range(G5):
                        for h in range(2):
                            mm = e.matmul(bank[6 + c % 2][h * D:(h + 1) * D, 0:HALF], tok_w3[:, g, :],
                                          gated[c % 2][:, g, h * HALF:(h + 1) * HALF],
                                          start=(g == 0), stop=(g == G5 - 1))
                    mm.then_inc(t_out, 1)

                first_product(0)
                for c in range(UC):
                    if c + 1 < UC:
                        first_product(c + 1)
                    gate_logits(c)
                    if c >= 1:
                        last_product(c - 1)
                last_product(UC - 1)
                for u in range(UB):
                    for k in range(0, TPB, TPC):
                        r = u * TGROUPS + k // TPC
                        if r == 0:
                            e.wait_ge(t_stored, at(UC + 2))
                            e.wait_ge(t_gate, i * (UC * G5) + (UC * G5 + 4))
                        e.wait_ge(t_inH, i * (UB * TGROUPS) + (r + 1))
                        for t in range(k, min(k + TPC, TPB)):
                            mm = e.transpose(bank[2 + r % 2][:, (t - k) * P:(t - k + 1) * P],
                                             tokT[u][:, t * P:(t + 1) * P], ident[:, :])
                        mm.then_inc(t_turned, 1)

        def tok_scalar(e):
            e.sem_inc(t_relu, 2)
            e.sem_inc(t_gate, 4)
            with e.Fori(0, TURNS) as i:
                for c in range(UC + 1):
                    if c < UC:
                        e.wait_ge(t_h, i * UC + (c + 1))
                        e.wait_ge(t_split, i * UC + max(c - 1, 0) + START)
                        for h in range(2):
                            for m in range(2):
                                a = e.activation(h1[c % 2][m * D:(m + 1) * D, h * HALF:(h + 1) * HALF],
                                                 bank[c % 2][h * D:(h + 1) * D, 0:HALF], ACT.Relu,
                                                 bias=bcol("tok_b1", 0, h * D, (h + 1) * D))
                        a.then_inc(t_relu, 1)
                    if c >= 1:
                        for g in range(G5):
                            k = (c - 1) * G5 + g
                            e.wait_ge(t_logit, i * (UC * G5) + (k + 1 + START))
                            e.wait_ge(t_gated, i * (UC * G5) + max(k + 1 - NG, 0) + START)
                            e.activation(gate[k % NG][:, :], bank[2 + k % 4][:, 0:CT], ACT.Sigmoid,
                                         bias=bcol("tok_b2", g)).then_inc(t_gate, 1)

        def tok_vector(e):
            e.sem_inc(t_stored, 2)
            e.sem_inc(t_inH, 2)
            e.wait_ge(img_zeroed, 3 * UB)
            with e.Fori(0, TURNS) as i:
                def split(c):
                    e.wait_ge(t_relu, i * UC + (c + 3))
                    e.wait_ge(t_logit, i * (UC * G5) + max(c - 1, 0) * G5 + START)
                    hi = h1_hi[c % 2]
                    e.tensor_copy(hi[:, :], h1[c % 2][:, :]).then_inc(t_halves, 1)
                    e.wait_ge(t_halves, i * UC + (c + 1))
                    e.tensor_tensor(h1_lo[c % 2][:, :], h1[c % 2][:, :], hi[:, :].bitcast(F32),
                                    ALU.subtract).then_inc(t_split, 1)

                def store(c):
                    u, j = divmod(c, CPB)
                    e.wait_ge(t_out, i * UC + (c + 1 + START))
                    if j == 0:
                        e.wait_ge(t_turned, i * (UB * TGROUPS) + START)
                    for h in range(2):
                        o = j * CT + h * HALF
                        a = e.tensor_scalar(tokT[u][0:D, o:o + HALF], bank[6 + c % 2][h * D:(h + 1) * D, 0:HALF],
                                            bcol("tok_b3", 0, h * D, (h + 1) * D), None, ALU.add)
                    a.then_inc(t_stored, 1)

                split(0)
                for c in range(UC):
                    u, j = divmod(c, CPB)
                    if c + 1 < UC:
                        split(c + 1)
                    e.wait_ge(t_out, i * UC + max(c - 1, 0) + START)
                    for g in range(G5):
                        e.wait_ge(t_gate, i * (UC * G5) + (c * G5 + g + 1 + 4))
                        e.tensor_tensor(gated[c % 2][:, g, :].rearrange("p (h w) -> p h w", w=IW),
                                        gate[(c * G5 + g) % NG][:, :].rearrange("p (h w) -> p h w", w=IW),
                                        taps(g, u, j), ALU.mult).then_inc(t_gated, 1)
                    if c >= 1:
                        store(c - 1)
                store(UC - 1)
                for u in range(UB):
                    for k in range(0, TPB, TPC):
                        r = u * TGROUPS + k // TPC
                        e.wait_ge(t_turned, i * (UB * TGROUPS) + (r + 1 + START))
                        whole = k + TPC < TPB
                        n, hi = (TPC, P) if whole else (1, IMG % P)
                        e.tensor_copy(H[0:hi, bass.ds(i * (UB * TPB) + (u * TPB + k), n), :],
                                      bank[2 + r % 2][0:hi, :].rearrange("p (t c) -> p t c", c=P)[:, 0:n, 0:D]
                                      ).then_inc(t_inH, 1)

        ctx_t.close()
        ctx_i.close()
        assert TPB % TPC == 1

        Y = sb("Y", [P, T, D])
        stat = sb("stat", [P, 4, T])
        ctx_n = ExitStack()
        squares = [sb(f"squares{j}", [P, TPB, D], F32, ctx_n) for j in range(2)]
        ctx_n.close()
        LN_LINKS = B + 1 + B + 1
        MEANS_AT = B + 1
        OWN = B - 1
        POOL_BEFORE = (0, 2, 6, 8)

        def rows_of(t, b):
            return t[:, b * TPB:(b + 1) * TPB, :]

        def over_d(row, b):
            return stat[:, row, b * TPB:(b + 1) * TPB].unsqueeze(2).broadcast_to([P, TPB, D])

        def over_t(row):
            return gb[:, row, :].unsqueeze(1).broadcast_to([P, TPB, D])

        def norm_vector(e, k, src, affine):
            ch = Chain(e, ln_dve, k * LN_LINKS)
            for b in range(B):
                ch.mark(e.tensor_reduce(stat[:, 0, b * TPB:(b + 1) * TPB], rows_of(src, b), X, ALU.add))
            ch.wait()
            ch.link(e.tensor_scalar(stat[:, 1, :], stat[:, 0, :], 1.0 / D, None, ALU.mult))
            for b in range(OWN):
                e.tensor_tensor(rows_of(Y, b), rows_of(src, b), over_d(1, b), ALU.subtract).then_inc(ln_centred, 1)
            for b in range(B):
                e.wait_ge(ln_squared, k * B + b + 1)
                ch.mark(e.tensor_reduce(stat[:, 2, b * TPB:(b + 1) * TPB], squares[b % 2][:, :, :], X, ALU.add))
            ch.wait()
            e.tensor_scalar(stat[:, 3, :], stat[:, 2, :], 1.0 / D, LN_EPS, ALU.mult, ALU.add).then_inc(ln_var, 1)
            e.wait_ge(ln_std, k + 1)
            ch.link(e.reciprocal(stat[:, 3, :], stat[:, 3, :]))
            for b in range(OWN):
                e.tensor_tensor(rows_of(Y, b), rows_of(Y, b), over_d(3, b), ALU.mult).then_inc(ln_scaled, 1)
            if affine is not None:
                for b in range(OWN):
                    e.wait_ge(ln_scaled, k * OWN + b + 1)
                    e.tensor_tensor(rows_of(Y, b), rows_of(Y, b), over_t(affine), ALU.mult).then_inc(ln_gamma, 1)
                for b in range(OWN):
                    e.wait_ge(ln_gamma, b + 1)
                    e.tensor_tensor(rows_of(H, b), rows_of(H, b), rows_of(Y, b), ALU.add).then_inc(ln_added, 1)

        def norm_gpsimd(e, k, src, affine):
            b = B - 1
            ch = Chain(e, ln_pool, POOL_BEFORE[k])
            e.wait_ge(ln_dve, k * LN_LINKS + MEANS_AT)
            ch.link(e.tensor_tensor(rows_of(Y, b), rows_of(src, b), over_d(1, b), ALU.subtract))
            e.wait_ge(ln_dve, k * LN_LINKS + LN_LINKS)
            ch.link(e.tensor_tensor(rows_of(Y, b), rows_of(Y, b), over_d(3, b), ALU.mult))
            if affine is not None:
                ch.link(e.tensor_tensor(rows_of(Y, b), rows_of(Y, b), over_t(affine), ALU.mult))
                ch.link(e.tensor_tensor(rows_of(H, b), rows_of(H, b), rows_of(Y, b), ALU.add))

        def norm_scalar(e, k):
            for b in range(B):
                if b < OWN:
                    e.wait_ge(ln_centred, k * OWN + b + 1)
                else:
                    e.wait_ge(ln_pool, POOL_BEFORE[k] + 1)
                if b >= 2:
                    e.wait_ge(ln_dve, k * LN_LINKS + MEANS_AT + b - 1)
                e.activation(squares[b % 2][:, :, :], rows_of(Y, b), ACT.Square).then_inc(ln_squared, 1)
            e.wait_ge(ln_var, k + 1)
            e.activation(stat[:, 3, :], stat[:, 3, :], ACT.Sqrt).then_inc(ln_std, 1)

        DUPS = 2
        CHUNKS_TURNED = [START]
        t_sems = {n: sem("x_" + n) for n in ("doubled", "turned", "high", "low")}

        def turner(name, stack, banks, chunks):
            CHUNKS_TURNED[0] += chunks
            return {"dup": [sb(f"{name}_dup{j}", [P, TPC, 2, D], F32, stack) for j in range(DUPS)],
                    "banks": banks, "before": CHUNKS_TURNED[0] - chunks, **t_sems}

        def turned_by(tr, done, n):
            return done + (tr["before"] + n)

        def double_chunk(e, tr, done, k, tokens, n):
            e.wait_ge(tr["turned"], turned_by(tr, done, max(k + 1 - DUPS, 0)))
            e.activation(tr["dup"][k % DUPS][:, 0:n, :, :], tokens.unsqueeze(2).broadcast_to([P, n, 2, D]),
                         ACT.Copy).then_inc(tr["doubled"], 1)

        def turn_chunk(e, tr, done, k, n):
            nb = len(tr["banks"])
            e.wait_ge(tr["low"], turned_by(tr, done, max(k + 1 - nb, 0)))
            e.wait_ge(tr["doubled"], turned_by(tr, done, k + 1))
            for t in range(n):
                mm = e.transpose(tr["banks"][k % nb][:, t * P:(t + 1) * P],
                                 tr["dup"][k % DUPS][:, t, :, :].rearrange("p a d -> p (a d)"), ident[:, :])
            mm.then_inc(tr["turned"], 1)

        def high_chunk(e, tr, done, k, n, hi):
            e.wait_ge(tr["turned"], turned_by(tr, done, k + 1))
            e.activation(hi, tr["banks"][k % len(tr["banks"])][:, 0:n * P], ACT.Copy).then_inc(tr["high"], 1)

        def low_chunk(e, tr, done, k, n, hi, lo):
            e.wait_ge(tr["high"], turned_by(tr, done, k + 1))
            e.tensor_tensor(lo, tr["banks"][k % len(tr["banks"])][:, 0:n * P], hi.bitcast(F32),
                            ALU.subtract).then_inc(tr["low"], 1)

        def product(e, out, weights, hi, lo):
            e.matmul(out, weights, hi, start=True, stop=False)
            return e.matmul(out, weights, lo, start=False, stop=True)

        g_names = ("logit lt_biased lt_turned stored place_set dve act exp ext_zeroed ext_ready w_turned w_ready h_ready "
                   "wb_ready wb_copied act_done weighted used summed y_turned y_added y_half x_doubled x_turned x_high x_low "
                   "n0_dve n1_dve n0_var n1_var n0_std n1_std n_beta")
        G = {n: sem("ffn_" + n) for n in g_names.split()}
        GATE_LINKS = 19

        def ffn(name, E, w2, kind, into, k, C0, N0, P0, L0, norms):
            st = ExitStack()
            XH = [sb(f"{name}_XH{j}", [P, BANK], F32R, st) for j in range(2)]
            XL = [sb(f"{name}_XL{j}", [P, BANK], F32R, st) for j in range(2)]
            x_dup = sb(f"{name}_xdup", [P, TPC, 2, D], F32, st)
            LG = sb(f"{name}_LG", [P, T, E], F32, st)
            WH = sb(f"{name}_WH", [P, T, E], F32R, st)
            keep = ExitStack()
            tr = turner(name, keep, [bank[0], bank[1]], NCH)
            LT = [sb(f"{name}_LT{j}", [P, BANK], F32, keep) for j in range(2)]
            g_logit, g_biased, g_turned, g_stored = G["logit"], G["lt_biased"], G["lt_turned"], G["stored"]
            keep.close()
            keep = ExitStack()
            place = sb(f"{name}_place", [P, E], F32, keep)
            oh1 = sb(f"{name}_oh1", [P, T, E], F32, keep)
            oh2 = sb(f"{name}_oh2", [P, T, E], F32, keep)
            oh3 = sb(f"{name}_oh3", [P, T, E], F32, keep)
            red = sb(f"{name}_red", [P, 6, T], F32, keep)
            place_set, g_dve, g_act, g_exp = G["place_set"], G["dve"], G["act"], G["exp"]
            keep.close()
            RING = 4
            TR = 3
            PAIRS_E = E // 2
            ext = [sb(f"{name}_ext{j}", [P, TPC, P], F32, st) for j in range(2)]
            GS = [sb(f"{name}_GS{j}", [P, BANK], F32R, st) for j in range(2)]
            hid = [sb(f"{name}_hid{j}", [P, BANK], F32, st) for j in range(RING)]
            term = [sb(f"{name}_term{j}", [P, BANK], F32, st) for j in range(TR)]
            wb = [sb(f"{name}_wb{j}", [P, BANK], F32, st) for j in range(2)]
            total = [sb(f"{name}_total{j}", [P, BANK], F32, st) for j in range(2)]
            cs = [sb(f"{name}_cs{j}", [P, 4, TPC], F32, st) for j in range(2)]
            csq = sb(f"{name}_csq", [P, TPC, D], F32, st)
            copier_is_vector = kind == "gelu"
            (ext_zeroed, ext_ready, w_turned, w_ready, h_ready, wb_ready, wb_copied, act_done, weighted, used, summed,
             y_turned, y_added, y_half, x_doubled, x_turned, x_high, x_low) = (G[x] for x in (
                 "ext_zeroed ext_ready w_turned w_ready h_ready wb_ready wb_copied act_done weighted used summed y_turned "
                 "y_added y_half x_doubled x_turned x_high x_low").split())
            st.close()
            func = ACT.Relu if kind == "relu" else ACT.Gelu

            def tiles(t, c, n=TPC):
                return t[:, bass.ds(c * TPC, n), :] if not isinstance(c, int) else t[:, c * TPC:c * TPC + n, :]

            def pipeline(e, first, second, third):
                first(0, 0)
                first(1, 1)
                second(0, 0)
                with e.Fori(0, (NCH - 3) // 2) as i:
                    for r in range(2):
                        first(i * 2 + (r + 2), r)
                        second(i * 2 + (r + 1), 1 - r)
                        third(i * 2 + r, r)
                first(NCH - 1, (NCH - 1) % 2)
                for c in range(NCH - 2, NCH):
                    second(c, c % 2)
                    third(c - 1, (c - 1) % 2)
                third(NCH - 1, (NCH - 1) % 2)

            def place_of(c, par):
                return (0, c) if isinstance(c, int) and c < 2 else (c - (par + 2), par + 2)

            def used_before(c):
                return not isinstance(c, int) or c >= 2

            def a_tensor(e):
                def turn(c, par):
                    turn_chunk(e, tr, *place_of(c, par), TPC)

                def logits(c, par):
                    if used_before(c):
                        e.wait_ge(g_biased, c + (C0 - 1 + START))
                    e.wait_ge(tr["low"], c + (tr["before"] + 1))
                    product(e, bank[3 + par][:, :], W(name + "_g"), XH[par][:, :], XL[par][:, :]).then_inc(g_logit, 1)

                def back(c, par):
                    if used_before(c):
                        e.wait_ge(g_stored, c + (C0 - 1 + START))
                    e.wait_ge(g_biased, c + (C0 + 1 + START))
                    for t in range(TPC):
                        mm = e.transpose(bank[5 + par][:, t * P:(t + 1) * P], LT[par][:, t * P:(t + 1) * P], ident[:, :])
                    mm.then_inc(g_turned, 1)

                pipeline(e, turn, logits, back)

            def a_scalar(e):
                def double(c, par):
                    double_chunk(e, tr, *place_of(c, par), tiles(Y, c), TPC)

                def tokens(c, par):
                    if used_before(c):
                        e.wait_ge(g_logit, c + (C0 - 1 + START))
                    high_chunk(e, tr, *place_of(c, par), TPC, XH[par][:, :])
                    if not isinstance(c, int) or c + 1 < NCH:
                        double(c + 1, 1 - par)

                def add_bias(c, par):
                    if used_before(c):
                        e.wait_ge(g_turned, c + (C0 - 1 + START))
                    e.wait_ge(g_logit, c + (C0 + 1 + START))
                    e.activation(LT[par][:, :], bank[3 + par][:, :], ACT.Identity,
                                 bias=bcol(name + "_gb")).then_inc(g_biased, 1)

                double(0, 0)
                pipeline(e, tokens, add_bias, lambda c, par: None)

            def a_vector(e):
                def low(c, par):
                    low_chunk(e, tr, *place_of(c, par), TPC, XH[par][:, :], XL[par][:, :])

                def store(c, par):
                    e.wait_ge(g_turned, c + (C0 + 1 + START))
                    e.tensor_copy(tiles(LG, c), bank[5 + par][:, :].rearrange("p (t c) -> p t c", c=P)[:, :, 0:E]
                                  ).then_inc(g_stored, 1)

                pipeline(e, low, lambda c, par: None, store)

            def over_e(v):
                return v.unsqueeze(2).broadcast_to([P, T, E])

            def b_gpsimd(e):
                e.iota(place[:, :], pattern=[[1, E]], base=-99, channel_multiplier=0,
                       allow_small_or_imprecise_dtypes=True).then_inc(place_set, 1)

            def b_vector(e):
                ch = Chain(e, g_dve, L0)
                L, top, pos, ex = LG[:, :, :], red[:, 0, :], red[:, 1, :], red[:, 2, :]
                places = place[:, :].unsqueeze(1).broadcast_to([P, T, E])
                e.wait_ge(place_set, k + 1)
                if kind == "gelu":
                    ch.link(e.tensor_reduce(top, L, X, ALU.max))
                    e.tensor_tensor(L, L, over_e(top), ALU.subtract).then_inc(g_exp, 1)
                    e.wait_ge(g_act, k + 1)
                    ch.link(e.tensor_reduce(top, L, X, ALU.add))
                    ch.link(e.reciprocal(top, top))
                    ch.link(e.tensor_tensor(L, L, over_e(top), ALU.mult))

                def best(oh, values, top):
                    ch.link(e.tensor_reduce(top, values, X, ALU.max))
                    ch.link(e.tensor_tensor(oh, values, over_e(top), ALU.is_equal))
                    ch.link(e.tensor_tensor(oh, oh, places, ALU.mult))
                    ch.link(e.tensor_reduce(pos, oh, X, ALU.min))
                    ch.link(e.tensor_tensor(oh, places, over_e(pos), ALU.is_equal))

                first, second, rest = oh1[:, :, :], oh2[:, :, :], oh3[:, :, :]
                best(first, L, top)
                ch.link(e.scalar_tensor_tensor(out=rest, in0=first, scalar=MASKED, in1=L, op0=ALU.mult, op1=ALU.add))
                best(second, rest, red[:, 3, :])
                if kind == "gelu":
                    ch.link(e.tensor_tensor(first, first, second, ALU.add))
                    ch.link(e.tensor_tensor(L, L, first, ALU.mult))
                else:
                    e.tensor_tensor(ex, red[:, 3, :], top, ALU.subtract).then_inc(g_exp, 1)
                    e.wait_ge(g_act, k + 1)
                    ch.link(e.tensor_scalar(red[:, 4, :], ex, 1.0, None, ALU.add))
                    ch.link(e.reciprocal(red[:, 4, :], red[:, 4, :]))
                    ch.link(e.tensor_tensor(red[:, 5, :], ex, red[:, 4, :], ALU.mult))
                    ch.link(e.tensor_tensor(first, first, over_e(red[:, 4, :]), ALU.mult))
                    ch.link(e.tensor_tensor(second, second, over_e(red[:, 5, :]), ALU.mult))
                    ch.link(e.tensor_tensor(L, first, second, ALU.add))
                ch.link(e.tensor_copy(WH[:, :, :], L))
                ch.link(e.tensor_tensor(L, L, WH[:, :, :].bitcast(F32), ALU.subtract))
                assert ch.close() == GATE_LINKS, ch.n

            def b_scalar(e):
                e.wait_ge(g_exp, k + 1)
                v = LG[:, :, :] if kind == "gelu" else red[:, 2, :]
                e.activation(v, v, ACT.Exp).then_inc(g_act, 1)

            def loop_chunks(e, body):
                body(0, 0, 0, False)
                body(1, 1, 1, False)
                with e.Fori(0, (NCH - 3) // 2) as i:
                    body(i * 2 + 2, 0, 2, False)
                    body(i * 2 + 3, 1, 2, False)
                body(NCH - 1, 0, 2, True)

            ADDS = PAIRS_E - 1

            def c_gpsimd(e):
                for j in range(2):
                    e.memset(ext[j][:, :, :], 0.0).then_inc(ext_zeroed, 1)
                e.wait_ge(ext_zeroed, 2 * k + 2)

                def widen(c, par, fresh):
                    if not fresh:
                        e.wait_ge(w_turned, c + (C0 - 1))
                    v = ext[par][:, :, :].rearrange("p t (g x) -> p g t x", g=4)
                    for g in range(4):
                        src = (WH[:, :, :].bitcast(F32), LG[:, :, :])[g % 2]
                        a = e.tensor_copy(v[:, g, :, 0:E], tiles(src, c))
                    a.then_inc(ext_ready, 1)

                def beta(c):
                    h = tiles(H, c)
                    e.tensor_tensor(h, h, gb[:, 3, :].unsqueeze(1).broadcast_to([P, TPC, D]), ALU.add).then_inc(G["n_beta"], 1)

                widen(0, 0, True)

                def body(c, par, past, last):
                    if not last:
                        widen(c + 1, 1 - par, not past)
                    for p in range(1, PAIRS_E):
                        e.wait_ge(weighted, c * PAIRS_E + (P0 + p + 1))
                        e.wait_ge(summed, c * ADDS + (P0 - C0 + p - 1))
                        e.tensor_tensor(total[par][:, :], total[par][:, :], term[p % TR][:, :], ALU.add).then_inc(summed, 1)
                        if p == 2 and norms:
                            beta(c)
                loop_chunks(e, body)

            def c_tensor(e):
                def turn_tokens(c):
                    e.wait_ge(w_ready, c + C0)
                    e.wait_ge(x_doubled, c + (C0 + 1))
                    for t in range(TPC):
                        mm = e.transpose(bank[6][:, t * P:(t + 1) * P],
                                         x_dup[:, t, :, :].rearrange("p a d -> p (a d)"), ident[:, :])
                    mm.then_inc(x_turned, 1)

                def turn_weights(c, par):
                    e.wait_ge(x_low, c + (C0 + 1))
                    e.wait_ge(ext_ready, c + (C0 + 1))
                    for t in range(TPC):
                        mm = e.transpose(bank[6][:, t * P:(t + 1) * P], ext[par][:, t, :], ident[:, :])
                    mm.then_inc(w_turned, 1)

                def hidden(c, par, x):
                    n, r = c * E + x, x % 2
                    if not (isinstance(n, int) and n < 2):
                        e.wait_ge(act_done, n + (N0 - 1))
                    product(e, bank[r][:, :], W(name + "_w1", x), XH[par][:, :], XL[par][:, :]).then_inc(h_ready, 1)

                def spread(c, par, p):
                    m = c * PAIRS_E + p
                    if p == 0:
                        e.wait_ge(w_ready, c + (C0 + 1))
                    if not (isinstance(m, int) and m < 2):
                        e.wait_ge(wb_copied, m + (P0 - 1))
                    e.matmul(bank[2 + p % 2][:, :], SEL[:, 2 * p:2 * p + 2, :].rearrange("k a m -> k (a m)"), GS[par][:, :],
                             start=True, stop=True).then_inc(wb_ready, 1)

                def output(c, x):
                    m = c * PAIRS_E + x // 2
                    if x % 2 == 0 and not (isinstance(m, int) and m < 2):
                        e.wait_ge(weighted, m + (P0 - 1))
                    e.wait_ge(act_done, c * E + (N0 + x + 1))
                    y = bank[4 + (x // 2) % 2]
                    e.matmul(y[(x % 2) * D:(x % 2 + 1) * D, :], w2[:, x, :], hid[x % RING][:, :],
                             start=True, stop=True, skip_group_check=True).then_inc(used, 1)

                def turn_out(c, par):
                    e.wait_ge(y_added, c + C0)
                    e.wait_ge(summed, c * ADDS + (P0 - C0 + ADDS))
                    for t in range(TPC):
                        mm = e.transpose(bank[7][:, t * P:(t + 1) * P], total[par][:, t * P:(t + 1) * P], ident[:, :])
                    mm.then_inc(y_turned, 1)

                turn_tokens(0)
                turn_weights(0, 0)
                hidden(0, 0, 0)
                hidden(0, 0, 1)
                spread(0, 0, 0)

                def body(c, par, past, last):
                    for x in range(E):
                        if x == min(4, E // 2 - 1) and past:
                            turn_out(c - 1, 1 - par)
                        if x == E - 7 and not last:
                            turn_tokens(c + 1)
                        if x == E - 3 and not last:
                            turn_weights(c + 1, 1 - par)
                        if x % 2 == 1 and x + 1 < E:
                            spread(c, par, x // 2 + 1)
                        elif x % 2 == 1 and not last:
                            spread(c + 1, 1 - par, 0)
                        if x + 2 < E:
                            hidden(c, par, x + 2)
                        elif not last:
                            hidden(c + 1, 1 - par, x + 2 - E)
                        output(c, x)
                loop_chunks(e, body)
                turn_out(NCH - 1, (NCH - 1) % 2)

            def copy_spread(e, c, p):
                m = c * PAIRS_E + p
                e.wait_ge(wb_ready, m + (P0 + 1))
                if not isinstance(m, int) or m >= 2:
                    e.wait_ge(weighted, m + (P0 - 1))
                if copier_is_vector:
                    e.tensor_copy(wb[p % 2][:, :], bank[2 + p % 2][:, :]).then_inc(wb_copied, 1)
                else:
                    e.activation(wb[p % 2][:, :], bank[2 + p % 2][:, :], ACT.Copy).then_inc(wb_copied, 1)

            N_LINKS = (9, 7)

            def norm_step(e, c, w, step):
                y, src = tiles(Y, c), tiles((Y, H)[w], c)
                s = cs[w]
                ch = Chain(e, G[f"n{w}_dve"], (0, 2, 3, 5)[step], c, N_LINKS[w])
                if step == 0:
                    ch.link(e.tensor_reduce(s[:, 0, :], src, X, ALU.add))
                    ch.link(e.tensor_scalar(s[:, 1, :], s[:, 0, :], 1.0 / D, None, ALU.mult))
                elif step == 1:
                    ch.link(e.tensor_tensor(y, src, s[:, 1, :].unsqueeze(2).broadcast_to([P, TPC, D]), ALU.subtract))
                elif step == 2:
                    ch.link(e.tensor_tensor(csq[:, :, :], y, y, ALU.mult))
                    ch.link(e.tensor_reduce(s[:, 2, :], csq[:, :, :], X, ALU.add))
                    e.tensor_scalar(s[:, 3, :], s[:, 2, :], 1.0 / D, LN_EPS, ALU.mult, ALU.add).then_inc(G[f"n{w}_var"], 1)
                else:
                    e.wait_ge(G[f"n{w}_std"], c + 1)
                    ch.link(e.reciprocal(s[:, 3, :], s[:, 3, :]))
                    ch.link(e.tensor_tensor(y, y, s[:, 3, :].unsqueeze(2).broadcast_to([P, TPC, D]), ALU.mult))
                    if w == 0:
                        ch.link(e.tensor_tensor(y, y, gb[:, 2, :].unsqueeze(1).broadcast_to([P, TPC, D]), ALU.mult))
                        e.wait_ge(G["n_beta"], c + 1)
                        ch.link(e.tensor_tensor(tiles(H, c), tiles(H, c), y, ALU.add))

            def deviation(e, c, w):
                e.wait_ge(G[f"n{w}_var"], c + 1)
                e.activation(cs[w][:, 3, :], cs[w][:, 3, :], ACT.Sqrt).then_inc(G[f"n{w}_std"], 1)

            def c_scalar(e):
                def weights_in(c, par):
                    e.wait_ge(w_turned, c + (C0 + 1))
                    if not isinstance(c, int) or c >= 2:
                        e.wait_ge(wb_ready, (c - 1) * PAIRS_E + P0)
                    e.activation(GS[par][:, :], bank[6][:, :], ACT.Copy).then_inc(w_ready, 1)

                def double(c):
                    e.wait_ge(x_turned, c + C0)
                    e.activation(x_dup[:, :, :, :], tiles(Y, c).unsqueeze(2).broadcast_to([P, TPC, 2, D]),
                                 ACT.Copy).then_inc(x_doubled, 1)

                def high(c, par):
                    if not isinstance(c, int) or c >= 2:
                        e.wait_ge(h_ready, (c - 1) * E + N0)
                    e.wait_ge(x_turned, c + (C0 + 1))
                    e.activation(XH[par][:, :], bank[6][:, :], ACT.Copy).then_inc(x_high, 1)

                double(0)
                high(0, 0)
                weights_in(0, 0)
                if not copier_is_vector:
                    copy_spread(e, 0, 0)

                def body(c, par, past, last):
                    for x in range(E):
                        n = c * E + x
                        e.wait_ge(h_ready, n + (N0 + 1))
                        if not isinstance(n, int) or n >= RING:
                            e.wait_ge(used, n + (N0 - RING + 1))
                        e.activation(hid[x % RING][:, :], bank[x % 2][:, :], func,
                                     bias=bcol(name + "_b1", x)).then_inc(act_done, 1)
                        if x % 2 == 0 and x >= 2 and not copier_is_vector:
                            copy_spread(e, c, x // 2)
                        if x == 0 and not copier_is_vector and past:
                            copy_spread(e, c, 0)
                        if norms and past == 2 and x == 7:
                            deviation(e, c - 2, 1)
                        if norms and past and x == 13:
                            deviation(e, c - 1, 0)
                        if x == E - 8 and not last:
                            double(c + 1)
                        if x == E - 6 and not last:
                            high(c + 1, 1 - par)
                        if x == E - 2 and not last:
                            weights_in(c + 1, 1 - par)
                loop_chunks(e, body)
                if norms:
                    for c, w in ((NCH - 2, 1), (NCH - 1, 0), (NCH - 1, 1)):
                        deviation(e, c, w)

            def c_vector(e):
                def add_out(c):
                    e.wait_ge(y_turned, c + (C0 + 1))
                    both = bank[7][:, :].rearrange("p (t a d) -> p t a d", a=2, d=D)
                    e.tensor_tensor(tiles(into, c), tiles(into, c), both[:, :, 0, :], ALU.add).then_inc(y_half, 1)
                    e.wait_ge(y_half, c + (C0 + 1))
                    e.tensor_tensor(tiles(into, c), tiles(into, c), both[:, :, 1, :], ALU.add).then_inc(y_added, 1)
                    e.wait_ge(y_added, c + (C0 + 1))

                def low(c, par):
                    e.wait_ge(x_high, c + (C0 + 1))
                    e.tensor_tensor(XL[par][:, :], bank[6][:, :], XH[par][:, :].bitcast(F32),
                                    ALU.subtract).then_inc(x_low, 1)

                low(0, 0)
                if copier_is_vector:
                    copy_spread(e, 0, 0)

                def body(c, par, past, last):
                    for p in range(PAIRS_E):
                        m = c * PAIRS_E + p
                        if p == PAIRS_E - 3 and not last:
                            low(c + 1, 1 - par)
                        e.wait_ge(used, c * E + (N0 + 2 * p + 2))
                        e.wait_ge(wb_copied, m + (P0 + 1))
                        if p == 0:
                            if not isinstance(c, int) or c >= 2:
                                e.wait_ge(y_turned, c + (C0 - 1))
                            dst = total[par]
                        else:
                            dst = term[p % TR]
                            if p >= TR:
                                e.wait_ge(summed, c * ADDS + (P0 - C0 + p - TR))
                            elif past:
                                e.wait_ge(summed, c * ADDS + (P0 - C0))
                        e.scalar_tensor_tensor(out=dst[:, :], in0=bank[4 + p % 2][:, :], scalar=bcol(name + "_b2", p),
                                               in1=wb[p % 2][:, :], op0=ALU.add, op1=ALU.mult).then_inc(weighted, 1)
                        if copier_is_vector and not (last and p == PAIRS_E - 1):
                            copy_spread(e, c, p + 1)
                        if norms and past == 2:
                            for step in SECOND_NORM_AT[p]:
                                norm_step(e, c - 2, 1, step)
                        if p == min(2, PAIRS_E // 2 - 1) and past:
                            add_out(c - 1)
                        if norms and past:
                            for step in FIRST_NORM_AT[p]:
                                norm_step(e, c - 1, 0, step)
                loop_chunks(e, body)
                add_out(NCH - 1)
                if norms:
                    for c, w in ((NCH - 2, 1), (NCH - 1, 0), (NCH - 1, 1)):
                        for step in range(NORM_STEPS):
                            norm_step(e, c, w, step)

            NORM_STEPS = 4
            FIRST_NORM_AT = ((), (), (), (0, 1), (2,), (), (), (3,))
            SECOND_NORM_AT = ((0, 1), (2,), (), (), (), (3,), (), ())

            return {"a_scalar": a_scalar, "a_vector": a_vector, "a_tensor": a_tensor, "b_gpsimd": b_gpsimd,
                    "b_scalar": b_scalar, "b_vector": b_vector, "c_gpsimd": c_gpsimd, "c_scalar": c_scalar,
                    "c_vector": c_vector, "c_tensor": c_tensor}

        SPANS = [(c, min(BANK, NPAD - c)) for c in range(0, NPAD, BANK)]
        NS = len(SPANS)
        LATER = [(c // P, w // P) for c, w in SPANS[1:]]
        NV = len(LATER)
        VB = 2
        VT = VB * NV
        ctx_v = ExitStack()
        v_tr = turner("v0", ctx_v, [bank[0], bank[1]], B * NV)
        vXH = [sb(f"v0_XH{j}", [P, BANK], F32R, ctx_v) for j in range(2)]
        vXL = [sb(f"v0_XL{j}", [P, BANK], F32R, ctx_v) for j in range(2)]
        af = [sb(f"v0_af{j}", [P, BANK], F32, ctx_v) for j in range(2)]
        vVH = [sb(f"v0_VH{j}", [P, BANK], F32R, ctx_v) for j in range(2)]
        vVL = [sb(f"v0_VL{j}", [P, BANK], F32R, ctx_v) for j in range(2)]
        vot = [sb(f"v0_ot{j}", [P, BANK], F32, ctx_v) for j in range(2)]
        ctx_v.close()
        VS = {n: sem("v0_" + n) for n in "v_ready v_biased v_high v_low o_ready o_biased o_turned o_added".split()}

        def later_tokens(i, s):
            t, n = LATER[s % NV]
            return Y[:, bass.ds(i * (VB * TPB) + (s // NV * TPB + t), n), :], n

        def later_tensor(e):
            with e.Fori(0, B // VB) as i:
                for u in range(VT + 3):
                    if u < VT:
                        turn_chunk(e, v_tr, i * VT, u, LATER[u % NV][1])
                    if 1 <= u <= VT:
                        s = u - 1
                        w = LATER[s % NV][1] * P
                        e.wait_ge(v_tr["low"], turned_by(v_tr, i * VT, s + 1))
                        e.wait_ge(VS["v_biased"], i * VT + max(s - 1, 0) + START)
                        product(e, bank[2 + s % 2][:, 0:w], W("a0_v"), vXH[s % 2][:, 0:w], vXL[s % 2][:, 0:w]
                                ).then_inc(VS["v_ready"], 1)
                    if 2 <= u <= VT + 1:
                        s = u - 2
                        w = LATER[s % NV][1] * P
                        e.wait_ge(VS["v_low"], i * VT + (s + 1 + START))
                        e.wait_ge(VS["o_biased"], i * VT + max(s - 1, 0) + START)
                        product(e, bank[4 + s % 2][:, 0:w], W("a0_o"), vVH[s % 2][:, 0:w], vVL[s % 2][:, 0:w]
                                ).then_inc(VS["o_ready"], 1)
                    if u >= 3:
                        s = u - 3
                        e.wait_ge(VS["o_biased"], i * VT + (s + 1 + START))
                        e.wait_ge(VS["o_added"], i * VT + max(s - 1, 0) + START)
                        for t in range(LATER[s % NV][1]):
                            mm = e.transpose(bank[6 + s % 2][:, t * P:(t + 1) * P], vot[s % 2][:, t * P:(t + 1) * P], ident[:, :])
                        mm.then_inc(VS["o_turned"], 1)

        def later_scalar(e):
            with e.Fori(0, B // VB) as i:
                tokens, n = later_tokens(i, 0)
                double_chunk(e, v_tr, i * VT, 0, tokens, n)
                for u in range(VT + 2):
                    if u < VT:
                        n = LATER[u % NV][1]
                        e.wait_ge(VS["v_ready"], i * VT + max(u - 1, 0) + START)
                        high_chunk(e, v_tr, i * VT, u, n, vXH[u % 2][:, 0:n * P])
                    if u + 1 < VT:
                        tokens, n = later_tokens(i, u + 1)
                        double_chunk(e, v_tr, i * VT, u + 1, tokens, n)
                    if 1 <= u <= VT:
                        s = u - 1
                        w = LATER[s % NV][1] * P
                        e.wait_ge(VS["v_ready"], i * VT + (s + 1 + START))
                        e.wait_ge(VS["v_low"], i * VT + max(s - 1, 0) + START)
                        e.activation(af[s % 2][:, 0:w], bank[2 + s % 2][:, 0:w], ACT.Identity,
                                     bias=bcol("a0_bv")).then_inc(VS["v_biased"], 1)
                    if u >= 2:
                        s = u - 2
                        w = LATER[s % NV][1] * P
                        e.wait_ge(VS["o_ready"], i * VT + (s + 1 + START))
                        e.wait_ge(VS["o_turned"], i * VT + max(s - 1, 0) + START)
                        e.activation(vot[s % 2][:, 0:w], bank[4 + s % 2][:, 0:w], ACT.Identity,
                                     bias=bcol("a0_bo")).then_inc(VS["o_biased"], 1)

        def later_vector(e):
            with e.Fori(0, B // VB) as i:
                for u in range(VT + 3):
                    if u < VT:
                        w = LATER[u % NV][1] * P
                        low_chunk(e, v_tr, i * VT, u, w // P, vXH[u % 2][:, 0:w], vXL[u % 2][:, 0:w])
                    if 1 <= u <= VT:
                        s = u - 1
                        w = LATER[s % NV][1] * P
                        e.wait_ge(VS["v_biased"], i * VT + (s + 1 + START))
                        e.wait_ge(VS["o_ready"], i * VT + max(s - 1, 0) + START)
                        e.tensor_copy(vVH[s % 2][:, 0:w], af[s % 2][:, 0:w]).then_inc(VS["v_high"], 1)
                        e.wait_ge(VS["v_high"], i * VT + (s + 1 + START))
                        e.tensor_tensor(vVL[s % 2][:, 0:w], af[s % 2][:, 0:w], vVH[s % 2][:, 0:w].bitcast(F32),
                                        ALU.subtract).then_inc(VS["v_low"], 1)
                    if u >= 3:
                        s = u - 3
                        e.wait_ge(VS["o_turned"], i * VT + (s + 1 + START))
                        tokens, n = later_tokens(i, s)
                        e.tensor_tensor(tokens, tokens, bank[6 + s % 2][:, :].rearrange("p (t c) -> p t c", c=P)[:, 0:n, 0:D],
                                        ALU.add).then_inc(VS["o_added"], 1)

        ctx_a = ExitStack()
        AH = sb("a0_XH", [P, BANK], F32R, ctx_a)
        AL = sb("a0_XL", [P, BANK], F32R, ctx_a)
        a_tr = turner("a0", ctx_a, [bank[0], bank[1]], B)
        SCALE = float(DH) ** -0.5
        qf = sb("a0_qf", [P, BANK], F32, ctx_a)
        kf = sb("a0_kf", [P, BANK], F32, ctx_a)
        vf = sb("a0_vf", [P, BANK], F32, ctx_a)
        qh = sb("a0_qh", [P, BANK], F32R, ctx_a)
        ql = sb("a0_ql", [P, BANK], F32R, ctx_a)
        ks = sb("a0_ks", [P, BANK], F32R, ctx_a)
        kh = [sb(f"a0_kh{j}", [P, BANK], F32R, ctx_a) for j in range(2)]
        vx = sb("a0_vx", [P, TPC, HEADS, 32], F32, ctx_a)
        SB = 4
        LAG = 2
        PR = 4
        prob = [sb(f"a0_prob{j}", [P, BANK], F32, ctx_a) for j in range(PR)]
        AG = 4
        PT = 6
        probT = [sb(f"a0_probT{j}", [P, TPC, BANK], F32, ctx_a) for j in range(PT)]
        nmax = sb("a0_nmax", [P, TPC * HEADS], F32, ctx_a)
        oT = sb("a0_oT", [P, 2, BANK], F32, ctx_a)
        rsum = sb("a0_rsum", [P, TPC, HEADS], F32, ctx_a)
        att = [sb(f"a0_att{j}", [P, 2, D], F32, ctx_a) for j in range(2)]
        ot = sb("a0_ot", [P, BANK], F32, ctx_a)
        ctx_a.close()
        a_names = ("vx_set qkv_ready q_biased k_biased v_biased q_high q_low k_high k_low v_turned v_stored "
                   "kh_ready s_ready max_ready exp_ready p_turned p_copied_a p_copied_v o_ready "
                   "o_copied o_turned r_ready att_ready att_turned att_high att_low w_ready w_biased w_turned w_added")
        A = {n: sem("a0_" + n) for n in a_names.split()}
        TILES = HEADS * TPC

        def add_beta(e):
            for b in range(B):
                e.tensor_tensor(rows_of(H, b), rows_of(H, b), over_t(1), ALU.add).then_inc(ln_beta, 1)
            e.wait_ge(ln_beta, B)

        def a0_gpsimd(e):
            e.memset(vx[:, :, :, :], 0.0).then_inc(A["vx_set"], 1)
            e.wait_ge(A["vx_set"], 1 + START)
            e.memset(vx[:, :, :, DH:DH + 1], 1.0).then_inc(A["vx_set"], 1)
            add_beta(e)

        def a0_tensor(e):
            with e.Fori(0, B) as i:
                turn_chunk(e, a_tr, i, 0, TPC)
                e.wait_ge(a_tr["low"], turned_by(a_tr, i, 1))
                for j, name in enumerate("qkv"):
                    product(e, bank[2 + j][:, :], W("a0_" + name), AH[:, 0:BANK], AL[:, 0:BANK]).then_inc(A["qkv_ready"], 1)
                e.wait_ge(A["v_biased"], i + (1 + START))
                for t in range(TPC):
                    mm = e.transpose(bank[7][:, t * P:(t + 1) * P], vf[:, t * P:(t + 1) * P], ident[:, :])
                mm.then_inc(A["v_turned"], 1)

                def scores(n):
                    h, t = divmod(n, TPC)
                    s = bank[n % SB]
                    e.wait_ge(A["kh_ready"], i * HEADS + (h + 1 + START))
                    e.wait_ge(A["exp_ready"], i * TILES + max(n + 1 - SB, 0) + START)
                    e.matmul(s[:, :], qh[:, t * P:(t + 1) * P], kh[h % 2][:, :], start=True, stop=False)
                    e.matmul(s[:, :], ql[:, t * P:(t + 1) * P], kh[h % 2][:, :], start=False, stop=False)
                    e.matmul(s[:, :], ident_bf[:, :], mask0[:, t, :], start=False, stop=True).then_inc(A["s_ready"], 1)

                def turn_probs(n):
                    b = bank[SB + n % 2]
                    e.wait_ge(A[("p_copied_a", "p_copied_v")[n % 2]], i * (TILES // 2) + n // 2 + START)
                    e.wait_ge(A["exp_ready"], i * TILES + (n + 1 + START))
                    for t in range(TPC):
                        mm = e.transpose(b[:, t * P:(t + 1) * P], prob[n % PR][:, t * P:(t + 1) * P], ident[:, :])
                    mm.then_inc(A["p_turned"], 1)

                def attend(g):
                    done = (g + 1) * AG * (TPC // 2)
                    e.wait_ge(A["p_copied_a"], i * (TILES // 2) + (done + START))
                    e.wait_ge(A["p_copied_v"], i * (TILES // 2) + (done + START))
                    for t in range(TPC):
                        for h in range(g * AG, (g + 1) * AG):
                            mm = e.matmul(bank[6 + h // 4][(h % 4) * 32:(h % 4 + 1) * 32, :], vx[:, t, h, :],
                                          probT[h % PT][:, t, :], start=(t == 0), stop=(t == TPC - 1),
                                          skip_group_check=True)
                            if t == TPC - 1:
                                mm.then_inc(A["o_ready"], 1)

                e.wait_ge(A["w_added"], i + START)
                e.wait_ge(A["q_low"], i + (1 + START))
                e.wait_ge(A["k_low"], i + (1 + START))
                e.wait_ge(A["vx_set"], 2 + START)
                e.wait_ge(A["v_stored"], i + (1 + START))
                for n in range(SB - 1):
                    scores(n)
                for n in range(TILES):
                    if n + SB - 1 < TILES:
                        scores(n + SB - 1)
                    turn_probs(n)
                    if n % (AG * TPC) == 1 and n > AG * TPC:
                        attend(n // (AG * TPC) - 1)
                attend(HEADS // AG - 1)
                for t in range(TPC):
                    if t == 0:
                        e.wait_ge(A["o_copied"], i * 2 + (2 + START))
                    if t >= 2:
                        e.wait_ge(A["att_ready"], i * TPC + (t - 1 + START))
                    for g in range(2):
                        mm = e.transpose(bank[t % 2][:, g * P:(g + 1) * P], oT[:, g, t * P:(t + 1) * P], ident[:, :])
                    mm.then_inc(A["o_turned"], 1)
                    if t >= 1:
                        e.wait_ge(A["att_ready"], i * TPC + (t + START))
                        e.transpose(bank[2][:, (t - 1) * P:t * P], att[(t - 1) % 2][:, :, :].rearrange("p a d -> p (a d)"),
                                    ident[:, :]).then_inc(A["att_turned"], 1)
                e.wait_ge(A["att_ready"], i * TPC + (TPC + START))
                e.transpose(bank[2][:, (TPC - 1) * P:BANK], att[(TPC - 1) % 2][:, :, :].rearrange("p a d -> p (a d)"),
                            ident[:, :]).then_inc(A["att_turned"], 1)
                e.wait_ge(A["att_low"], i + (1 + START))
                product(e, bank[3][:, :], W("a0_o"), AH[:, :], AL[:, :]).then_inc(A["w_ready"], 1)
                e.wait_ge(A["w_biased"], i + (1 + START))
                for t in range(TPC):
                    mm = e.transpose(bank[5][:, t * P:(t + 1) * P], ot[:, t * P:(t + 1) * P], ident[:, :])
                mm.then_inc(A["w_turned"], 1)

        def a0_scalar(e):
            with e.Fori(0, B) as i:
                e.wait_ge(A["w_ready"], i + START)
                double_chunk(e, a_tr, i, 0, Y[:, bass.ds(i * TPB, TPC), :], TPC)
                high_chunk(e, a_tr, i, 0, TPC, AH[:, :])
                e.wait_ge(A["qkv_ready"], i * 3 + (2 + START))
                e.activation(kf[:, :], bank[3][:, :], ACT.Identity, bias=bcol("a0_bk")).then_inc(A["k_biased"], 1)
                e.wait_ge(A["qkv_ready"], i * 3 + (3 + START))
                e.activation(vf[:, :], bank[4][:, :], ACT.Identity, bias=bcol("a0_bv")).then_inc(A["v_biased"], 1)
                for n in range(TILES + LAG):
                    if n < TILES:
                        e.wait_ge(A["max_ready"], i * TILES + (n + 1 + START))
                        e.wait_ge(A["p_turned"], i * TILES + max(n - PR + 1, 0) + START)
                        e.activation(prob[n % PR][:, :], bank[n % SB][:, :], ACT.Exp,
                                     bias=nmax[:, n:n + 1]).then_inc(A["exp_ready"], 1)
                    if n >= LAG and (n - LAG) % 2 == 0:
                        copy_probs(e, i, n - LAG, "p_copied_a")
                for g in range(2):
                    e.wait_ge(A["o_ready"], i * HEADS + 4 * (g + 1) + START)
                    e.activation(oT[:, g, :], bank[6 + g][:, :], ACT.Copy).then_inc(A["o_copied"], 1)
                e.wait_ge(A["att_turned"], i * TPC + (TPC + START))
                e.activation(AH[:, 0:BANK], bank[2][:, :], ACT.Copy).then_inc(A["att_high"], 1)
                e.wait_ge(A["w_ready"], i + (1 + START))
                e.activation(ot[:, :], bank[3][:, :], ACT.Identity, bias=bcol("a0_bo")).then_inc(A["w_biased"], 1)

        def copy_probs(e, i, n, done):
            h, t = divmod(n, TPC)
            e.wait_ge(A["o_ready"], i * HEADS + max(h + 1 - PT, 0) + START)
            e.wait_ge(A["p_turned"], i * TILES + (n + 1 + START))
            dst = probT[h % PT][:, :, t * P:(t + 1) * P]
            src = bank[SB + n % 2][:, :].rearrange("p (k q) -> p k q", k=TPC)
            if done == "p_copied_a":
                e.activation(dst, src, ACT.Copy).then_inc(A[done], 1)
            else:
                e.tensor_copy(dst, src).then_inc(A[done], 1)

        def a0_vector(e):
            with e.Fori(0, B) as i:
                low_chunk(e, a_tr, i, 0, TPC, AH[:, :], AL[:, :])
                e.wait_ge(A["qkv_ready"], i * 3 + (1 + START))
                e.tensor_scalar(qf[:, :], bank[2][:, :], bcol("a0_bq"), SCALE, ALU.add, ALU.mult).then_inc(A["q_biased"], 1)
                e.wait_ge(A["q_biased"], i + (1 + START))
                e.tensor_copy(qh[:, :], qf[:, :]).then_inc(A["q_high"], 1)
                e.wait_ge(A["q_high"], i + (1 + START))
                e.tensor_tensor(ql[:, :], qf[:, :], qh[:, :].bitcast(F32), ALU.subtract).then_inc(A["q_low"], 1)
                e.wait_ge(A["k_biased"], i + (1 + START))
                e.tensor_copy(ks[:, :], kf[:, :]).then_inc(A["k_high"], 1)
                e.wait_ge(A["k_high"], i + (1 + START))
                e.tensor_tensor(ks[D:P, :], kf[D:P, :], ks[D:P, :].bitcast(F32), ALU.subtract).then_inc(A["k_low"], 1)
                e.wait_ge(A["vx_set"], 2 + START)
                e.wait_ge(A["v_turned"], i + (1 + START))
                e.tensor_copy(vx[:, :, :, 0:DH], bank[7][:, :].rearrange("p (t c) -> p t c", c=P)[:, :, 0:D]
                              .rearrange("p t (h d) -> p t h d", d=DH)).then_inc(A["v_stored"], 1)
                e.wait_ge(A["k_low"], i + (1 + START))

                def keys_of(h):
                    e.wait_ge(A["s_ready"], i * TILES + max((h - 1) * TPC, 0) + START)
                    e.tensor_scalar(kh[h % 2][:, :], ks[:, :].bitcast(F32), head_rows[:, h:h + 1], None,
                                    ALU.mult).then_inc(A["kh_ready"], 1)

                keys_of(0)
                keys_of(1)
                for n in range(TILES + LAG):
                    if n < TILES:
                        if n % TPC == TPC - 1 and n // TPC + 2 < HEADS:
                            keys_of(n // TPC + 2)
                        e.wait_ge(A["s_ready"], i * TILES + (n + 1 + START))
                        e.tensor_reduce(nmax[:, n:n + 1], bank[n % SB][:, :], X, ALU.max, negate=True).then_inc(A["max_ready"], 1)
                    if n >= LAG and (n - LAG) % 2 == 1:
                        copy_probs(e, i, n - LAG, "p_copied_v")
                for t in range(TPC):
                    o = bank[t % 2][:, 0:2 * P].rearrange("p (h x) -> p h x", x=32)
                    e.wait_ge(A["o_turned"], i * TPC + (t + 1 + START))
                    e.reciprocal(rsum[:, t, :], o[:, :, DH]).then_inc(A["r_ready"], 1)
                    e.wait_ge(A["r_ready"], i * TPC + (t + 1 + START))
                    e.wait_ge(A["att_turned"], i * TPC + max(t - 1, 0) + START)
                    for m in range(2):
                        a = e.tensor_tensor(att[t % 2][:, m, :].rearrange("p (h d) -> p h d", d=DH), o[:, :, 0:DH],
                                            rsum[:, t, :].unsqueeze(2).broadcast_to([P, HEADS, DH]), ALU.mult)
                    a.then_inc(A["att_ready"], 1)
                e.wait_ge(A["att_high"], i + (1 + START))
                e.tensor_tensor(AL[:, 0:BANK], bank[2][:, :], AH[:, 0:BANK].bitcast(F32), ALU.subtract).then_inc(A["att_low"], 1)
                e.wait_ge(A["w_turned"], i + (1 + START))
                yt = Y[:, bass.ds(i * TPB, TPC), :]
                e.tensor_tensor(yt, yt, bank[5][:, :].rearrange("p (t c) -> p t c", c=P)[:, :, 0:D],
                                ALU.add).then_inc(A["w_added"], 1)

        ctx_f = ExitStack()
        fmask = sb("far_mask", [P, NPAD], BF16, ctx_f)
        hotq = [sb(f"far_hotq{j}", [P, P], BF16, ctx_f) for j in range(2)]
        hotk = [sb(f"far_hotk{j}", [P, NPAD], BF16, ctx_f) for j in range(2)]
        eq = sb("far_eq", [P, E_PER], F32, ctx_f)
        ekr = sb("far_ekr", [P, NS, E_PER], F32, ctx_f)
        selfk = sb("far_self", [P, NS], F32, ctx_f)
        f_dup = sb("far_dup", [P, TPC, 2, D], F32, ctx_f)
        f_xh = sb("far_xh", [P, BANK], F32R, ctx_f)
        f_xl = sb("far_xl", [P, BANK], F32R, ctx_f)
        f_kf = sb("far_kf", [P, BANK], F32, ctx_f)
        f_ks = sb("far_ks", [P, NPAD], F32R, ctx_f)
        f_kh = sb("far_kh", [P, NPAD], F32R, ctx_f)
        f_vt = sb("far_vt", [P, TPB, HEADS, DH + 1], F32, ctx_f)
        f_vh = sb("far_vh", [P, TPB, DH + 1], F32, ctx_f)
        f_qf = sb("far_qf", [P, P], F32, ctx_f)
        f_qh = sb("far_qh", [P, P], F32R, ctx_f)
        f_ql = sb("far_ql", [P, P], F32R, ctx_f)
        f_nm = sb("far_nm", [P, NS + 1], F32, ctx_f)
        f_prob = sb("far_prob", [P, NPAD], F32, ctx_f)
        f_rs = sb("far_rs", [P, 1], F32, ctx_f)
        f_att = sb("far_att", [P, 2, D], F32, ctx_f)
        f_ah = sb("far_ah", [P, P], F32R, ctx_f)
        f_al = sb("far_al", [P, P], F32R, ctx_f)
        far_out = sb("far_out", [P, T, D], F32, ctx_f)
        ctx_f.close()
        f_names = ("set dve zeroed hot_ready hot_used mask_ready unit_done job_done doubled turned high low projected "
                   "unit_dve kh_ready scored max_ready head_dve expd p_turned copied attended att_ready att_turned "
                   "att_high att_low out_ready")
        FS = dict(zip(f_names.split(), A.values()))
        SLOTS = E_PER + 1
        JOBS = NS + 1
        JOB_LINKS, QUERY_LINKS, OUT_LINKS, HEAD_LINKS = 4, 3, 2, 3
        UNIT_LINKS = NS * JOB_LINKS + QUERY_LINKS + OUT_LINKS

        def far_gpsimd(e):
            add_beta(e)
            e.memset(f_vt[:, :, :, :], 1.0).then_inc(FS["set"], 1)
            e.iota(selfk[:, :], pattern=[[-BANK, NS]], base=0, channel_multiplier=1,
                   allow_small_or_imprecise_dtypes=True).then_inc(FS["set"], 1)
            for n in t_sems:
                e.sem_inc(t_sems[n], B * NS)

        def far_tensor(e):
            e.sem_inc(FS["hot_used"], 2)
            with e.Fori(0, TPB) as q:
                with e.Fori(0, E_PER // 2) as j:
                    e.wait_ge(FS["zeroed"], q + (1 + START))
                    for u in range(2):
                        e.wait_ge(FS["hot_ready"], q * SLOTS + j * 2 + (u + 1 + START))
                        for k, (c, w) in enumerate(SPANS):
                            mm = e.matmul(bank[k][:, 0:w], hotq[u][:, :], hotk[u][:, c:c + w],
                                          start=False, stop=False, skip_group_check=True)
                        mm.then_inc(FS["hot_used"], 1)
                e.wait_ge(FS["hot_ready"], q * SLOTS + (SLOTS + START))
                for k, (c, w) in enumerate(SPANS):
                    mm = e.matmul(bank[k][:, 0:w], ident_bf[:, :], hotk[0][:, c:c + w],
                                  start=False, stop=False, skip_group_check=True)
                mm.then_inc(FS["hot_used"], 1)
                with e.Fori(0, B) as b:
                    r = q * B + b
                    e.wait_ge(FS["mask_ready"], q + (1 + START))
                    e.wait_ge(FS["unit_done"], r + (1 + START))
                    for m in range(JOBS):
                        n = SPANS[m][1] // P if m < NS else 1
                        e.wait_ge(FS["job_done"], r * JOBS + (m + 1 + START))
                        e.wait_ge(FS["doubled"], r * JOBS + (m + 1 + START))
                        for t in range(n):
                            mm = e.transpose(bank[0][:, t * P:(t + 1) * P],
                                             f_dup[:, t, :, :].rearrange("p a d -> p (a d)"), ident[:, :])
                        mm.then_inc(FS["turned"], 1)
                        e.wait_ge(FS["low"], r * JOBS + (m + 1 + START))
                        mm = product(e, bank[1][:, 0:n * P], W("a0_k" if m < NS else "a0_q"), f_xh[:, 0:n * P], f_xl[:, 0:n * P])
                        if m < NS:
                            for t in range(n):
                                v = bank[2][:, t * D:(t + 1) * D]
                                e.matmul(v, f_xh[:, t * P:(t + 1) * P], W("a0_v", 0, D), start=True, stop=False)
                                mm = e.matmul(v, f_xl[:, t * P:(t + 1) * P], W("a0_v", 0, D), start=False, stop=True)
                        mm.then_inc(FS["projected"], 1)
                    with e.Fori(0, HEADS) as h:
                        u = r * HEADS + h
                        e.wait_ge(FS["kh_ready"], u * 2 + (2 + START))
                        for k, (c, w) in enumerate(SPANS):
                            e.matmul(bank[k][:, 0:w], f_qh[:, :], f_kh[:, c:c + w], start=True, stop=False)
                            e.matmul(bank[k][:, 0:w], f_ql[:, :], f_kh[:, c:c + w], start=False, stop=False)
                            e.matmul(bank[k][:, 0:w], ident_bf[:, :], fmask[:, c:c + w],
                                     start=False, stop=True).then_inc(FS["scored"], 1)
                        for k, (c, w) in enumerate(SPANS):
                            e.wait_ge(FS["expd"], u * NS + (k + 1 + START))
                            for t in range(w // P):
                                mm = e.transpose(bank[k][:, t * P:(t + 1) * P], f_prob[:, c + t * P:c + (t + 1) * P], ident[:, :])
                            mm.then_inc(FS["p_turned"], 1)
                        e.wait_ge(FS["copied"], u * NS + (NS + START))
                        for t in range(TPB):
                            mm = e.matmul(bank[7][:, 0:DH + 1], f_prob[:, t * P:(t + 1) * P], f_vh[:, t, :],
                                          start=(t == 0), stop=(t == TPB - 1))
                        mm.then_inc(FS["attended"], 1)
                    e.wait_ge(FS["att_ready"], r + (1 + START))
                    e.transpose(bank[0][:, 0:P], f_att[:, :, :].rearrange("p a d -> p (a d)"), ident[:, :]
                                ).then_inc(FS["att_turned"], 1)
                    e.wait_ge(FS["att_low"], r + (1 + START))
                    e.matmul(bank[1][:, 0:D], f_ah[:, :], W("a0_o", 0, D), start=True, stop=False)
                    e.matmul(bank[1][:, 0:D], f_al[:, :], W("a0_o", 0, D), start=False, stop=True).then_inc(FS["out_ready"], 1)

        def far_scalar(e):
            with e.Fori(0, TPB) as q:
                with e.Fori(0, B) as b:
                    r = q * B + b
                    for m in range(JOBS):
                        e.wait_ge(FS["job_done"], r * JOBS + (m + 1 + START))
                        n = SPANS[m][1] // P if m < NS else 1
                        first = b * TPB + m * TPC if m < NS else b * TPB + q
                        e.activation(f_dup[:, 0:n, :, :], Y[:, bass.ds(first, n), :].unsqueeze(2).broadcast_to([P, n, 2, D]),
                                     ACT.Copy).then_inc(FS["doubled"], 1)
                        e.wait_ge(FS["turned"], r * JOBS + (m + 1 + START))
                        e.activation(f_xh[:, 0:n * P], bank[0][:, 0:n * P], ACT.Copy).then_inc(FS["high"], 1)
                    with e.Fori(0, HEADS) as h:
                        u = r * HEADS + h
                        e.wait_ge(FS["max_ready"], u + (1 + START))
                        for k, (c, w) in enumerate(SPANS):
                            e.activation(f_prob[:, c:c + w], bank[k][:, 0:w], ACT.Exp, bias=f_nm[:, NS:NS + 1]
                                         ).then_inc(FS["expd"], 1)
                        for k, (c, w) in enumerate(SPANS):
                            e.wait_ge(FS["p_turned"], u * NS + (k + 1 + START))
                            e.activation(f_prob[:, c:c + w], bank[k][:, 0:w], ACT.Copy).then_inc(FS["copied"], 1)
                    e.wait_ge(FS["att_turned"], r + (1 + START))
                    e.activation(f_ah[:, :], bank[0][:, 0:P], ACT.Copy).then_inc(FS["att_high"], 1)

        def far_vector(e):
            e.wait_ge(FS["set"], 2 + START)
            s = Chain(e, FS["dve"], START)
            s.mark(e.tensor_copy(eq[:, :], edges_f[:, 0, :]))
            for k, (c, w) in enumerate(SPANS):
                s.mark(e.tensor_scalar(ekr[:, k, :], edges_f[:, 1, :], float(-c), None, ALU.add))
            s.wait()
            e.sem_inc(FS["unit_done"], 1)
            e.sem_inc(FS["job_done"], 1)
            with e.Fori(0, TPB) as q:
                for k in range(NS):
                    a = e.memset(bank[k][:, :], 0.0)
                a.then_inc(FS["zeroed"], 1)

                def hot_keys(buf, ids):
                    for k, (c, w) in enumerate(SPANS):
                        a = e.tensor_scalar(buf[:, c:c + w], node[:, 0:w], ids(k), None, ALU.is_equal)
                    a.then_inc(FS["hot_ready"], 1)

                with e.Fori(0, E_PER // 2) as j:
                    for u in range(2):
                        e.wait_ge(FS["hot_used"], q * SLOTS + j * 2 + (u + 1 + START))
                        e.tensor_scalar(hotq[u][:, :], node[:, 0:P], eq[:, bass.ds(j * 2 + u, 1)], None, ALU.is_equal)
                        hot_keys(hotk[u], lambda k: ekr[:, k, bass.ds(j * 2 + u, 1)])
                e.wait_ge(FS["hot_used"], q * SLOTS + (SLOTS + 1 + START))
                hot_keys(hotk[0], lambda k: selfk[:, k:k + 1])
                e.wait_ge(FS["hot_used"], q * SLOTS + (SLOTS + 2 + START))
                s = Chain(e, FS["dve"], START + 1 + NS, q, NS + 1)
                for k, (c, w) in enumerate(SPANS):
                    s.mark(e.tensor_scalar(fmask[:, c:c + w], bank[k][:, 0:w], 0.5, MASKED, ALU.is_lt, ALU.mult))
                s.wait()
                s.link(e.memset(fmask[:, N:NPAD], MASKED))
                s.close()
                e.tensor_scalar(eq[:, :], eq[:, :], float(-P), None, ALU.add)
                e.tensor_scalar(selfk[:, :], selfk[:, :], float(P), None, ALU.add).then_inc(FS["mask_ready"], 1)
                with e.Fori(0, B) as b:
                    r = q * B + b
                    e.wait_ge(FS["mask_ready"], q + (1 + START))
                    s = Chain(e, FS["unit_dve"], START, r, UNIT_LINKS)
                    for m in range(JOBS):
                        n = SPANS[m][1] // P if m < NS else 1
                        w = n * P
                        e.wait_ge(FS["high"], r * JOBS + (m + 1 + START))
                        e.tensor_tensor(f_xl[:, 0:w], bank[0][:, 0:w], f_xh[:, 0:w].bitcast(F32), ALU.subtract
                                        ).then_inc(FS["low"], 1)
                        e.wait_ge(FS["projected"], r * JOBS + (m + 1 + START))
                        if m < NS:
                            c = SPANS[m][0]
                            s.link(e.tensor_scalar(f_kf[:, 0:w], bank[1][:, 0:w], bcol("a0_bk"), None, ALU.add))
                            s.link(e.tensor_copy(f_ks[:, c:c + w], f_kf[:, 0:w]))
                            s.mark(e.tensor_tensor(f_ks[D:P, c:c + w], f_kf[D:P, 0:w], f_ks[D:P, c:c + w].bitcast(F32),
                                                   ALU.subtract))
                            for t in range(n):
                                a = e.tensor_tensor(f_vt[:, m * TPC + t, :, 0:DH],
                                                    bank[2][:, t * D:(t + 1) * D].rearrange("p (h d) -> p h d", d=DH),
                                                    row_bias[:, 0, :].rearrange("p (h d) -> p h d", d=DH), ALU.add)
                            s.link(a)
                        else:
                            s.link(e.tensor_scalar(f_qf[:, :], bank[1][:, 0:P], bcol("a0_bq"), SCALE, ALU.add, ALU.mult))
                            s.link(e.tensor_copy(f_qh[:, :], f_qf[:, :]))
                            s.link(e.tensor_tensor(f_ql[:, :], f_qf[:, :], f_qh[:, :].bitcast(F32), ALU.subtract))
                        e.sem_inc(FS["job_done"], 1)
                    with e.Fori(0, HEADS) as h:
                        u = r * HEADS + h
                        e.tensor_scalar(f_kh[:, :], f_ks[:, :].bitcast(F32), head_rows[:, bass.ds(h, 1)], None, ALU.mult
                                        ).then_inc(FS["kh_ready"], 1)
                        e.tensor_copy(f_vh[:, :, :], f_vt[:, :, bass.ds(h, 1), :].rearrange("p t h d -> p t (h d)")
                                      ).then_inc(FS["kh_ready"], 1)
                        ch = Chain(e, FS["head_dve"], START, u, HEAD_LINKS)
                        for k, (c, w) in enumerate(SPANS):
                            e.wait_ge(FS["scored"], u * NS + (k + 1 + START))
                            a = e.tensor_reduce(f_nm[:, k:k + 1], bank[k][:, 0:w], X, ALU.max, negate=True)
                        ch.link(a)
                        e.tensor_reduce(f_nm[:, NS:NS + 1], f_nm[:, 0:NS], X, ALU.min).then_inc(FS["max_ready"], 1)
                        e.wait_ge(FS["attended"], u + (1 + START))
                        ch.link(e.reciprocal(f_rs[:, :], bank[7][:, DH:DH + 1]))
                        for g in range(2):
                            a = e.tensor_scalar(f_att[:, g, bass.ds(h * DH, DH)], bank[7][:, 0:DH], f_rs[:, :], None, ALU.mult)
                        ch.link(a)
                        ch.close()
                    e.sem_inc(FS["att_ready"], 1)
                    e.wait_ge(FS["att_high"], r + (1 + START))
                    e.tensor_tensor(f_al[:, :], bank[0][:, 0:P], f_ah[:, :].bitcast(F32), ALU.subtract).then_inc(FS["att_low"], 1)
                    e.wait_ge(FS["out_ready"], r + (1 + START))
                    o = far_out[:, bass.ds(b * TPB + q, 1), :].rearrange("p t d -> p (t d)")
                    y = Y[:, bass.ds(b * TPB + q, 1), :].rearrange("p t d -> p (t d)")
                    s.link(e.tensor_tensor(o, y, bank[1][:, 0:D], ALU.add))
                    s.link(e.tensor_tensor(o, o, row_bias[:, 1, :], ALU.add))
                    s.close()
                    e.sem_inc(FS["unit_done"], 1)
            for b in range(B):
                a = e.tensor_copy(rows_of(Y, b), rows_of(far_out, b))
            a.then_inc(FS["zeroed"], 1)
            e.wait_ge(FS["zeroed"], TPB + (1 + START))

        def near_only(e, stage):
            beyond = e.value_load(any_far[0:1, 0:1])
            with e.If(beyond <= 0):
                stage(e)

        def near_or_far(e, near, far_):
            beyond = e.value_load(any_far[0:1, 0:1])
            with e.If(beyond <= 0):
                near(e)
            with e.If(beyond > 0):
                far_(e)

        f0 = ffn("f0", E0, f0_w2, "relu", Y, 0, 0, 0, 0, 0, True)

        ctx_b = ExitStack()
        QH = sb("a1_QH", [P, NPAD], F32R, ctx_b)
        QL = sb("a1_QL", [P, NPAD], F32R, ctx_b)
        KS = sb("a1_KS", [P, NPAD], F32R, ctx_b)
        b_tr = turner("a1", ctx_b, [bank[0], bank[1]], B * NS)
        qf1 = [sb(f"a1_qf{j}", [P, BANK], F32, ctx_b) for j in range(2)]
        kf1 = [sb(f"a1_kf{j}", [P, BANK], F32, ctx_b) for j in range(2)]
        vf1 = [sb(f"a1_vf{j}", [P, BANK], F32, ctx_b) for j in range(2)]
        V = sb("a1_V", [P, TPB, D], F32, ctx_b)
        PB = 2
        pT = [sb(f"a1_pT{j}", [P, NS, BANK], F32, ctx_b) for j in range(PB)]
        vs = [sb(f"a1_vs{j}", [P, NS, D], F32, ctx_b) for j in range(2)]
        oS = sb("a1_oS", [P, 4, BANK], F32, ctx_b)
        nm = [sb(f"a1_nm{j}", [P, NS], F32, ctx_b) for j in range(2)]
        sm = [sb(f"a1_sm{j}", [P, NS], F32, ctx_b) for j in range(2)]
        fc = [sb(f"a1_fc{j}", [P, NS], F32, ctx_b) for j in range(2)]
        tot = [sb(f"a1_tot{j}", [P, 4], F32, ctx_b) for j in range(2)]
        later = sb("a1_later", [P, P], BF16, ctx_b)
        laterf = sb("a1_laterf", [P, BANK], F32, ctx_b)
        first_key = sb("a1_first", [P, 1], F32, ctx_b)
        ctx_b.close()
        b_names = ("set qkv_ready q_scaled k_copied v_copied q_high q_low k_high k_low v_turned v_stored s_ready masked "
                   "max_ready exp_ready min_ready f_ready dve scaled pv_done o_copied o_turned o_added")
        Z = {n: sem("a1_" + n) for n in b_names.split()}
        MASK_ALL = -1.0e10 / 8.0

        def widths(j):
            if j == 0:
                return [min(BANK, N - c * BANK) for c in range(NS)]
            end = min((j + 1) * P, N)
            return [min(BANK, end - c * BANK) for c in range(j // TPC + 1)]

        first_chunk, at_chunk = [], 0
        for j in range(TPB):
            first_chunk.append(at_chunk)
            at_chunk += len(widths(j))
        CHUNKS = at_chunk
        RS = 4
        SMALL = 4

        def a1_gpsimd(e):
            e.memset(V[:, :, :], 0.0).then_inc(Z["set"], 1)
            e.memset(oS[:, :, :], 0.0).then_inc(Z["set"], 1)
            e.memset(laterf[:, :], 0.0).then_inc(Z["set"], 1)
            e.memset(first_key[:, :], MASKED).then_inc(Z["set"], 1)
            e.wait_ge(Z["set"], 4 + START)
            e.memset(first_key[0:1, :], MASK_ALL).then_inc(Z["set"], 1)
            e.affine_select(out=laterf[:, :], in_=laterf[:, :], compare_op=ALU.is_gt, fill=MASKED, base=0,
                            pattern=[[-1, BANK]], channel_multiplier=1).then_inc(Z["set"], 1)
            e.wait_ge(Z["set"], 6 + START)
            e.tensor_copy(later[:, :], laterf[:, 0:P]).then_inc(Z["set"], 1)
            e.wait_ge(Z["set"], 7 + START)
            e.memset(laterf[0:1, :], MASK_ALL).then_inc(Z["set"], 1)
            with e.Fori(0, B) as i:
                for k, (c, w) in enumerate(SPANS):
                    e.wait_ge(Z["k_high"], i * NS + (k + 1 + START))
                    e.tensor_tensor(KS[D:P, c:c + w], kf1[k % 2][D:P, 0:w], KS[D:P, c:c + w].bitcast(F32),
                                    ALU.subtract).then_inc(Z["k_low"], 1)
                for j in range(TPB):
                    nc_ = len(widths(j))
                    e.wait_ge(Z["pv_done"], i * CHUNKS + (first_chunk[j - 1] if j >= 1 else 0 + START))
                    e.wait_ge(Z["dve"], i * (TPB * SMALL) + (j + 1) * SMALL + START)
                    e.tensor_tensor(vs[j % 2][:, 0:nc_, :], V[:, j, :].unsqueeze(1).broadcast_to([P, nc_, D]),
                                    fc[j % 2][:, 0:nc_].unsqueeze(2).broadcast_to([P, nc_, D]),
                                    ALU.mult).then_inc(Z["scaled"], 1)

        def a1_tensor(e):
            e.wait_ge(Z["set"], 8 + START)
            with e.Fori(0, B) as i:
                def projections(k):
                    c, w = SPANS[k]
                    hi, lo = QH[:, c:c + w], QL[:, c:c + w]
                    e.wait_ge(b_tr["low"], turned_by(b_tr, i * NS, k + 1))
                    e.wait_ge(Z["q_scaled"], i * NS + (k + START))
                    product(e, bank[2][:, 0:w], W("a1_q"), hi, lo).then_inc(Z["qkv_ready"], 1)
                    e.wait_ge(Z["k_copied"], i * NS + (k + START))
                    product(e, bank[3][:, 0:w], W("a1_k"), hi, lo).then_inc(Z["qkv_ready"], 1)
                    e.wait_ge(Z["v_copied"], i * NS + (k + START))
                    product(e, bank[4][:, 0:w], W("a1_v"), hi, lo).then_inc(Z["qkv_ready"], 1)

                def values(k):
                    e.wait_ge(Z["v_stored"], i * NS + max(k - 1, 0) + START)
                    e.wait_ge(Z["v_copied"], i * NS + (k + 1 + START))
                    for t in range(SPANS[k][1] // P):
                        mm = e.transpose(bank[5 + k % 2][:, t * P:(t + 1) * P], vf1[k % 2][:, t * P:(t + 1) * P], ident[:, :])
                    mm.then_inc(Z["v_turned"], 1)

                turn_chunk(e, b_tr, i * NS, 0, SPANS[0][1] // P)
                for k in range(NS + 1):
                    if k + 1 < NS:
                        turn_chunk(e, b_tr, i * NS, k + 1, SPANS[k + 1][1] // P)
                    if k < NS:
                        projections(k)
                    if k >= 1:
                        values(k - 1)

                def scores(j, c):
                    n = first_chunk[j] + c
                    w = widths(j)[c]
                    s = bank[n % RS]
                    e.wait_ge(Z["exp_ready"], i * CHUNKS + max(n + 1 - RS, 0) + START)
                    diagonal = j > 0 and c == len(widths(j)) - 1
                    k = KS[:, j * P:(j + 1) * P]
                    e.matmul(s[:, 0:w], k, QH[:, c * BANK:c * BANK + w], start=True, stop=False)
                    if diagonal:
                        lo = j * P - c * BANK
                        e.matmul(s[:, lo:w], ident_bf[:, :], later[:, 0:w - lo], start=False, stop=False,
                                 skip_group_check=True)
                    mm = e.matmul(s[:, 0:w], k, QL[:, c * BANK:c * BANK + w], start=False, stop=True)
                    mm.then_inc(Z["s_ready"], 1)

                def attend(j):
                    e.wait_ge(Z["scaled"], i * TPB + (j + 1 + START))
                    for c, w in enumerate(widths(j)):
                        n = first_chunk[j] + c
                        r = c % 2
                        mm = e.matmul(bank[4 + c // 2][r * D:(r + 1) * D, 0:w], vs[j % 2][:, c, :], pT[j % PB][:, c, 0:w],
                                      start=(j == 0), stop=(j == TPB - 1), skip_group_check=True)
                        mm.then_inc(Z["pv_done"], 1)

                e.wait_ge(Z["q_low"], i * NS + (NS + START))
                e.wait_ge(Z["k_low"], i * NS + (NS + START))
                e.wait_ge(Z["v_stored"], i * NS + (NS + START))
                for j in range(TPB + 1):
                    ahead = widths(j) if j < TPB else []
                    split = min(len(ahead), RS - 1)
                    for c in range(split):
                        scores(j, c)
                    if j >= 2:
                        attend(j - 2)
                    for c in range(split, len(ahead)):
                        scores(j, c)
                attend(TPB - 1)
                for q in range(4):
                    e.wait_ge(Z["o_added"], i * 4 + max(q - 1, 0) + START)
                    e.wait_ge(Z["o_copied"], i * 4 + (q + 1 + START))
                    for t in range(TPC if q < 3 else 1):
                        mm = e.transpose(bank[q % 2][:, t * P:(t + 1) * P], oS[:, q, t * P:(t + 1) * P], ident[:, :])
                    mm.then_inc(Z["o_turned"], 1)
                e.wait_ge(Z["o_added"], i * 4 + (4 + START))

        def a1_scalar(e):
            with e.Fori(0, B) as i:
                e.wait_ge(Z["s_ready"], i * CHUNKS + START)

                def double(k):
                    n = SPANS[k][1] // P
                    double_chunk(e, b_tr, i * NS, k, Y[:, bass.ds(i * TPB + k * TPC, n), :], n)

                def high(k):
                    c, w = SPANS[k]
                    high_chunk(e, b_tr, i * NS, k, w // P, QH[:, c:c + w])

                double(0)
                double(1)
                high(0)
                for k, (c, w) in enumerate(SPANS):
                    if k + 1 < NS:
                        high(k + 1)
                    if k + 2 < NS:
                        double(k + 2)
                    e.wait_ge(Z["qkv_ready"], i * (NS * 3) + (3 * k + 1 + START))
                    e.wait_ge(Z["q_low"], i * NS + max(k - 1, 0) + START)
                    e.activation(qf1[k % 2][:, 0:w], bank[2][:, 0:w], ACT.Copy, scale=1.0 / 8.0).then_inc(Z["q_scaled"], 1)
                    e.wait_ge(Z["qkv_ready"], i * (NS * 3) + (3 * k + 2 + START))
                    e.wait_ge(Z["k_low"], i * NS + max(k - 1, 0) + START)
                    e.activation(kf1[k % 2][:, 0:w], bank[3][:, 0:w], ACT.Copy).then_inc(Z["k_copied"], 1)
                    e.wait_ge(Z["qkv_ready"], i * (NS * 3) + (3 * k + 3 + START))
                    e.wait_ge(Z["v_turned"], i * NS + max(k - 1, 0) + START)
                    e.activation(vf1[k % 2][:, 0:w], bank[4][:, 0:w], ACT.Copy).then_inc(Z["v_copied"], 1)
                for j in range(TPB):
                    for c, w in enumerate(widths(j)):
                        n = first_chunk[j] + c
                        p = pT[j % PB][:, c, 0:w]
                        e.wait_ge(Z["max_ready"], i * CHUNKS + (n + 1 + START))
                        if j >= PB:
                            e.wait_ge(Z["pv_done"], i * CHUNKS + (first_chunk[j - PB] + min(c, len(widths(j - PB)) - 1) + 1 + START))
                            if c == 0:
                                e.wait_ge(Z["dve"], i * (TPB * SMALL) + (j - 1) * SMALL + START)
                        src = p if j == 0 else bank[n % RS][:, 0:w]
                        e.activation(p, src, ACT.Exp, bias=nm[j % 2][:, c:c + 1],
                                     accum_out=sm[j % 2][:, c:c + 1]).then_inc(Z["exp_ready"], 1)
                    e.wait_ge(Z["min_ready"], i * TPB + (j + 1 + START))
                    e.wait_ge(Z["scaled"], i * TPB + max(j - 1, 0) + START)
                    nc_ = len(widths(j))
                    e.activation(fc[j % 2][:, 0:nc_], nm[j % 2][:, 0:nc_], ACT.Exp, bias=tot[j % 2][:, 0:1],
                                 scale=-1.0).then_inc(Z["f_ready"], 1)
                for q in range(4):
                    e.wait_ge(Z["pv_done"], i * CHUNKS + (CHUNKS + START))
                    if q < 3:
                        a = e.activation(oS[:, q, :], bank[4 + q][:, :], ACT.Copy)
                    else:
                        a = e.activation(oS[0:D, q, 0:LAST], bank[4 + q][0:D, 0:LAST], ACT.Copy)
                    a.then_inc(Z["o_copied"], 1)

        def a1_vector(e):
            e.wait_ge(Z["set"], 8 + START)
            with e.Fori(0, B) as i:
                def store_values(k):
                    e.wait_ge(Z["v_turned"], i * NS + (k + 1 + START))
                    n = SPANS[k][1] // P
                    hi = P if k < NS - 1 else LAST
                    e.tensor_copy(V[0:hi, k * TPC:k * TPC + n, :],
                                  bank[5 + k % 2][0:hi, :].rearrange("p (t c) -> p t c", c=P)[:, 0:n, 0:D]
                                  ).then_inc(Z["v_stored"], 1)

                low_chunk(e, b_tr, i * NS, 0, SPANS[0][1] // P, QH[:, 0:BANK], QL[:, 0:BANK])
                for k, (c, w) in enumerate(SPANS):
                    if k + 1 < NS:
                        c2, w2 = SPANS[k + 1]
                        low_chunk(e, b_tr, i * NS, k + 1, w2 // P, QH[:, c2:c2 + w2], QL[:, c2:c2 + w2])
                    e.wait_ge(Z["k_copied"], i * NS + (k + 1 + START))
                    e.tensor_copy(KS[:, c:c + w], kf1[k % 2][:, 0:w]).then_inc(Z["k_high"], 1)
                    e.wait_ge(Z["qkv_ready"], i * (NS * 3) + (3 * k + 3 + START))
                    e.wait_ge(Z["q_scaled"], i * NS + (k + 1 + START))
                    e.tensor_copy(QH[:, c:c + w], qf1[k % 2][:, 0:w]).then_inc(Z["q_high"], 1)
                    e.wait_ge(Z["q_high"], i * NS + (k + 1 + START))
                    e.tensor_tensor(QL[:, c:c + w], qf1[k % 2][:, 0:w], QH[:, c:c + w].bitcast(F32),
                                    ALU.subtract).then_inc(Z["q_low"], 1)
                    if k >= 1:
                        store_values(k - 1)
                store_values(NS - 1)

                def tile_sums(j):
                    nc_ = len(widths(j))
                    r = j % 2
                    ch = Chain(e, Z["dve"], START + j * SMALL, i, TPB * SMALL)
                    e.wait_ge(Z["f_ready"], i * TPB + (j + 1 + START))
                    ch.link(e.tensor_tensor(sm[r][:, 0:nc_], sm[r][:, 0:nc_], fc[r][:, 0:nc_], ALU.mult))
                    ch.link(e.tensor_reduce(tot[r][:, 1:2], sm[r][:, 0:nc_], X, ALU.add))
                    ch.link(e.reciprocal(tot[r][:, 2:3], tot[r][:, 1:2]))
                    ch.mark(e.tensor_scalar(fc[r][:, 0:nc_], fc[r][:, 0:nc_], tot[r][:, 2:3], None, ALU.mult))

                for j in range(TPB):
                    ws = widths(j)
                    for c, w in enumerate(ws):
                        n = first_chunk[j] + c
                        src = bank[n % RS][:, 0:w]
                        e.wait_ge(Z["s_ready"], i * CHUNKS + (n + 1 + START))
                        if j == 0:
                            src = pT[0][:, c, 0:w]
                            e.wait_ge(Z["pv_done"], i * CHUNKS + START)
                            if c == 0:
                                a = e.tensor_tensor(src, bank[n % RS][:, 0:w], laterf[:, 0:w], ALU.add)
                            else:
                                a = e.tensor_scalar(src, bank[n % RS][:, 0:w], first_key[:, :], None, ALU.add)
                            a.then_inc(Z["masked"], 1)
                            e.wait_ge(Z["masked"], i * NS + (n + 1 + START))
                        e.tensor_reduce(nm[j % 2][:, c:c + 1], src, X, ALU.max, negate=True).then_inc(Z["max_ready"], 1)
                        if j >= 1 and c == min(1, len(ws) - 1):
                            tile_sums(j - 1)
                    e.wait_ge(Z["max_ready"], i * CHUNKS + (first_chunk[j] + len(ws) + START))
                    e.tensor_reduce(tot[j % 2][:, 0:1], nm[j % 2][:, 0:len(ws)], X, ALU.min).then_inc(Z["min_ready"], 1)
                tile_sums(TPB - 1)
                for q in range(4):
                    e.wait_ge(Z["o_turned"], i * 4 + (q + 1 + START))
                    if q < 3:
                        h = H[:, bass.ds(i * TPB + 2 * q * TPC, 2 * TPC), :].rearrange("p (a t) d -> p t a d", a=2)
                        o = bank[q % 2][:, :].rearrange("p (t a d) -> p t a d", a=2, d=D)
                        e.tensor_tensor(h, h, o, ALU.add).then_inc(Z["o_added"], 1)
                    else:
                        h = H[0:LAST, bass.ds(i * TPB + 2 * q * TPC, 1), :].rearrange("p t d -> p (t d)")
                        e.tensor_tensor(h, h, bank[q % 2][0:LAST, 0:D], ALU.add).then_inc(Z["o_added"], 1)

        def started():
            return [t_split, t_logit, t_out, t_turned, t_gated, *t_sems.values(), *VS.values(), *A.values(),
                    *(G[n] for n in ("logit", "lt_biased", "lt_turned", "stored")), *Z.values()]

        f1 = ffn("f1", E1, f1_w2, "gelu", H, 1, NCH, NCH * E0, NCH * E0 // 2, GATE_LINKS, False)
        block = ctx.enter_context(nc.Block())

        @block.sync
        def _(e):
            weights_sync(e)
            stage_end(e, 1)
            tok_sync(e)
            for stage in range(2, STAGES):
                stage_end(e, stage)
            stores = 0
            for b in range(B):
                parts = [(0, TPB - 1)] if b < B - 1 else [(0, TPB // 2), (TPB // 2, TPB - 5), (TPB - 5, TPB - 1)]
                for lo, hi in parts:
                    e.wait_ge(G["y_added"], NCH + -(-(b * TPB + hi) // TPC))
                    e.dma_start(out[b, lo * P:hi * P, :].rearrange("(t p) d -> p t d", p=P),
                                H[:, b * TPB + lo:b * TPB + hi, :]).then_inc(stored, 16)
                    stores += 1
                e.wait_ge(G["y_added"], NCH + -(-(b + 1) * TPB // TPC))
                e.dma_start(out[b, (TPB - 1) * P:N, :], H[0:LAST, (b + 1) * TPB - 1, :]).then_inc(stored, 16)
                stores += 1
            e.wait_ge(stored, stores * 16)
            stage_end(e, STAGES)

        @block.gpsimd
        def _(e):
            weights_gpsimd(e)
            stage_end(e, 1)
            tok_gpsimd(e)
            stage_end(e, 2)
            norm_gpsimd(e, 0, H, None)
            stage_end(e, 3)
            stage_end(e, 4)
            near_or_far(e, a0_gpsimd, far_gpsimd)
            stage_end(e, 5)
            norm_gpsimd(e, 1, Y, 0)
            stage_end(e, 6)
            norm_gpsimd(e, 2, H, None)
            stage_end(e, 7)
            stage_end(e, 8)
            f0["b_gpsimd"](e)
            stage_end(e, 9)
            f0["c_gpsimd"](e)
            stage_end(e, 10)
            a1_gpsimd(e)
            stage_end(e, 11)
            norm_gpsimd(e, 3, H, None)
            stage_end(e, 12)
            stage_end(e, 13)
            f1["b_gpsimd"](e)
            stage_end(e, 14)
            f1["c_gpsimd"](e)
            stage_end(e, STAGES)

        @block.scalar
        def _(e):
            weights_scalar(e)
            stage_end(e, 1)
            tok_scalar(e)
            stage_end(e, 2)
            norm_scalar(e, 0)
            stage_end(e, 3)
            near_only(e, later_scalar)
            stage_end(e, 4)
            near_or_far(e, a0_scalar, far_scalar)
            stage_end(e, 5)
            norm_scalar(e, 1)
            stage_end(e, 6)
            norm_scalar(e, 2)
            stage_end(e, 7)
            f0["a_scalar"](e)
            stage_end(e, 8)
            f0["b_scalar"](e)
            stage_end(e, 9)
            f0["c_scalar"](e)
            stage_end(e, 10)
            a1_scalar(e)
            stage_end(e, 11)
            norm_scalar(e, 3)
            stage_end(e, 12)
            f1["a_scalar"](e)
            stage_end(e, 13)
            f1["b_scalar"](e)
            stage_end(e, 14)
            f1["c_scalar"](e)
            stage_end(e, STAGES)

        @block.vector
        def _(e):
            weights_vector(e)
            stage_end(e, 1)
            tok_vector(e)
            stage_end(e, 2)
            norm_vector(e, 0, H, None)
            stage_end(e, 3)
            near_only(e, later_vector)
            stage_end(e, 4)
            near_or_far(e, a0_vector, far_vector)
            stage_end(e, 5)
            norm_vector(e, 1, Y, 0)
            stage_end(e, 6)
            norm_vector(e, 2, H, None)
            stage_end(e, 7)
            f0["a_vector"](e)
            stage_end(e, 8)
            f0["b_vector"](e)
            stage_end(e, 9)
            f0["c_vector"](e)
            stage_end(e, 10)
            a1_vector(e)
            stage_end(e, 11)
            norm_vector(e, 3, H, None)
            stage_end(e, 12)
            f1["a_vector"](e)
            stage_end(e, 13)
            f1["b_vector"](e)
            stage_end(e, 14)
            f1["c_vector"](e)
            stage_end(e, STAGES)

        @block.tensor
        def _(e):
            weights_tensor(e)
            stage_end(e, 1)
            tok_tensor(e)
            stage_end(e, 2)
            stage_end(e, 3)
            near_only(e, later_tensor)
            stage_end(e, 4)
            near_or_far(e, a0_tensor, far_tensor)
            stage_end(e, 5)
            stage_end(e, 6)
            stage_end(e, 7)
            f0["a_tensor"](e)
            stage_end(e, 8)
            stage_end(e, 9)
            f0["c_tensor"](e)
            stage_end(e, 10)
            a1_tensor(e)
            stage_end(e, 11)
            stage_end(e, 12)
            f1["a_tensor"](e)
            stage_end(e, 13)
            stage_end(e, 14)
            f1["c_tensor"](e)
            stage_end(e, STAGES)


_INS = ["x", "txt", "L0_tok_W1", "L0_tok_b1", "L0_tok_W2", "L0_tok_b2", "L0_tok_W3", "L0_tok_b3",
        "L0_attn_edge_index", "L0_attn_Wq", "L0_attn_bq", "L0_attn_Wk", "L0_attn_bk", "L0_attn_Wv", "L0_attn_bv",
        "L0_attn_Wo", "L0_attn_bo", "L0_attn_gamma", "L0_attn_beta", "L0_ffn_gate_w", "L0_ffn_gate_b",
        "L0_ffn_w1", "L0_ffn_b1", "L0_ffn_w2", "L0_ffn_b2", "L0_ffn_gamma", "L0_ffn_beta", "L1_attn_Wq",
        "L1_attn_Wk", "L1_attn_Wv", "L1_ffn_gate_w", "L1_ffn_gate_b", "L1_ffn_W1", "L1_ffn_b1", "L1_ffn_W2",
        "L1_ffn_b2"]


def kernel(**inputs):
    import numpy as _np
    import concourse.bacc as _bacc
    from concourse import mybir as _mybir
    from concourse.bass_utils import run_bass_kernel_spmd as _run

    nc = _bacc.Bacc("TRN2", target_bir_lowering=False, num_devices=1)
    arrays, ins = {}, {}
    for name in _INS:
        a = _np.ascontiguousarray(inputs[name])
        arrays[f"in_{name}_dram"] = a
        ins[name] = nc.dram_tensor(f"in_{name}_dram", a.shape, _mybir.dt.from_np(a.dtype), kind="ExternalInput").ap()
    shape = (inputs["x"].shape[0], inputs["x"].shape[2] * inputs["x"].shape[3] + inputs["txt"].shape[1],
             inputs["x"].shape[1])
    out = nc.dram_tensor("out_0_dram", shape, _mybir.dt.float32, kind="ExternalOutput").ap()
    build(nc, ins, out)
    r = _run(nc, [arrays], core_ids=[0])
    return r.results[0]["out_0_dram"]
```
